# Optimizing a Trainium2 kernel written in Bass

```python
import numpy as np
import jax
import jax.numpy as jnp

def _softmax(x, axis=-1):
    return jax.nn.softmax(x, axis=axis)

def _gelu(x):
    return jax.nn.gelu(x, approximate=True)

def _silu(x):
    return jax.nn.silu(x)

def _sigmoid(x):
    return jax.nn.sigmoid(x)

def _layernorm(x, axis=-1, eps=1e-05):
    m = jnp.mean(x, axis=axis, keepdims=True)
    v = jnp.var(x, axis=axis, keepdims=True)
    return (x - m) / jnp.sqrt(v + eps)

def _scatter_add(tgt, idx, src, axis=0):
    return tgt.at[idx].add(src)

def _segment_sum(src, seg, n):
    return jax.ops.segment_sum(src, seg, n)
kernel_name = 'mk_gps_d1_gnn_r32_b8a6df'

def setup_inputs(seed: int=0):
    np.random.seed(seed)
    _w = jnp.asarray

    def _rec_inputs():
        import jax
        import jax.numpy as jnp
        _gk = jax.random.key(seed)
        x = -0.0001126 + 1 * jax.random.normal(jax.random.fold_in(_gk, 1), (3125, 256), jnp.float32)
        src = jax.random.randint(jax.random.fold_in(_gk, 2), (50000,), 0, 3125, jnp.int32)
        dst = jnp.minimum((3125 * jax.random.uniform(jax.random.fold_in(_gk, 3), (50000,)) ** 2.0).astype(jnp.int32), 99999)
        _o = jnp.argsort(dst, stable=True)
        src = src[_o]
        dst = dst[_o]
        edge_type_8 = jax.random.randint(jax.random.fold_in(_gk, 12), (50000,), 0, 8, jnp.int32)
        return (x, src, dst, edge_type_8)
    x, src, dst, edge_type_8 = _rec_inputs()

    def _L0_gnn_setup():
        import jax, jax.numpy as jnp
        import numpy as np
        N, E, R, H, D = (30000, 9375, 8, 8, 32)
        IN_F = 256
        NEG_SLOPE = 0.2
        key = jax.random.key(seed)
        k = jax.random.split(key, 6)
        x = jax.random.normal(k[0], (N, IN_F), dtype=jnp.float32)
        W = jax.random.normal(k[1], (R, H * D, IN_F), dtype=jnp.float32) * 0.05
        attn_src = jax.random.normal(k[2], (H, D), dtype=jnp.float32) * 0.1
        attn_dst = jax.random.normal(k[3], (H, D), dtype=jnp.float32) * 0.1
        edge_index = jax.random.randint(k[4], (2, E), 0, N, dtype=jnp.int64) if jax.config.read('jax_enable_x64') else jax.random.randint(k[4], (2, E), 0, N, dtype=jnp.int32)
        edge_type = jax.random.randint(k[5], (E,), 0, R, dtype=edge_index.dtype)
        return dict(x=x, W=W, attn_src=attn_src, attn_dst=attn_dst, edge_index=edge_index, edge_type=edge_type)
    _L0_gnn_all = _L0_gnn_setup()
    _L0_gnn_in = {k: v for k, v in _L0_gnn_all.items() if k in ('W', 'attn_src', 'attn_dst')}
    del _L0_gnn_all

    def _L0_mix_setup():
        import jax, jax.numpy as jnp
        import numpy as np
        NUM_HEADS = 8
        key = jax.random.key(seed)
        ks = jax.random.split(key, 5)
        B, N, C = (8, 512, 256)
        x = jax.random.normal(ks[0], (B, N, C), dtype=jnp.float32)
        Wq = jax.random.normal(ks[1], (C, C), dtype=jnp.float32) * 0.02
        Wkv = jax.random.normal(ks[2], (2 * C, C), dtype=jnp.float32) * 0.02
        Wproj = jax.random.normal(ks[3], (C, C), dtype=jnp.float32) * 0.02
        bproj = jnp.zeros((C,), dtype=jnp.float32)
        return {'x': x, 'Wq': Wq, 'Wkv': Wkv, 'Wproj': Wproj, 'bproj': bproj}
    _L0_mix_all = _L0_mix_setup()
    _L0_mix_in = {k: v for k, v in _L0_mix_all.items() if k in ('Wq', 'Wkv', 'Wproj', 'bproj')}
    del _L0_mix_all

    def _L0_ffn_setup():
        import jax, jax.numpy as jnp
        import numpy as np
        DIM = 256
        H = 8
        D = 64
        G = 64
        INNER = H * D
        SCALE = D ** (-0.5)
        key = jax.random.key(seed)
        ks = jax.random.split(key, 12)
        B, N = (4, 512)
        x = jax.random.normal(ks[0], (B, N, DIM), dtype=jnp.float32)
        s = lambda fan_in: 1.0 / np.sqrt(fan_in)
        W_fx = jax.random.normal(ks[1], (DIM, INNER), dtype=jnp.float32) * s(DIM)
        b_fx = jnp.zeros((INNER,), dtype=jnp.float32)
        W_x = jax.random.normal(ks[2], (DIM, INNER), dtype=jnp.float32) * s(DIM)
        b_x = jnp.zeros((INNER,), dtype=jnp.float32)
        A = jax.random.normal(ks[3], (G, D), dtype=jnp.float32)
        Q, _ = jnp.linalg.qr(A.T)
        W_slice = Q[:, :G].astype(jnp.float32)
        b_slice = jnp.zeros((G,), dtype=jnp.float32)
        W_q = jax.random.normal(ks[4], (D, D), dtype=jnp.float32) * s(D)
        W_k = jax.random.normal(ks[5], (D, D), dtype=jnp.float32) * s(D)
        W_v = jax.random.normal(ks[6], (D, D), dtype=jnp.float32) * s(D)
        W_out = jax.random.normal(ks[7], (INNER, DIM), dtype=jnp.float32) * s(INNER)
        b_out = jnp.zeros((DIM,), dtype=jnp.float32)
        temperature = jnp.ones((1, H, 1, 1), dtype=jnp.float32) * 0.5
        return {'x': x, 'W_fx': W_fx, 'b_fx': b_fx, 'W_x': W_x, 'b_x': b_x, 'W_slice': W_slice, 'b_slice': b_slice, 'W_q': W_q, 'W_k': W_k, 'W_v': W_v, 'W_out': W_out, 'b_out': b_out, 'temperature': temperature}
    _L0_ffn_all = _L0_ffn_setup()
    _L0_ffn_in = {k: v for k, v in _L0_ffn_all.items() if k in ('W_fx', 'b_fx', 'W_x', 'b_x', 'W_slice', 'b_slice', 'W_q', 'W_k', 'W_v', 'W_out', 'b_out', 'temperature')}
    del _L0_ffn_all
    return {'x': x, 'src': src, 'dst': dst, 'edge_type_8': edge_type_8, 'L0_gnn_W': _L0_gnn_in['W'], 'L0_gnn_attn_src': _L0_gnn_in['attn_src'], 'L0_gnn_attn_dst': _L0_gnn_in['attn_dst'], 'L0_mix_Wq': _L0_mix_in['Wq'], 'L0_mix_Wkv': _L0_mix_in['Wkv'], 'L0_mix_Wproj': _L0_mix_in['Wproj'], 'L0_mix_bproj': _L0_mix_in['bproj'], 'L0_ffn_W_fx': _L0_ffn_in['W_fx'], 'L0_ffn_b_fx': _L0_ffn_in['b_fx'], 'L0_ffn_W_x': _L0_ffn_in['W_x'], 'L0_ffn_b_x': _L0_ffn_in['b_x'], 'L0_ffn_W_slice': _L0_ffn_in['W_slice'], 'L0_ffn_b_slice': _L0_ffn_in['b_slice'], 'L0_ffn_W_q': _L0_ffn_in['W_q'], 'L0_ffn_W_k': _L0_ffn_in['W_k'], 'L0_ffn_W_v': _L0_ffn_in['W_v'], 'L0_ffn_W_out': _L0_ffn_in['W_out'], 'L0_ffn_b_out': _L0_ffn_in['b_out'], 'L0_ffn_temperature': _L0_ffn_in['temperature']}

def reference(x, src, dst, edge_type_8, L0_gnn_W, L0_gnn_attn_src, L0_gnn_attn_dst, L0_mix_Wq, L0_mix_Wkv, L0_mix_Wproj, L0_mix_bproj, L0_ffn_W_fx, L0_ffn_b_fx, L0_ffn_W_x, L0_ffn_b_x, L0_ffn_W_slice, L0_ffn_b_slice, L0_ffn_W_q, L0_ffn_W_k, L0_ffn_W_v, L0_ffn_W_out, L0_ffn_b_out, L0_ffn_temperature):
    import jax
    import jax.numpy as jnp

    def _L0_gnn_ref(x, W, attn_src, attn_dst, edge_index, edge_type):
        import jax, jax.numpy as jnp
        import numpy as np
        N, E, R, H, D = (30000, 9375, 8, 8, 32)
        IN_F = 256
        NEG_SLOPE = 0.2
        n = x.shape[0]
        r = W.shape[0]
        h, d = attn_src.shape
        h_all = jnp.einsum('nf,rof->rno', x, W).reshape(r, n, h, d)
        src, dst = (edge_index[0], edge_index[1])
        h_src = h_all[edge_type, src]
        h_dst = h_all[edge_type, dst]
        scores = jnp.einsum('ehd,hd->eh', h_src, attn_src) + jnp.einsum('ehd,hd->eh', h_dst, attn_dst)
        scores = jnp.where(scores > 0, scores, NEG_SLOPE * scores)
        amax = jnp.maximum(jax.ops.segment_max(scores, dst, num_segments=n), 0.0)
        w = jnp.exp(scores - amax[dst])
        denom = jax.ops.segment_sum(w, dst, num_segments=n) + 1e-12
        w = w / denom[dst]
        msg = h_src * w[..., None]
        out = jax.ops.segment_sum(msg, dst, num_segments=n)
        return out.reshape(n, h * d)

    def _L0_mix_ref(x, Wq, Wkv, Wproj, bproj):
        import jax, jax.numpy as jnp
        import numpy as np
        NUM_HEADS = 8
        B, N, C = x.shape
        h = NUM_HEADS
        d = C // h
        q = jnp.einsum('bnc,oc->bno', x, Wq).reshape(B, N, h, d).transpose(0, 2, 1, 3)
        kv = jnp.einsum('bnc,oc->bno', x, Wkv).reshape(B, N, 2, h, d)
        k = kv[:, :, 0].transpose(0, 2, 1, 3)
        v = kv[:, :, 1].transpose(0, 2, 1, 3)
        q = jax.nn.elu(q) + 1.0
        k = jax.nn.elu(k) + 1.0
        k_sum = k.sum(axis=2)
        D_inv = 1.0 / jnp.maximum(jnp.einsum('bhnd,bhd->bhn', q, k_sum), 1e-06)
        context = jnp.einsum('bhnd,bhne->bhde', k, v)
        attn = jnp.einsum('bhnd,bhde->bhne', q, context) * D_inv[..., None]
        out = attn.transpose(0, 2, 1, 3).reshape(B, N, C)
        out = jnp.einsum('bnc,oc->bno', out, Wproj) + bproj
        return out

    def _L0_ffn_ref(x, W_fx, b_fx, W_x, b_x, W_slice, b_slice, W_q, W_k, W_v, W_out, b_out, temperature):
        import jax, jax.numpy as jnp
        import numpy as np
        DIM = 256
        H = 8
        D = 64
        G = 64
        INNER = H * D
        SCALE = D ** (-0.5)
        B, N, _ = x.shape
        fx_mid = (x @ W_fx + b_fx).reshape(B, N, H, D).transpose(0, 2, 1, 3)
        x_mid = (x @ W_x + b_x).reshape(B, N, H, D).transpose(0, 2, 1, 3)
        temp = jnp.clip(temperature, 0.1, 5.0)
        slice_weights = jax.nn.softmax((x_mid @ W_slice + b_slice) / temp, axis=-1)
        slice_norm = slice_weights.sum(axis=2)
        slice_token = jnp.einsum('bhnc,bhng->bhgc', fx_mid, slice_weights)
        slice_token = slice_token / (slice_norm[..., None] + 1e-05)
        q = slice_token @ W_q
        k = slice_token @ W_k
        v = slice_token @ W_v
        attn = jax.nn.softmax(jnp.einsum('bhgc,bhkc->bhgk', q, k) * SCALE, axis=-1)
        out_slice = jnp.einsum('bhgk,bhkc->bhgc', attn, v)
        out_x = jnp.einsum('bhgc,bhng->bhnc', out_slice, slice_weights)
        out_x = out_x.transpose(0, 2, 1, 3).reshape(B, N, INNER)
        return out_x @ W_out + b_out
    edge_index = jnp.stack([src, dst])
    xn = _layernorm(x, axis=-1)
    x = x + _L0_gnn_ref(xn, L0_gnn_W, L0_gnn_attn_src, L0_gnn_attn_dst, edge_index, edge_type_8) + _L0_mix_ref(xn[None], L0_mix_Wq, L0_mix_Wkv, L0_mix_Wproj, L0_mix_bproj)[0]
    x = x + _L0_ffn_ref(_layernorm(x, axis=-1)[None], L0_ffn_W_fx, L0_ffn_b_fx, L0_ffn_W_x, L0_ffn_b_x, L0_ffn_W_slice, L0_ffn_b_slice, L0_ffn_W_q, L0_ffn_W_k, L0_ffn_W_v, L0_ffn_W_out, L0_ffn_b_out, L0_ffn_temperature)[0]
    return x

_drawn_inputs = setup_inputs


def setup_inputs(seed=0):
    import zlib

    import numpy as np

    out = dict(_drawn_inputs(seed))
    spreads = {'L0_mix_bproj': (0.0, 0.1),
     'L0_ffn_b_fx': (0.0, 0.1),
     'L0_ffn_b_x': (0.0, 0.8),
     'L0_ffn_b_slice': (0.0, 0.8),
     'L0_ffn_b_out': (0.0, 0.1),
     'L0_ffn_temperature': (0.5, 0.6)}
    factors = {'L0_mix_Wq': 8.0,
     'L0_mix_Wkv': 8.0,
     'L0_mix_Wproj': 8.0,
     'L0_ffn_W_x': 8.0,
     'L0_ffn_W_slice': 8.0,
     'L0_ffn_W_q': 8.0,
     'L0_ffn_W_k': 8.0}
    for name, (base, spread) in spreads.items():
        noise = np.random.default_rng([zlib.crc32(name.encode()), seed]).standard_normal(out[name].shape)
        drawn = base * np.exp(spread * noise) if base else spread * noise
        out[name] = jnp.asarray(drawn.astype(out[name].dtype))
    for name, factor in factors.items():
        out[name] = (out[name] * factor).astype(out[name].dtype)
    return out
```

```python
from contextlib import ExitStack

import concourse.bass as bass
from concourse import mybir

ds = bass.ds
ALU = mybir.AluOpType
ACT = mybir.ActivationFunctionType
F32 = mybir.dt.float32
BF16 = mybir.dt.bfloat16
I32 = mybir.dt.int32
U32 = mybir.dt.uint32
AX = mybir.AxisListType.X

P = 128
BIG = 1.0e30
LN_EPS = 1e-5


class Chain:

    def __init__(self, eng, sem):
        self.eng, self.sem, self.base, self.n, self.done = eng, sem, 0, 0, 0

    def link(self, ins):
        self.n += 1
        ins.then_inc(self.sem, 1)
        self.eng.wait_ge(self.sem, self.base + self.n)

    def enter(self, i, per):
        self.done += self.n
        self.base, self.n, self.per = i * per + self.done, 0, per

    def leave(self, turns):
        assert self.n == self.per, (self.n, self.per)
        self.done += self.per * turns
        self.base, self.n = self.done, 0


def build(nc, a, out):
    x_d, src_d, dst_d, typ_d = a["x"], a["src"], a["dst"], a["edge_type_8"]
    N, F = x_d.shape
    E = src_d.shape[0]
    R = a["L0_gnn_W"].shape[0]
    H, D = a["L0_gnn_attn_src"].shape
    G, DH = a["L0_ffn_W_slice"].shape
    INNER = a["L0_ffn_W_fx"].shape[1]
    FULL, TAIL = N // P, N % P
    NB = FULL + 1
    FC = F // P
    ROW = F + H
    TILES = -(-E // P)
    TJ = -(-TILES // P)
    SG = 16
    NSG = -(-(TILES + NB - 1) // SG)
    STEPS = NSG * SG
    KC = -(-STEPS // P)
    PAD_DST = 8191
    assert H * D == F and SG * H == P and NSG % 2 == 0 and FULL % 2 == 0 and G == DH == 64
    C_DST, C_IDX, C_TYP, C_BRK, C_FIRST, C_BLK, TROW = 0, P, 2 * P, 3 * P, 4 * P + 1, 4 * P + 2, 4 * P + 4

    table_d = nc.dram_tensor("table", (NB * P * R, ROW), F32)
    tiles_d = nc.dram_tensor("tiles", (TJ * P, TROW), F32)
    table_rows = table_d.ap()
    table_blocks = table_d.ap().rearrange("(n r) c -> n (r c)", r=R)

    with ExitStack() as ctx:
        def sb(name, shape, dt=F32):
            return ctx.enter_context(nc.sbuf_tensor(name, shape, dt))

        def sem(name):
            return ctx.enter_context(nc.semaphore(name))

        pb = [ctx.enter_context(nc.psum_tensor(f"bank{i}", [P, 512], F32)) for i in range(8)]

        x_sb = sb("x_sb", [P, NB, F])
        ident = sb("ident", [P, P])
        upper = sb("upper", [P, P])
        ones = sb("ones", [P, P])
        iota_row = sb("iota_row", [P, 512])
        step_no = sb("step_no", [P, KC])
        step_i = sb("step_i", [P, KC], I32)
        mv = sb("mv", [P, NB, 2])
        bn6 = sb("bn6", [P, NB, 6])
        rstd = sb("rstd", [P, NB])
        nmr = sb("nmr", [P, NB])

        work = sb("work", [P, 5200])

        class Phase:
            def __init__(self):
                self.at = 0

            def __call__(self, shape, dt=F32, parts=P):
                n = 1
                for k in shape[1:]:
                    n *= k
                words = n if dt is not BF16 else n // 2
                t = work[0:shape[0], self.at:self.at + words]
                self.at += words
                assert self.at <= 5200
                t = t if dt is F32 else t.bitcast(dt)
                names = "abcd"[:len(shape) - 1]
                sizes = {k: v for k, v in zip(names, shape[1:])}
                return t.rearrange(f"p ({' '.join(names)}) -> p {' '.join(names)}", **sizes) if len(names) > 1 else t
        mixing, edging, slicing = Phase(), Phase(), Phase()

        arena = sb("arena", [P, NB * INNER])
        w_nat = arena[:, 0:R * FC * F].rearrange("p (r c f) -> p r c f", r=R, c=FC)
        w_t = arena[:, R * FC * F:R * FC * F + FC * R * ROW].rearrange("p (c r k) -> p c r k", c=FC, r=R)
        a1 = R * FC * F + FC * R * ROW
        tab_row = arena[:, a1:a1 + 2 * R * ROW].rearrange("p (s k) -> p s k", s=2)
        rows = arena[:, 0:2 * SG * ROW].rearrange("p (s t k) -> p s t k", s=2, t=SG)
        oh = arena[:, 2 * SG * ROW:2 * SG * ROW + 2 * SG * P].rearrange("p (s t d) -> p s t d", s=2, t=SG)
        sw = arena[:, :].rearrange("p (b k) -> p b k", b=NB)
        arena2 = sb("arena2", [P, NB * ROW])
        xnT_all = arena2[:, 0:FC * NB * P].rearrange("p (c n) -> p c n", c=FC)
        acc = arena2[:, :].rearrange("p (b k) -> p b k", b=NB)
        tile_row = arena2[:, 0:TJ * TROW].rearrange("p (j c) -> p j c", j=TJ)
        a2 = [TJ * TROW]

        def place(width, dt=F32):
            a2[0] += TJ * width
            t = arena2[:, a2[0] - TJ * width:a2[0]]
            return (t if dt is F32 else t.bitcast(dt)).rearrange("p (j e) -> p j e", j=TJ)
        dstw_i, dstw = place(P + 2, I32), place(P + 2)
        src_i, typ_i, real = place(P, I32), place(P, I32), place(P)
        step_row = arena2[:, TJ * TROW:(TJ + KC) * TROW].rearrange("p (c k) -> p c k", c=KC)
        tcol = sb("tcol", [P, 8, TJ])
        tcol_i = sb("tcol_i", [P, 4, TJ], I32)
        reached = sb("reached", [P, TJ, 512], BF16)
        ones_bf = sb("ones_bf", [P, 1], BF16)

        dstlT = sb("dstlT", [P, 512])
        idxT = sb("idxT", [P, 512], I32)
        typT = sb("typT", [P, 512])
        tyoh = sb("tyoh", [P, STEPS, R], BF16)
        brow = sb("brow", [P, 512], I32)
        brk = sb("brk", [P, NSG, P + 1])
        brk_sum = sb("brk_sum", [P, NSG, 2])
        adst = sb("adst", [P, NB, 3, H * R], BF16)

        nat = sb("nat", [P, 2048])
        wq_nat, wkv_nat = nat[:, 0:512], nat[:, 512:1536]
        wproj_nat = nat[:, 1536:2048]
        wqT = sb("wqT", [P, FC, F])
        wkvT = sb("wkvT", [P, FC, 2 * F])
        wprojT = sb("wprojT", [P, FC, F])
        wx_nat, wfx = nat[:, 0:1024].rearrange("p (c k) -> p c k", c=FC), nat[:, 1024:2048].rearrange("p (c k) -> p c k", c=FC)
        wout = wkvT[:, :, :].rearrange("p c k -> p (c k)").rearrange("p (c k) -> p c k", k=F)
        slice2 = wprojT[:, 0, 0:P]
        att = sb("att", [P, 2, FC])
        attbd = sb("attbd", [P, FC, 2 * H])
        w_adst = sb("w_adst", [P, FC, H, R])
        bproj_b = sb("bproj_b", [P, F])
        bout_b = sb("bout_b", [P, F])

        xn = sb("xn", [P, 2, F])
        xnT = sb("xnT", [P, 2, FC, P])
        kphi = mixing([P, 2, F])
        kmin = mixing([P, 2, F])
        kexp = mixing([P, 2, F])
        vones = mixing([P, 2, FC, P + 1])
        ad_tmp = sb("ad_tmp", [P, 2, H * R])
        ctx_bd = sb("ctx_bd", [P, FC, P])
        ks_bd = sb("ks_bd", [P, FC, P])
        ctx_sb = sb("ctx_sb", [P, FC, P + 1])
        qbuf = mixing([P, FC, 512])
        qT = mixing([P, FC, 512])
        attT = mixing([P, FC, 512])
        bproj_r, bout_r = kphi[0:1, 0, :], kphi[0:1, 1, :]
        iota_i = qT[:, 0, :].bitcast(I32)
        spread = attT[:, :, :].rearrange("p c n -> p (c n)")

        SLOTS = 18
        idx_stage = sb("idx_stage", [P, 2, SG], I32)
        idle = sb("idle", [P, 2])
        ohT = edging([P, SG, P], BF16)
        sel = edging([P, SG // 2, H, R])
        score = edging([P, SG, H])
        brk2 = edging([P, 2])
        brk_g = edging([P, P + 1])
        run = edging([P, 2, P])
        chunk_row = sb("chunk_row", [1, 4, H, SLOTS])
        carry = edging([1, 2, H, SLOTS])
        carry_flat = edging([1, 2, P])
        ex = sb("ex", [1, 4, H])
        seg0 = edging([P, 2])
        below = edging([P, P])
        wT = edging([P, P])
        w_sb = edging([P, SG, H])
        fac = edging([P, H])
        rden = edging([P, NB, H])

        PAIRS = INNER // P
        late = Phase()
        late.at = 3700
        wqkv = late([DH, 3, DH])
        bx_col = late([P, PAIRS])
        temp_r, bslice_r, bfx_r = late([1, H]), late([1, G]), late([1, INNER])
        itemp_b = slicing([P, INNER])
        itemp_r, bias_r = slicing([1, INNER]), slicing([1, INNER])
        logit = slicing([P, 2, INNER])
        top, tot = slicing([P, 2, H]), slicing([P, 2, H])
        a3 = [0]

        def place3(n):
            a3[0] += n
            return arena2[:, a3[0] - n:a3[0]]
        wxT = place3(PAIRS * F).rearrange("p (q f) -> p q f", q=PAIRS)
        comb = place3(FC * INNER).rearrange("p (c k) -> p c k", c=FC)
        swsum = place3(INNER)
        swxT = place3(FC * INNER).rearrange("p (c k) -> p c k", c=FC)
        v2 = place3(PAIRS * F).rearrange("p (q f) -> p q f", q=PAIRS)
        norm_r = slicing([1, INNER])
        rnorm = place3(INNER)
        tokT = slicing([DH, INNER])
        assert max(slicing.at, edging.at) <= 3700
        qs, ks, vs = place3(INNER), place3(INNER), tokT
        att_g = itemp_b
        attnT = logit[:, 0, :]
        osbd = logit[:, 1, :].rearrange("p (q k) -> p q k", q=PAIRS)
        sws = arena2[:, a3[0] - 2 * INNER:a3[0]].rearrange("p (s k) -> p s k", s=2)
        swT = logit
        y = xn

        sems = {}

        def S(name):
            if name not in sems:
                sems[name] = sem(name)
            return sems[name]

        dve_own, act_own, pool_own, pe_own = S("dve_own"), S("act_own"), S("pool_own"), S("pe_own")
        square = lambda t, o, f: t[:, o * F + f * P:o * F + (f + 1) * P]
        set_jobs = [(w_t[:, :, r, 0:F], [w_nat[:, r, o, f * P:(f + 1) * P] for f in range(FC) for o in range(FC)]) for r in range(R)]
        set_jobs += [(wqT[:, :, :], [square(wq_nat, o, f) for f in range(FC) for o in range(FC)])]
        set_jobs += [(wkvT[:, f, :], [square(wkv_nat, o, f) for o in range(2 * FC)]) for f in range(FC)]
        set_jobs += [(wprojT[:, :, :], [square(wproj_nat, o, f) for f in range(FC) for o in range(FC)])]
        FFN_LOADS = 11 + INNER // P
        NCH = FULL * P // 512

        block = ctx.enter_context(nc.Block())

        @block.sync
        def _(sp):
            sp.sem_inc(S("row_free"), 2)
            sp.sem_inc(S("y_free"), 2)
            sp.wait_ge(S("x_zeroed"), 1)
            sp.dma_start(x_sb[:, 0:FULL, :], x_d[0:FULL * P, :].rearrange("(b p) f -> p b f", p=P)).then_inc(S("ld_x"), 16)
            sp.dma_start(x_sb[0:TAIL, FULL, :], x_d[FULL * P:N, :]).then_inc(S("ld_x"), 16)
            sp.wait_ge(S("pads_set"), 1)
            per = P * P
            flat = [(src_i, src_d), (typ_i, typ_d)]
            whole, rest = TJ - 1, E - (TJ - 1) * per
            for t, d in flat:
                sp.dma_start(t[:, 0:whole, :], d[0:whole * per].rearrange("(j p e) -> p j e", p=P, e=P)).then_inc(S("ld_edges"), 16)
                sp.dma_start(t[0:rest // P, whole, :], d[whole * per:whole * per + rest // P * P].rearrange("(p e) -> p e", e=P)).then_inc(S("ld_edges"), 16)
                sp.dma_start(t[rest // P:rest // P + 1, whole, 0:rest % P], d[E - rest % P:E].rearrange("(p e) -> p e", p=1)).then_inc(S("ld_edges"), 16)
            dt_ = dst_d.tensor
            sp.dma_start(dstw_i[0:1, 0, 1:P + 2], dst_d[0:P + 1].rearrange("(p e) -> p e", p=1)).then_inc(S("ld_edges"), 16)
            sp.dma_start(dstw_i[1:P, 0, :], bass.AP(dt_, P - 1, [[P, P - 1], [1, P + 2]])).then_inc(S("ld_edges"), 16)
            for j in range(1, whole):
                sp.dma_start(dstw_i[:, j, :], bass.AP(dt_, j * per - 1, [[P, P], [1, P + 2]])).then_inc(S("ld_edges"), 16)
            sp.dma_start(dstw_i[0:rest // P, whole, :], bass.AP(dt_, whole * per - 1, [[P, rest // P], [1, P + 2]])).then_inc(S("ld_edges"), 16)
            sp.dma_start(dstw_i[rest // P:rest // P + 1, whole, 0:rest % P + 1],
                         dst_d[E - rest % P - 1:E].rearrange("(p e) -> p e", p=1)).then_inc(S("ld_edges"), 16)
            sp.wait_ge(S("tiles_ready"), 1)
            sp.wait_ge(S("consts"), 1)
            sp.dma_start(tiles_d.ap().rearrange("(j p) c -> p j c", p=P), tile_row[:, :, :]).then_inc(S("tiles_stored"), 16)

            def store_rows(b, s):
                for k in range(2):
                    sp.wait_ge(S(f"tab_taken{k}"), (b + 1) * (R // 2) + 1)
                sp.dma_start(table_blocks[ds(b * P, P), :], tab_row[:, s, :]).then_inc(S("tab_stored"), 16)
                sp.wait_ge(S("tab_stored"), (b + 1) * 16)
                sp.sem_inc(S("row_free"), 1)
            with sp.Fori(0, FULL // 2) as i:
                for s in range(2):
                    store_rows(i * 2 + s, s)
            store_rows(FULL, 0)

            sp.wait_ge(S("proj_taken"), NB + 1)
            sp.wait_ge(S("slice2_zeroed"), 1)
            row = lambda name: a[name].rearrange("(p f) -> p f", p=1)
            ffn = [(wx_nat, a["L0_ffn_W_x"].rearrange("(c p) k -> p c k", p=P)), (wfx, a["L0_ffn_W_fx"].rearrange("(c p) k -> p c k", p=P)),
                   (wout, a["L0_ffn_W_out"].rearrange("(c p) k -> p c k", p=P)),
                   (slice2[0:DH, 0:G], a["L0_ffn_W_slice"]), (slice2[DH:P, G:2 * G], a["L0_ffn_W_slice"]),
                   (wqkv[:, 0, :], a["L0_ffn_W_q"]), (wqkv[:, 1, :], a["L0_ffn_W_k"]), (wqkv[:, 2, :], a["L0_ffn_W_v"]),
                   (temp_r, a["L0_ffn_temperature"].rearrange("a h b c -> (a b) (h c)")), (bslice_r, row("L0_ffn_b_slice")), (bfx_r, row("L0_ffn_b_fx"))]
            ffn += [(bx_col[:, q:q + 1], a["L0_ffn_b_x"][q * P:(q + 1) * P].rearrange("(p o) -> p o", o=1)) for q in range(PAIRS)]
            assert len(ffn) == FFN_LOADS
            for to, frm in ffn:
                sp.dma_start(to, frm).then_inc(S("ld_ffn"), 16)

            def store_out(b, s, n):
                sp.wait_ge(S("y_ready"), b + 3)
                sp.dma_start(out[ds(b * P, n), :], y[0:n, s, :]).then_inc(S("out_done"), 16)
                sp.wait_ge(S("out_done"), (b + 1) * 16)
                sp.sem_inc(S("y_free"), 1)
            with sp.Fori(0, FULL // 2) as i:
                for s in range(2):
                    store_out(i * 2 + s, s, P)
            store_out(FULL, 0, TAIL)

        @block.gpsimd
        def _(pool):
            own = Chain(pool, pool_own)
            g = nc.gpsimd
            g.memset(x_sb[:, FULL, :], 0.0).then_inc(S("x_zeroed"), 1)
            own.link(g.memset(src_i[:, :, :], 0))
            own.link(g.memset(typ_i[:, :, :], 0))
            g.memset(dstw_i[:, :, :], PAD_DST).then_inc(S("pads_set"), 1)
            own.link(g.memset(ident[:, :], 0.0))
            own.link(g.memset(ones[:, :], 1.0))
            own.link(g.memset(ones_bf[:, :], 1.0))
            own.link(g.affine_select(out=ident[:, :], in_=ident[:, :], compare_op=ALU.not_equal, fill=1.0,
                                     base=0, pattern=[[-1, P]], channel_multiplier=1))
            own.link(g.affine_select(out=upper[:, :], in_=ones[:, :], compare_op=ALU.is_gt, fill=0.0,
                                     base=0, pattern=[[1, P]], channel_multiplier=-1))
            own.link(g.iota(iota_i[:, :], pattern=[[1, 512]], base=0, channel_multiplier=0))
            own.link(g.iota(step_i[:, :], pattern=[[P, KC]], base=0, channel_multiplier=1))
            own.link(g.tensor_copy(iota_row[:, :], iota_i[:, :]))
            own.link(g.tensor_copy(step_no[:, :], step_i[:, :]))
            own.link(g.tensor_copy(spread.rearrange("p (k h) -> p k h", h=H), ident[:, :].unsqueeze(2).to_broadcast([P, P, H])))
            own.link(g.memset(idle[:, :], 0.0))
            own.link(g.memset(chunk_row[:, :, :, :], -BIG))
            own.link(g.memset(attbd[:, :, :], 0.0))
            own.link(g.memset(tile_row[:, :, C_BLK + 1], 0.0))
            own.link(g.memset(ctx_bd[:, :, :], 0.0))
            own.link(g.memset(ks_bd[:, :, :], 0.0))
            own.link(g.memset(vones[:, :, :, P:P + 1], 1.0))
            for c in range(FC):
                if c == 0:
                    pool.wait_ge(S("ld_small"), 16 * 4)
                for j in range(P // D):
                    h = c * (P // D) + j
                    q = slice(D * j, D * j + D)
                    for k in range(2):
                        ins = g.tensor_copy(attbd[q, c, k * H + h:k * H + h + 1], att[q, k, c:c + 1])
                        if c == FC - 1 and j == P // D - 1 and k == 1:
                            ins.then_inc(S("consts"), 1)
                        else:
                            own.link(ins)
            pool.wait_ge(S("tiles_stored"), 16)
            pool.wait_ge(S("tk_ready"), 1)
            for c in range(KC):
                g.indirect_dma_start(step_row[:, c, :], None, tiles_d.ap(),
                                     bass.IndirectOffsetOnAxis(tcol_i[:, 3, c:c + 1].bitcast(U32), 0)).then_inc(S("steps_here"), 16)
            pool.wait_ge(S("xnT_ps"), NB)
            pool.wait_ge(S("bcast_done"), 1)
            g.tensor_tensor(x_sb[:, :, :], x_sb[:, :, :], bproj_b[:, :].unsqueeze(1).to_broadcast([P, NB, F]), ALU.add).then_inc(S("x_biased"), 1)

            pool.wait_ge(S("tab_stored"), 16 * NB)
            pool.wait_ge(S("cols_taken"), KC)

            def gather(g_, s):
                pool.wait_ge(S("msg_ps"), g_ * SG + SG)
                own.link(g.tensor_copy(idx_stage[:, s, :], idxT[:, ds(g_ * SG, SG)]))
                g.tensor_tensor(idle[:, 0:1], idle[:, 1:2], idle[:, 1:2], ALU.add)
                for t in range(SG):
                    g.indirect_dma_start(rows[:, s, t, :], None, table_rows,
                                         bass.IndirectOffsetOnAxis(idx_stage[:, s, t:t + 1].bitcast(U32), 0)).then_inc(S(f"rows_here{s}"), 16)
            with pool.Fori(0, NSG // 2) as i:
                own.enter(i, 2)
                for s in range(2):
                    gather(i * 2 + s, s)
                own.leave(NSG // 2)

        @block.scalar
        def _(act):
            own = Chain(act, act_own)
            act.sem_inc(S("tab_taken0"), 1)
            act.sem_inc(S("ohT_ready"), 2)
            s_ = nc.scalar
            for k, name in enumerate(("L0_gnn_attn_src", "L0_gnn_attn_dst")):
                for c in range(FC):
                    act.dma_start(att[:, k, c:c + 1], a[name][c * (P // D):(c + 1) * (P // D), :].rearrange("h (d o) -> (h d) o", o=1)) \
                       .then_inc(S("ld_small"), 16)
            act.dma_start(w_nat, a["L0_gnn_W"].rearrange("r (c o) f -> o r c f", c=FC)).then_inc(S("ld_w"), 16)
            act.dma_start(wq_nat.rearrange("p (c f) -> p c f", c=FC), a["L0_mix_Wq"].rearrange("(c o) f -> o c f", o=P)).then_inc(S("ld_w"), 16)
            act.dma_start(wkv_nat.rearrange("p (c f) -> p c f", f=F), a["L0_mix_Wkv"].rearrange("(c o) f -> o c f", o=P)).then_inc(S("ld_w"), 16)
            act.dma_start(wproj_nat.rearrange("p (c f) -> p c f", c=FC), a["L0_mix_Wproj"].rearrange("(c o) f -> o c f", o=P)).then_inc(S("ld_w"), 16)
            act.dma_start(bproj_r, a["L0_mix_bproj"].rearrange("(p f) -> p f", p=1)).then_inc(S("ld_w"), 16)
            act.dma_start(bout_r, a["L0_ffn_b_out"].rearrange("(p f) -> p f", p=1)).then_inc(S("ld_w"), 16)
            act.wait_ge(S("stats"), 1)
            s_.activation(rstd[:, :], rstd[:, :], ACT.Sqrt).then_inc(S("sqrt_done"), 1)
            n = 0
            for dst, _ in set_jobs:
                act.wait_ge(S("set_ps"), n + 1)
                src = pb[n % 4][:, 0:dst.free_size()]
                if len(dst.shape) == 3:
                    src = src.rearrange("p (a b) -> p a b", a=dst.shape[1])
                s_.activation(dst, src, ACT.Copy).then_inc(S("set_taken"), 1)
                n += 1
            act.wait_ge(S("att_ready"), 1)
            wa = pb[4][:, 0:FC * R * 2 * H].rearrange("p (c r k) -> p c r k", c=FC, r=R)
            for c in range(FC):
                own.link(s_.activation(w_t[:, c, :, F:ROW], wa[:, c, :, 0:H], ACT.Copy))
            for c in range(FC):
                ins = s_.activation(w_adst[:, c, :, :].rearrange("p h r -> p r h"), wa[:, c, :, H:2 * H], ACT.Copy)
                if c == FC - 1:
                    ins.then_inc(S("set_taken"), 1)
                else:
                    own.link(ins)

            def normalise(b, s):
                s_.activation(xn[:, s, :], x_sb[:, ds(b, 1), :].rearrange("p b f -> p (b f)"), ACT.Identity,
                              bias=nmr[:, ds(b, 1)], scale=rstd[:, ds(b, 1)]).then_inc(S("xn_ready"), 1)

            def block_work(b, s, last=False):
                act.wait_ge(S("xnT_ps"), b + 1)
                s_.activation(xnT[:, s, :, :].rearrange("p c n -> p (c n)"), pb[s][:, 0:FC * P], ACT.Copy).then_inc(S("xnT_ready"), 1)
                if not last:
                    normalise(b + 1, 1 - s)
                act.wait_ge(S("kv_ps"), b + 1)
                s_.activation(vones[:, s, :, 0:P], pb[5 + s][:, F:2 * F].rearrange("p (c n) -> p c n", c=FC), ACT.Copy).then_inc(S("v_ready"), 1)
                act.wait_ge(S("kmin_ready"), b + 1)
                s_.activation(kexp[:, s, :], kmin[:, s, :], ACT.Exp).then_inc(S("kexp_ready"), 1)
                for r in range(0, R, 2):
                    act.wait_ge(S("tab_ps0"), b * (R // 2) + r // 2 + 1)
                    if r == 0:
                        act.wait_ge(S("row_free"), b + 1)
                    s_.activation(tab_row[:, s, r * ROW:(r + 1) * ROW], pb[2][:, 0:ROW], ACT.Copy).then_inc(S("tab_taken0"), 1)

            act.wait_ge(S("rstd_ready"), 1)
            act.wait_ge(S("consts"), 1)
            normalise(0, 0)
            with act.Fori(0, FULL // 2) as i:
                for s in range(2):
                    block_work(i * 2 + s, s)
            block_work(FULL, 0, last=True)

            act.wait_ge(S("ctx_ps"), 1)
            own.link(s_.activation(ctx_sb[:, :, :], pb[7][:, 0:FC * (P + 1)].rearrange("p (c n) -> p c n", c=FC), ACT.Copy))
            for c in range(FC):
                for j in range(P // D):
                    q = slice(D * j, D * j + D)
                    own.link(s_.activation(ctx_bd[q, c, D * j:D * j + D], ctx_sb[q, c, D * j:D * j + D], ACT.Copy))
                    ins = s_.activation(ks_bd[q, c, D * j:D * j + D], ones[q, 0:D], ACT.Copy, scale=ctx_sb[q, c, P:P + 1])
                    if c == FC - 1 and j == P // D - 1:
                        ins.then_inc(S("ctx_ready"), 1)
                    else:
                        own.link(ins)

            def chunk(qn, n):
                for c in range(FC):
                    act.wait_ge(S("qmin_ready"), qn * FC + c + 1)
                    s_.activation(qbuf[:, c, 0:n], qbuf[:, c, 0:n], ACT.Exp).then_inc(S("qexp_ready"), 1)
            with act.Fori(0, NCH) as i:
                chunk(i, 512)
            chunk(NCH, TAIL)


            def edges(g_, s):
                for q in range(4):
                    act.wait_ge(S("ohT_ps"), g_ * 4 + q + 1)
                    s_.activation(ohT[:, q * 4:q * 4 + 4, :].rearrange("p t e -> p (t e)"), pb[q % 2][:, :], ACT.Copy).then_inc(S("ohT_ready"), 1)
                act.wait_ge(S("fac_ps"), g_ + 1)
                s_.activation(fac[:, :], pb[5][:, 8:8 + H], ACT.Exp).then_inc(S("fac_ready"), 1)
                act.wait_ge(S("below_ready"), g_ + 1)
                s_.activation(wT[:, :], below[:, :], ACT.Exp).then_inc(S("exp_ready"), 1)
                act.wait_ge(S("w_ps"), g_ + 1)
                wp = pb[4][:, P:2 * P].rearrange("p (t h) -> p t h", h=H)
                s_.activation(w_sb[:, :, :], wp, ACT.Copy).then_inc(S("w_ready"), 1)
                s_.activation(rows[:, s, :, F:ROW], wp, ACT.Copy).then_inc(S("w_ready"), 1)
            with act.Fori(0, NSG // 2) as i:
                for s in range(2):
                    edges(i * 2 + s, s)
            act.wait_ge(S("stats"), 2)
            s_.activation(rstd[:, :], rstd[:, :], ACT.Sqrt).then_inc(S("sqrt_done"), 1)

            act.wait_ge(S("x2_ready"), 1)
            for k in range(2):
                act.wait_ge(S("wxT_ps"), k + 1)
                s_.activation(wxT[:, k * 2:k * 2 + 2, :].rearrange("p q f -> p (q f)"), pb[k][:, :], ACT.Copy).then_inc(S("wxT_ready"), 1)

            def slice_block(b, s, last=False):
                act.wait_ge(S("xnT_ps"), NB + b + 1)
                s_.activation(xnT[:, s, :, :].rearrange("p c n -> p (c n)"), pb[s][:, 0:FC * P], ACT.Copy).then_inc(S("xnT_ready"), 1)
                if not last:
                    normalise(b + 1, 1 - s)
                act.wait_ge(S("logit_ready"), b + 1)
                s_.activation(logit[:, s, :], logit[:, s, :], ACT.Exp).then_inc(S("lexp_ready"), 1)
            act.wait_ge(S("rstd_ready"), 2)
            normalise(0, 0)
            with act.Fori(0, FULL // 2) as i:
                for s in range(2):
                    slice_block(i * 2 + s, s)
            slice_block(FULL, 0, last=True)
            for k, to in enumerate((qs, ks, vs)):
                act.wait_ge(S("qkv_ps"), k + 1)
                s_.activation(to[0:DH, :], pb[k][0:DH, :], ACT.Copy).then_inc(S("qkv_ready"), 1)
            act.wait_ge(S("attn_below"), 1)
            s_.activation(att_g[0:G, :], att_g[0:G, :], ACT.Exp, scale=float(DH) ** -0.5).then_inc(S("attn_exp"), 1)
            for k in range(2):
                act.wait_ge(S("v2_ps"), k + 1)
                s_.activation(v2[:, 2 * k:2 * k + 2, :].rearrange("p q f -> p (q f)"), pb[6 + k][:, :], ACT.Copy).then_inc(S("v2_ready"), 1)

            def stage(b, s):
                s_.activation(sws[:, s, :], sw[:, ds(b, 1), :].rearrange("p b k -> p (b k)"), ACT.Copy).then_inc(S("sws_ready"), 1)

            def out_block(b, s, more):
                act.wait_ge(S("swT_ps"), b + 1)
                s_.activation(swT[:, s, :], pb[s][:, :], ACT.Copy).then_inc(S("swT_ready"), 1)
                if more:
                    stage(b + 2, s)
            act.wait_ge(S("v2_ready"), 2)
            stage(0, 0)
            stage(1, 1)
            with act.Fori(0, FULL // 2 - 1) as i:
                for s in range(2):
                    out_block(i * 2 + s, s, True)
            out_block(FULL - 2, 0, True)
            out_block(FULL - 1, 1, False)
            out_block(FULL, 0, False)

        @block.tensor
        def _(pe):
            mm, tr = nc.tensor.matmul, nc.tensor.transpose
            pe.sem_inc(S("msg_ps"), 2 * SG)
            pe.wait_ge(S("consts"), 1)
            pe.wait_ge(S("ld_w"), 16 * 6)
            pe.wait_ge(S("n_ready"), 1)
            mm(pb[5][:, 0:TJ], upper[:, :], tcol[:, 0, :], start=True, stop=False)
            mm(pb[5][:, 0:TJ], ones[:, :], tcol[:, 1, :], start=False, stop=True).then_inc(S("first_ps"), 1)
            pe.wait_ge(S("cmp_ready"), 1)
            for c in range(KC):
                for j in range(TJ):
                    ins = mm(pb[6][:, c:c + 1], reached[:, j, c * P:(c + 1) * P], ones_bf[:, :], start=(j == 0), stop=(j == TJ - 1))
            ins.then_inc(S("tk_ps"), 1)
            n = 0
            for _, srcs in set_jobs:
                if n >= 4:
                    pe.wait_ge(S("set_taken"), n - 3)
                for k, src in enumerate(srcs):
                    ins = tr(pb[n % 4][:, k * P:(k + 1) * P], src, ident[:, :])
                ins.then_inc(S("set_ps"), 1)
                n += 1
            for c in range(FC):
                for r in range(R):
                    o = (c * R + r) * 2 * H
                    for k in range(FC):
                        ins = mm(pb[4][:, o:o + 2 * H], w_nat[:, r, k, c * P:(c + 1) * P], attbd[:, k, :], start=(k == 0), stop=(k == FC - 1))
            ins.then_inc(S("att_ready"), 1)
            mm(pb[7][:, 0:F], ones[0:1, :], bproj_r, start=True, stop=True)
            mm(pb[7][:, F:2 * F], ones[0:1, :], bout_r, start=True, stop=True).then_inc(S("bcast_ps"), 1)
            pe.wait_ge(S("steprow_ready"), 1)
            pe.wait_ge(S("set_taken"), len(set_jobs))
            for k, col in enumerate((C_DST, C_IDX, C_TYP)):
                for c in range(KC):
                    ins = tr(pb[k][:, c * P:(c + 1) * P], step_row[:, c, col:col + P], ident[:, :])
                ins.then_inc(S("cols_ps"), 1)
            for c in range(KC):
                ins = tr(pb[3][0:1, c * P:(c + 1) * P], tcol[:, 6, c:c + 1], ident[:, :])
            ins.then_inc(S("b_ps"), 1)
            for gq in range(0, NSG, 3):
                bank = pb[5 + (gq // 3) % 2]
                if gq >= 6:
                    pe.wait_ge(S("brk_taken"), gq // 3 - 1)
                for gg in range(gq, min(gq + 3, NSG)):
                    c, off = gg * SG // P, gg * SG % P
                    ins = mm(bank[:, (gg - gq) * (P + 1):(gg - gq + 1) * (P + 1)], spread[:, off * H:off * H + P], step_row[:, c, C_BRK:C_BRK + P + 1], start=True, stop=True)
                ins.then_inc(S("brk_ps"), 1)
            pe.wait_ge(S("brk_taken"), -(-NSG // 3))
            pe.wait_ge(S("bcast_done"), 1)
            pe.wait_ge(S("set_taken"), len(set_jobs) + 1)
            pe.wait_ge(S("cols_taken"), 4)

            mm(pb[7][:, 0:FC * (P + 1)], ks_bd[:, 0, :], iota_row[:, 0:FC * (P + 1)], start=True, stop=False, skip_group_check=True)

            def block_work(b, s, last=False):
                k = TAIL if last else P
                pe.wait_ge(S("xn_ready"), b + 1)
                pe.wait_ge(S("xnT_kept"), b + 1)
                for c in range(FC):
                    ins = tr(pb[s][:, c * P:(c + 1) * P], xn[:, s, c * P:(c + 1) * P], ident[:, :])
                ins.then_inc(S("xnT_ps"), 1)
                pe.wait_ge(S("xnT_ready"), b + 1)
                pe.wait_ge(S("ad_taken"), b + 1)
                for c in range(FC):
                    ins = mm(pb[4][:, 0:H * R], xnT[:, s, c, :], w_adst[:, c, :, :].rearrange("p h r -> p (h r)"), start=(c == 0), stop=(c == FC - 1))
                ins.then_inc(S("ad_ps"), 1)
                for c in range(FC):
                    ins = mm(pb[5 + s][:, :], xnT[:, s, c, :], wkvT[:, c, :], start=(c == 0), stop=(c == FC - 1))
                ins.then_inc(S("kv_ps"), 1)
                for r in range(R):
                    pe.wait_ge(S(f"tab_taken{r % 2}"), b * (R // 2) + r // 2 + 1)
                    for c in range(FC):
                        ins = mm(pb[2 + r % 2][:, 0:ROW], xnT[:, s, c, :], w_t[:, c, r, :], start=(c == 0), stop=(c == FC - 1))
                    ins.then_inc(S(f"tab_ps{r % 2}"), 1)
                pe.wait_ge(S("k_ready"), b + 1)
                pe.wait_ge(S("v_ready"), b + 1)
                for c in range(FC):
                    ins = mm(pb[7][:, c * (P + 1):(c + 1) * (P + 1)], kphi[0:k, s, c * P:(c + 1) * P], vones[0:k, s, c, :],
                             start=False, stop=last and c == FC - 1, skip_group_check=True)
                if last:
                    ins.then_inc(S("ctx_ps"), 1)

            with pe.Fori(0, FULL // 2) as i:
                for s in range(2):
                    block_work(i * 2 + s, s)
            block_work(FULL, 0, last=True)

            pe.wait_ge(S("ctx_ready"), 1)

            def chunk(qn, n):
                cols = ds(qn * 512, n)
                for c in range(FC):
                    for f in range(FC):
                        ins = mm(pb[c][:, 0:n], wqT[:, f, c * P:(c + 1) * P], xnT_all[:, f, cols], start=(f == 0), stop=(f == FC - 1))
                    ins.then_inc(S("q_ps"), 1)
                for c in range(FC):
                    pe.wait_ge(S("q_ready"), qn * FC + c + 1)
                    mm(pb[2 + c][:, 0:n], ctx_bd[:, c, :], qT[:, c, 0:n], start=True, stop=True)
                    mm(pb[4 + c][:, 0:n], ks_bd[:, c, :], qT[:, c, 0:n], start=True, stop=True).then_inc(S("lin_ps"), 1)
                pe.wait_ge(S("lin_ready"), qn * FC + FC)
                for j in range(-(-n // P)):
                    m = min(P, n - j * P)
                    pe.wait_ge(S("proj_taken"), qn * 4 + max(j - 1, 0) + 1)
                    for c in range(FC):
                        ins = mm(pb[6 + j % 2][0:m, 0:F], attT[:, c, j * P:j * P + m], wprojT[:, c, :], start=(c == 0), stop=(c == FC - 1))
                    ins.then_inc(S("proj_ps"), 1)
            with pe.Fori(0, NCH) as i:
                chunk(i, 512)
            chunk(NCH, TAIL)


            def edges(g_, s):
                pe.wait_ge(S("oh_ready"), g_ + 1)
                for q in range(4):
                    pe.wait_ge(S("ohT_ready"), g_ * 4 + q + 1)
                    for t in range(4):
                        ins = tr(pb[q % 2][:, t * P:(t + 1) * P], oh[:, s, q * 4 + t, :], ident[:, :])
                    ins.then_inc(S("ohT_ps"), 1)
                for t in range(SG):
                    if t % 4 == 0:
                        pe.wait_ge(S("ohT_ready"), g_ * 4 + t // 4 + 3)
                    b = pe.value_load(brow[0:1, ds(g_ * SG + t, 1)], min_val=0, max_val=NB - 1)
                    for k in range(3):
                        ins = mm(pb[2 + t // 8][:, t % 8 * H * R:(t % 8 + 1) * H * R], ohT[:, t, :], adst[:, ds(b, 1), k, :].rearrange("p b k -> p (b k)"),
                                 start=(k == 0), stop=(k == 2))
                    if t % 8 == 7:
                        ins.then_inc(S("dsc_ps"), 1)
                pe.wait_ge(S("score_ready"), g_ + 1)
                tr(pb[4][:, 0:P], score[:, :, :].rearrange("p t h -> p (t h)"), ident[:, :]).then_inc(S("scoreT_ps"), 1)
                pe.wait_ge(S("ends_ready"), g_ + 1)
                for k, col in enumerate((run[:, 0, P - 1:P], run[:, 1, 0:1], brk2[:, 0:1], brk2[:, 1:2])):
                    ins = tr(pb[5][0:1, k * P:(k + 1) * P], col, ident[:, :])
                ins.then_inc(S("ends_ps"), 1)
                pe.wait_ge(S("carry_ready"), g_ + 1)
                for k in range(2):
                    ins = mm(pb[5][:, k:k + 1], carry_flat[0:1, k, :], ones[0:1, 0:1], start=True, stop=True)
                ins.then_inc(S("seg0_ps"), 1)
                pe.wait_ge(S("seg0_taken"), g_ + 1)
                mm(pb[5][:, 8:8 + H], oh[0:1, s, 0, :], ex[0:1, 2, :], start=True, stop=True).then_inc(S("fac_ps"), 1)
                pe.wait_ge(S("exp_ready"), g_ + 1)
                tr(pb[4][:, P:2 * P], wT[:, :], ident[:, :]).then_inc(S("w_ps"), 1)
                for t in range(SG):
                    if t % 8 == 0:
                        pe.wait_ge(S("msg_ready"), g_ * 2 + t // 8 + 1)
                    pe.wait_ge(S("acc_added"), g_ * SG + t + 1)
                    mm(pb[6 + t % 2][:, 0:ROW], oh[:, s, t, :], rows[:, s, t, :], start=True, stop=True).then_inc(S("msg_ps"), 1)
            with pe.Fori(0, NSG // 2) as i:
                for s in range(2):
                    edges(i * 2 + s, s)

            pe.wait_ge(S("ld_ffn"), 16 * FFN_LOADS)
            pe.wait_ge(S("acc_added"), STEPS + 2)
            for k in range(2):
                for q in range(2):
                    for c in range(FC):
                        ins = tr(pb[k][:, (q * FC + c) * P:(q * FC + c + 1) * P], wx_nat[:, c, (2 * k + q) * P:(2 * k + q + 1) * P], ident[:, :])
                ins.then_inc(S("wxT_ps"), 1)
            for q in range(PAIRS):
                mm(pb[4][0:1, q * P:(q + 1) * P], bx_col[:, q:q + 1], slice2, start=True, stop=True)
            pe.wait_ge(S("itemp_ready"), 1)
            mm(pb[5][:, :], ones[0:1, :], itemp_r, start=True, stop=True).then_inc(S("itemp_ps"), 1)
            pe.wait_ge(S("wxT_ready"), 2)
            for c in range(FC):
                for q in range(PAIRS):
                    ins = mm(pb[2 + c][:, q * P:(q + 1) * P], wxT[:, q, c * P:(c + 1) * P], slice2, start=True, stop=True)
                ins.then_inc(S("comb_ps"), 1)
            pe.wait_ge(S("comb_ready"), 1)
            for c in range(FC):
                mm(pb[4 + c][:, :], ctx_bd[:, 0, :], iota_row[:, :], start=True, stop=False, skip_group_check=True)

            def slice_block(b, s, last=False):
                k = TAIL if last else P
                pe.wait_ge(S("xn_ready"), NB + b + 1)
                for c in range(FC):
                    ins = tr(pb[s][:, c * P:(c + 1) * P], xn[:, s, c * P:(c + 1) * P], ident[:, :])
                ins.then_inc(S("xnT_ps"), 1)
                pe.wait_ge(S("xnT_ready"), NB + b + 1)
                mm(pb[2 + s][:, :], ones[0:1, :], bias_r, start=True, stop=False)
                for c in range(FC):
                    ins = mm(pb[2 + s][:, :], xnT[:, s, c, :], comb[:, c, :], start=False, stop=(c == FC - 1))
                ins.then_inc(S("logit_ps"), 1)
                pe.wait_ge(S("sw_ready"), b + 1)
                for c in range(FC):
                    ins = mm(pb[4 + c][:, :], xn[0:k, s, c * P:(c + 1) * P], sw[0:k, ds(b, 1), :].rearrange("p b k -> p (b k)"),
                             start=False, stop=last, skip_group_check=True)
                ins.then_inc(S("swx_ps"), 1)
            with pe.Fori(0, FULL // 2) as i:
                for s in range(2):
                    slice_block(i * 2 + s, s)
            slice_block(FULL, 0, last=True)

            heads = [slice(h * G, (h + 1) * G) for h in range(H)]
            pe.wait_ge(S("sw_summed"), NB)
            mm(pb[6][:, :], ones[:, :], swsum, start=True, stop=True).then_inc(S("norm_ps"), 1)
            pe.wait_ge(S("norm_ready"), 1)
            for h in heads:
                for c in range(FC):
                    mm(pb[7][0:DH, h], wfx[:, c, h], swxT[:, c, h], start=(c == 0), stop=False)
                ins = mm(pb[7][0:DH, h], bfx_r[0:1, h], norm_r[0:1, h], start=False, stop=True)
            ins.then_inc(S("tok_ps"), 1)
            pe.wait_ge(S("tok_ready"), 1)
            for k in range(2):
                mm(pb[k][0:DH, :], wqkv[:, k, :], tokT[:, :], start=True, stop=True).then_inc(S("qkv_ps"), 1)
            for h in heads:
                ins = mm(pb[2][0:G, h], tokT[:, h], wqkv[:, 2, :], start=True, stop=True)
            ins.then_inc(S("qkv_ps"), 1)
            pe.wait_ge(S("qkv_ready"), 2)
            for h in heads:
                ins = mm(pb[3][0:G, h], qs[0:DH, h], ks[0:DH, h], start=True, stop=True)
            ins.then_inc(S("attn_ps"), 1)
            pe.wait_ge(S("attn_ready"), 1)
            for h in heads:
                ins = tr(pb[4][0:G, h], att_g[0:G, h], ident[0:G, 0:G])
            ins.then_inc(S("attnT_ps"), 1)
            pe.wait_ge(S("attnT_ready"), 1)
            pe.wait_ge(S("qkv_ready"), 3)
            for n, h in enumerate(heads):
                ins = mm(pb[5][:, h], vs[0:G, n // 2 * P:n // 2 * P + P], attnT[0:G, h], start=True, stop=True)
            ins.then_inc(S("os_ps"), 1)
            pe.wait_ge(S("os_ready"), 1)
            for k in range(2):
                for q in range(2):
                    ins = mm(pb[6 + k][:, q * F:(q + 1) * F], osbd[:, 2 * k + q, :], wout[:, 2 * k + q, :], start=True, stop=True)
                ins.then_inc(S("v2_ps"), 1)

            pe.wait_ge(S("v2_ready"), 2)

            def out_block(b, s):
                pe.wait_ge(S("sws_ready"), b + 1)
                for q in range(PAIRS):
                    ins = tr(pb[s][:, q * P:(q + 1) * P], sws[:, s, q * P:(q + 1) * P], ident[:, :])
                ins.then_inc(S("swT_ps"), 1)
                pe.wait_ge(S("swT_ready"), b + 1)
                pe.wait_ge(S("y_ready"), b + 1)
                for q in range(PAIRS):
                    ins = mm(pb[2 + s][:, 0:F], swT[:, s, q * P:(q + 1) * P], v2[:, q, :], start=(q == 0), stop=(q == PAIRS - 1))
                ins.then_inc(S("y_ps"), 1)
            with pe.Fori(0, FULL // 2) as i:
                for s in range(2):
                    out_block(i * 2 + s, s)
            out_block(FULL, 0)

        @block.vector
        def _(dve):
            own = Chain(dve, dve_own)
            for name, free in (("xnT_kept", 1), ("ad_taken", 1), ("tab_taken1", 1), ("proj_taken", 1), ("acc_added", 2), ("y_ready", 2)):
                dve.sem_inc(S(name), free)
            v = nc.vector
            tt, ts, stt, cp = v.tensor_tensor, v.tensor_scalar, v.scalar_tensor_tensor, v.tensor_copy
            dve.wait_ge(S("ld_edges"), 16 * (6 + 2 + (TJ - 2) + 2))
            own.link(cp(dstw[:, :, :], dstw_i[:, :, :]))
            own.link(cp(tile_row[:, :, C_DST:C_DST + P], dstw_i[:, :, 1:P + 1]))
            own.link(stt(tile_row[:, :, C_IDX:C_IDX + P], src_i[:, :, :], float(R), typ_i[:, :, :], ALU.mult, ALU.add))
            own.link(cp(tile_row[:, :, C_TYP:C_TYP + P], typ_i[:, :, :]))
            own.link(tt(tile_row[:, :, C_BRK:C_BRK + P + 1], dstw[:, :, 1:P + 2], dstw[:, :, 0:P + 1], ALU.not_equal))
            own.link(ts(tile_row[:, :, C_BRK:C_BRK + P + 1], tile_row[:, :, C_BRK:C_BRK + P + 1], -BIG, None, ALU.mult))
            own.link(cp(tcol_i[:, 0, :], dstw_i[:, :, 1]))
            own.link(stt(real, dstw[:, :, 1:P + 1], float(PAD_DST), dstw[:, :, 1:P + 1], ALU.is_lt, ALU.mult))
            own.link(v.tensor_reduce(tcol[:, 2, :], real, AX, ALU.max))
            own.link(cp(tcol_i[:, 1, :], tcol[:, 2, :]))
            own.link(ts(tcol_i[:, 2:4, :], tcol_i[:, 0:2, :], 7, None, ALU.arith_shift_right))
            own.link(cp(tcol[:, 3:5, :], tcol_i[:, 2:4, :]))
            own.link(tt(tcol[:, 0, :], tcol[:, 4, :], tcol[:, 3, :], ALU.subtract))
            own.link(ts(tcol[:, 0, :], tcol[:, 0, :], 1.0, 0.0, ALU.add, ALU.max))
            own.link(v.memset(tcol[:, 1, 0:1], 0.0))
            for j in range(1, TJ):
                own.link(tt(tcol[:, 1, j:j + 1], tcol[:, 1, j - 1:j], tcol[:, 0, j - 1:j], ALU.add))
            cp(tile_row[:, :, C_BLK], tcol[:, 3, :]).then_inc(S("n_ready"), 1)
            dve.wait_ge(S("first_ps"), 1)
            cp(tile_row[:, :, C_FIRST], pb[5][:, 0:TJ]).then_inc(S("tiles_ready"), 1)
            dve.wait_ge(S("tiles_ready"), 1)
            dve.wait_ge(S("consts"), 1)
            tt(reached[:, :, :], iota_row[:, :].unsqueeze(1).to_broadcast([P, TJ, 512]),
               tile_row[:, :, C_FIRST:C_FIRST + 1].to_broadcast([P, TJ, 512]), ALU.is_ge).then_inc(S("cmp_ready"), 1)
            dve.wait_ge(S("ld_x"), 32)

            def node_stats(turn):
                with dve.Fori(0, NB) as i:
                    v.bn_stats(bn6[:, ds(i, 1), :].rearrange("p b k -> p (b k)"), x_sb[:, ds(i, 1), :].rearrange("p b f -> p (b f)")).then_inc(S("bn_done"), 1)
                dve.wait_ge(S("bn_done"), turn * NB)
                for b in range(NB):
                    ins = v.bn_aggr(mv[:, b, :], bn6[:, b, :])
                own.link(ins)

            def node_rstd(turn):
                ts(rstd[:, :], mv[:, :, 1], LN_EPS, None, ALU.add).then_inc(S("stats"), 1)
                dve.wait_ge(S("sqrt_done"), turn)
                own.link(v.reciprocal(rstd[:, :], rstd[:, :]))
                stt(nmr[:, :], mv[:, :, 0], -1.0, rstd[:, :], ALU.mult, ALU.mult).then_inc(S("rstd_ready"), 1)
            node_stats(1)
            dve.wait_ge(S("tk_ps"), 1)
            own.link(ts(tcol[:, 5, :], pb[6][:, 0:KC], -1.0, float(TILES - 1), ALU.add, ALU.min))
            cp(tcol_i[:, 3, :], tcol[:, 5, :]).then_inc(S("tk_ready"), 1)
            node_rstd(1)
            dve.wait_ge(S("bcast_ps"), 1)
            own.link(cp(bproj_b[:, :], pb[7][:, 0:F]))
            cp(bout_b[:, :], pb[7][:, F:2 * F]).then_inc(S("bcast_done"), 1)
            dve.wait_ge(S("steps_here"), 16 * KC)
            own.link(tt(tcol[:, 7, :], step_no[:, :], step_row[:, :, C_FIRST], ALU.subtract))
            own.link(tt(tcol[:, 7, :], tcol[:, 7, :], step_row[:, :, C_BLK], ALU.add))
            own.link(ts(tcol[:, 5, :], tcol[:, 7, :], -float(P), None, ALU.mult))
            for c in range(KC):
                own.link(ts(step_row[:, c, C_DST:C_DST + P], step_row[:, c, C_DST:C_DST + P], tcol[:, 5, c:c + 1], None, ALU.add))
            ts(tcol[:, 6, :], tcol[:, 7, :], float(NB - 1), None, ALU.min).then_inc(S("steprow_ready"), 1)
            for k, dst in enumerate((dstlT, idxT, typT)):
                dve.wait_ge(S("cols_ps"), k + 1)
                cp(dst[:, :], pb[k][:, :]).then_inc(S("cols_taken"), 1)
            dve.wait_ge(S("b_ps"), 1)
            cp(brow[0:1, :], pb[3][0:1, :]).then_inc(S("cols_taken"), 1)
            dve.wait_ge(S("cols_taken"), 4)
            own.link(tt(tyoh[:, :, :], typT[:, 0:STEPS].unsqueeze(2).to_broadcast([P, STEPS, R]),
                        iota_row[:, 0:R].unsqueeze(1).to_broadcast([P, STEPS, R]), ALU.is_equal))
            for q, gq in enumerate(range(0, NSG, 3)):
                m = min(3, NSG - gq)
                dve.wait_ge(S("brk_ps"), q + 1)
                cp(brk[:, gq:gq + m, :], pb[5 + q % 2][:, 0:m * (P + 1)].rearrange("p (g e) -> p g e", g=m)).then_inc(S("brk_taken"), 1)
            dve.wait_ge(S("brk_taken"), -(-NSG // 3))
            for k in range(2):
                own.link(v.tensor_reduce(brk_sum[:, :, k], brk[:, :, k:k + P], AX, ALU.add))

            def block_work(b, s):
                dve.wait_ge(S("xnT_ready"), b + 1)
                cp(xnT_all[:, :, ds(b * P, P)], xnT[:, s, :, :]).then_inc(S("xnT_kept"), 1)
                dve.wait_ge(S("ad_ps"), b + 1)
                part = lambda k: adst[:, ds(b, 1), k, :].rearrange("p b k -> p (b k)")
                own.link(cp(part(0), pb[4][:, 0:H * R]))
                own.link(tt(ad_tmp[:, 0, :], pb[4][:, 0:H * R], part(0), ALU.subtract))
                own.link(cp(part(1), ad_tmp[:, 0, :]))
                own.link(tt(ad_tmp[:, 1, :], ad_tmp[:, 0, :], part(1), ALU.subtract))
                cp(part(2), ad_tmp[:, 1, :]).then_inc(S("ad_taken"), 1)
                dve.wait_ge(S("v_ready"), b + 1)
                ts(kmin[:, s, :], pb[5 + s][:, 0:F], 0.0, None, ALU.min).then_inc(S("kmin_ready"), 1)
                for r in range(1, R, 2):
                    dve.wait_ge(S("tab_ps1"), b * (R // 2) + r // 2 + 1)
                    if r == 1:
                        dve.wait_ge(S("row_free"), b + 1)
                    cp(tab_row[:, s, r * ROW:(r + 1) * ROW], pb[3][:, 0:ROW]).then_inc(S("tab_taken1"), 1)
                    if r == 1:
                        dve.wait_ge(S("kexp_ready"), b + 1)
                        stt(kphi[:, s, :], pb[5 + s][:, 0:F], 0.0, kexp[:, s, :], ALU.max, ALU.add).then_inc(S("k_ready"), 1)
            with dve.Fori(0, FULL // 2) as i:
                own.enter(i, 8)
                for s in range(2):
                    block_work(i * 2 + s, s)
                own.leave(FULL // 2)
            block_work(FULL, 0)

            dve.wait_ge(S("x_biased"), 1)

            def chunk(qn, n):
                for c in range(FC):
                    dve.wait_ge(S("q_ps"), qn * FC + c + 1)
                    ts(qbuf[:, c, 0:n], pb[c][:, 0:n], 0.0, None, ALU.min).then_inc(S("qmin_ready"), 1)
                for c in range(FC):
                    dve.wait_ge(S("qexp_ready"), qn * FC + c + 1)
                    stt(qT[:, c, 0:n], pb[c][:, 0:n], 0.0, qbuf[:, c, 0:n], ALU.max, ALU.add).then_inc(S("q_ready"), 1)
                for c in range(FC):
                    dve.wait_ge(S("lin_ps"), qn * FC + c + 1)
                    own.link(ts(qbuf[:, c, 0:n], pb[4 + c][:, 0:n], 1e-6, None, ALU.max))
                    own.link(v.reciprocal(qbuf[:, c, 0:n], qbuf[:, c, 0:n]))
                    tt(attT[:, c, 0:n], pb[2 + c][:, 0:n], qbuf[:, c, 0:n], ALU.mult).then_inc(S("lin_ready"), 1)
                for j in range(-(-n // P)):
                    m = min(P, n - j * P)
                    dve.wait_ge(S("proj_ps"), qn * 4 + j + 1)
                    xb = x_sb[0:m, ds(qn * 4 + j, 1), :].rearrange("p b f -> p (b f)")
                    tt(xb, xb, pb[6 + j % 2][0:m, 0:F], ALU.add).then_inc(S("proj_taken"), 1)
            with dve.Fori(0, NCH) as i:
                own.enter(i, 4)
                chunk(i, 512)
                own.leave(NCH)
            chunk(NCH, TAIL)

            v.memset(slice2, 0.0).then_inc(S("slice2_zeroed"), 1)
            own.link(v.memset(arena2[:, :], 0.0))
            dve.wait_ge(S("tab_stored"), 16 * NB)
            flatrow = lambda t: t.rearrange("p h c -> p (h c)")
            scan = lambda o, brk_, data, first: v.tensor_tensor_scan(o, brk_, data, first, ALU.add, ALU.max)

            def edges(g_, s, turn):
                tt(oh[:, s, :, :], iota_row[:, 0:P].unsqueeze(1).to_broadcast([P, SG, P]),
                   dstlT[:, ds(g_ * SG, SG)].unsqueeze(2).to_broadcast([P, SG, P]), ALU.is_equal).then_inc(S("oh_ready"), 1)
                own.link(cp(brk_g[:, :], brk[:, ds(g_, 1), :].rearrange("p g e -> p (g e)")))
                own.link(cp(brk2[:, :], brk_sum[:, ds(g_, 1), :].rearrange("p g k -> p (g k)")))
                dve.wait_ge(S(f"rows_here{s}"), (turn + 1) * SG * 16)
                for half in range(2):
                    dve.wait_ge(S("dsc_ps"), g_ * 2 + half + 1)
                    own.link(tt(sel[:, :, :, :], pb[2 + half][:, :].rearrange("p (t h r) -> p t h r", h=H, r=R),
                                tyoh[:, ds(g_ * SG + half * 8, 8), :].unsqueeze(2).to_broadcast([P, SG // 2, H, R]), ALU.mult))
                    own.link(v.tensor_reduce(score[:, half * 8:half * 8 + 8, :], sel[:, :, :, :], AX, ALU.add))
                own.link(tt(score[:, :, :], score[:, :, :], rows[:, s, :, F:ROW], ALU.add))
                stt(score[:, :, :], score[:, :, :], 0.2, score[:, :, :], ALU.mult, ALU.max).then_inc(S("score_ready"), 1)
                dve.wait_ge(S("scoreT_ps"), g_ + 1)
                sT = pb[4][:, 0:P]
                own.link(scan(run[:, 0, :], brk_g[:, 0:P], sT, -BIG))
                scan(run[:, 1, ::-1], brk_g[:, P:0:-1], sT[:, ::-1], -BIG).then_inc(S("ends_ready"), 1)
                dve.wait_ge(S("ends_ps"), g_ + 1)
                own.link(cp(chunk_row[0:1, :, :, 1:SG + 1], pb[5][0:1, :].rearrange("p (k t h) -> p k h t", k=4, h=H)))
                own.link(scan(flatrow(carry[0:1, 0]), flatrow(chunk_row[0:1, 2]), flatrow(chunk_row[0:1, 0]), -BIG))
                own.link(scan(flatrow(carry[0:1, 1])[:, ::-1], flatrow(chunk_row[0:1, 3])[:, ::-1], flatrow(chunk_row[0:1, 1])[:, ::-1], -BIG))
                own.link(cp(carry_flat[0:1, 0, :].rearrange("p (t h) -> p h t", h=H), carry[0:1, 0, :, 0:SG]))
                cp(carry_flat[0:1, 1, :].rearrange("p (t h) -> p h t", h=H), carry[0:1, 1, :, 2:SG + 2]).then_inc(S("carry_ready"), 1)
                own.link(tt(ex[0:1, 0, :], carry[0:1, 1, :, 1], carry[0:1, 0, :, 0], ALU.max))
                own.link(ts(ex[0:1, 0, :], ex[0:1, 0, :], 0.0, None, ALU.max))
                own.link(stt(ex[0:1, 1, :], carry[0:1, 0, :, 0], 0.0, ex[0:1, 0, :], ALU.max, ALU.subtract))
                own.link(ts(ex[0:1, 3, 0:1], brk_g[0:1, 0:1], 0.0, None, ALU.is_equal))
                own.link(ts(ex[0:1, 2, :], ex[0:1, 1, :], ex[0:1, 3, 0:1], None, ALU.mult))
                own.link(cp(chunk_row[0:1, 0, :, 0], carry[0:1, 0, :, SG]))
                dve.wait_ge(S("seg0_ps"), g_ + 1)
                cp(seg0[:, :], pb[5][:, 0:2]).then_inc(S("seg0_taken"), 1)
                dve.wait_ge(S("seg0_taken"), g_ + 1)
                own.link(scan(run[:, 0, :], brk_g[:, 0:P], sT, seg0[:, 0:1]))
                own.link(scan(run[:, 1, ::-1], brk_g[:, P:0:-1], sT[:, ::-1], seg0[:, 1:2]))
                own.link(stt(run[:, 0, :], run[:, 0, :], 0.0, run[:, 1, :], ALU.max, ALU.max))
                tt(below[:, :], sT, run[:, 0, :], ALU.subtract).then_inc(S("below_ready"), 1)
                b = dve.value_load(brow[0:1, ds(g_ * SG, 1)], min_val=0, max_val=NB - 1)
                dve.wait_ge(S("fac_ready"), g_ + 1)
                dve.wait_ge(S("acc_added"), g_ * SG + 2)
                at = acc[:, ds(b, 1), 0:F].rearrange("p b (h d) -> p (b h) d", h=H)
                own.link(tt(at, at, fac[:, :].unsqueeze(2).to_broadcast([P, H, D]), ALU.mult))
                at = acc[:, ds(b, 1), F:ROW].rearrange("p b h -> p (b h)")
                own.link(tt(at, at, fac[:, :], ALU.mult))
                dve.wait_ge(S("w_ready"), g_ * 2 + 2)
                for half in range(2):
                    t8 = slice(half * 8, half * 8 + 8)
                    m = rows[:, s, t8, 0:F].rearrange("p t (h d) -> p t h d", h=H)
                    tt(m, m, w_sb[:, t8, :].unsqueeze(3).to_broadcast([P, SG // 2, H, D]), ALU.mult).then_inc(S("msg_ready"), 1)
                for t in range(SG):
                    b = dve.value_load(brow[0:1, ds(g_ * SG + t, 1)], min_val=0, max_val=NB - 1)
                    dve.wait_ge(S("msg_ps"), g_ * SG + 2 * SG + t + 1)
                    dve.wait_ge(S("acc_added"), g_ * SG + t + 2)
                    at = acc[:, ds(b, 1), :].rearrange("p b k -> p (b k)")
                    tt(at, at, pb[6 + t % 2][:, 0:ROW], ALU.add).then_inc(S("acc_added"), 1)
            with dve.Fori(0, NSG // 2) as i:
                own.enter(i, 46)
                for s in range(2):
                    edges(i * 2 + s, s, i)
                own.leave(NSG // 2)
            dve.wait_ge(S("acc_added"), STEPS + 2)
            own.link(ts(rden[:, :, :], acc[:, :, F:ROW], 1e-12, None, ALU.add))
            own.link(v.reciprocal(rden[:, :, :], rden[:, :, :]))
            at = acc[:, :, 0:F].rearrange("p b (h d) -> p b h d", h=H)
            own.link(tt(at, at, rden[:, :, :].unsqueeze(3).to_broadcast([P, NB, H, D]), ALU.mult))
            tt(x_sb[:, :, :], x_sb[:, :, :], acc[:, :, 0:F], ALU.add).then_inc(S("x2_ready"), 1)
            dve.wait_ge(S("x2_ready"), 1)
            node_stats(2)
            node_rstd(2)

            own.link(v.memset(ctx_bd[:, 0, :], 0.0))
            own.link(v.memset(swsum, 0.0))
            dve.wait_ge(S("ld_ffn"), 16 * FFN_LOADS)
            own.link(ts(temp_r, temp_r, 0.1, 5.0, ALU.max, ALU.min))
            own.link(v.reciprocal(temp_r, temp_r))
            by_head = lambda t: t.rearrange("p (h g) -> p h g", h=H)
            cp(by_head(itemp_r), temp_r.unsqueeze(2).to_broadcast([1, H, G])).then_inc(S("itemp_ready"), 1)
            dve.wait_ge(S("itemp_ps"), 1)
            own.link(cp(itemp_b[:, :], pb[5][:, :]))
            own.link(tt(by_head(bias_r), by_head(pb[4][0:1, :]), bslice_r.unsqueeze(1).to_broadcast([1, H, G]), ALU.add))
            own.link(tt(bias_r, bias_r, itemp_r, ALU.mult))
            for c in range(FC):
                dve.wait_ge(S("comb_ps"), c + 1)
                ins = tt(comb[:, c, :], pb[2 + c][:, :], itemp_b[:, :], ALU.mult)
            ins.then_inc(S("comb_ready"), 1)

            def slice_block(b, s, last=False):
                k = TAIL if last else P
                dve.wait_ge(S("logit_ps"), b + 1)
                lg = by_head(logit[:, s, :])
                own.link(v.tensor_reduce(top[:, s, :], by_head(pb[2 + s][:, :]), AX, ALU.max))
                tt(lg, by_head(pb[2 + s][:, :]), top[:, s, :].unsqueeze(2).to_broadcast([P, H, G]), ALU.subtract).then_inc(S("logit_ready"), 1)
                dve.wait_ge(S("lexp_ready"), b + 1)
                own.link(v.tensor_reduce(tot[:, s, :], lg, AX, ALU.add))
                own.link(v.reciprocal(tot[:, s, :], tot[:, s, :]))
                sw_b = sw[:, ds(b, 1), :].rearrange("p b k -> p (b k)")
                tt(by_head(sw_b), lg, tot[:, s, :].unsqueeze(2).to_broadcast([P, H, G]), ALU.mult).then_inc(S("sw_ready"), 1)
                dve.wait_ge(S("sw_ready"), b + 1)
                tt(swsum[0:k, :], swsum[0:k, :], sw_b[0:k, :], ALU.add).then_inc(S("sw_summed"), 1)
            with dve.Fori(0, FULL // 2) as i:
                own.enter(i, 6)
                for s in range(2):
                    slice_block(i * 2 + s, s)
                own.leave(FULL // 2)
            slice_block(FULL, 0, last=True)

            dve.wait_ge(S("norm_ps"), 1)
            own.link(cp(norm_r, pb[6][0:1, :]))
            own.link(ts(rnorm, pb[6][:, :], 1e-5, None, ALU.add))
            own.link(v.reciprocal(rnorm, rnorm))
            dve.wait_ge(S("swx_ps"), NB)
            for c in range(FC):
                ins = cp(swxT[:, c, :], pb[4 + c][:, :])
            ins.then_inc(S("norm_ready"), 1)
            dve.wait_ge(S("tok_ps"), 1)
            tt(tokT[:, :], pb[7][0:DH, :], rnorm[0:DH, :], ALU.mult).then_inc(S("tok_ready"), 1)
            dve.wait_ge(S("attn_ps"), 1)
            scores, ag = by_head(pb[3][0:G, :]), by_head(att_g[0:G, :])
            own.link(v.tensor_reduce(top[0:G, 0, :], scores, AX, ALU.max))
            tt(ag, scores, top[0:G, 0, :].unsqueeze(2).to_broadcast([G, H, G]), ALU.subtract).then_inc(S("attn_below"), 1)
            dve.wait_ge(S("attn_exp"), 1)
            own.link(v.tensor_reduce(tot[0:G, 0, :], ag, AX, ALU.add))
            own.link(v.reciprocal(tot[0:G, 0, :], tot[0:G, 0, :]))
            tt(ag, ag, tot[0:G, 0, :].unsqueeze(2).to_broadcast([G, H, G]), ALU.mult).then_inc(S("attn_ready"), 1)
            dve.wait_ge(S("attnT_ps"), 1)
            cp(attnT[0:G, :], pb[4][0:G, :]).then_inc(S("attnT_ready"), 1)
            own.link(v.memset(osbd, 0.0))
            dve.wait_ge(S("os_ps"), 1)
            own.link(cp(osbd[0:G, :, 0:G], pb[5][0:G, :].rearrange("p (q e g) -> p q e g", e=2, g=G)[:, :, 0, :]))
            cp(osbd[G:P, :, G:P], pb[5][G:P, :].rearrange("p (q e g) -> p q e g", e=2, g=G)[:, :, 1, :]).then_inc(S("os_ready"), 1)

            def out_block(b, s):
                dve.wait_ge(S("y_ps"), b + 1)
                dve.wait_ge(S("y_free"), b + 1)
                own.link(tt(y[:, s, :], pb[2 + s][:, 0:F], x_sb[:, ds(b, 1), :].rearrange("p b f -> p (b f)"), ALU.add))
                tt(y[:, s, :], y[:, s, :], bout_b[:, :], ALU.add).then_inc(S("y_ready"), 1)
            with dve.Fori(0, FULL // 2) as i:
                own.enter(i, 2)
                for s in range(2):
                    out_block(i * 2 + s, s)
                own.leave(FULL // 2)
            out_block(FULL, 0)


def kernel(**inputs):
    import numpy as np
    import concourse.bacc as bacc
    from concourse.bass_utils import run_bass_kernel_spmd

    nc = bacc.Bacc("TRN2", target_bir_lowering=False, num_devices=1)
    arrays, aps = {}, {}
    for name, value in inputs.items():
        value = np.ascontiguousarray(value)
        arrays[f"in_{name}"] = value
        aps[name] = nc.dram_tensor(f"in_{name}", value.shape, mybir.dt.from_np(value.dtype), kind="ExternalInput").ap()
    out = nc.dram_tensor("out_0", inputs["x"].shape, F32, kind="ExternalOutput").ap()
    build(nc, aps, out)
    result = run_bass_kernel_spmd(nc, [arrays], core_ids=[0])
    return result.results[0]["out_0"]
```

```python
from contextlib import ExitStack

import concourse.bass as bass
from concourse import mybir

ds = bass.ds
ALU = mybir.AluOpType
ACT = mybir.ActivationFunctionType
F32 = mybir.dt.float32
BF16 = mybir.dt.bfloat16
I32 = mybir.dt.int32
U32 = mybir.dt.uint32
AX = mybir.AxisListType.X

P = 128
BIG = 1.0e30
LN_EPS = 1e-5


class Chain:

    def __init__(self, eng, sem):
        self.eng, self.sem, self.base, self.n, self.done = eng, sem, 0, 0, 0

    def link(self, ins):
        self.count(ins)
        self.settle()

    def count(self, ins):
        self.n += 1
        ins.then_inc(self.sem, 1)

    def settle(self):
        self.eng.wait_ge(self.sem, self.base + self.n)

    def enter(self, i, per):
        self.done += self.n
        self.base, self.n, self.per = i * per + self.done, 0, per

    def leave(self, turns):
        assert self.n == self.per, (self.n, self.per)
        self.done += self.per * turns
        self.base, self.n = self.done, 0


def load_blocks(eng, row, most, regs):
    eng.load(regs, row)
    return [eng.snap(r, min_val=0, max_val=most) for r in regs]


def build(nc, a, out):
    x_d, src_d, dst_d, typ_d = a["x"], a["src"], a["dst"], a["edge_type_8"]
    N, F = x_d.shape
    E = src_d.shape[0]
    R = a["L0_gnn_W"].shape[0]
    H, D = a["L0_gnn_attn_src"].shape
    G, DH = a["L0_ffn_W_slice"].shape
    INNER = a["L0_ffn_W_fx"].shape[1]
    FULL, TAIL = N // P, N % P
    NB = FULL + 1
    FC = F // P
    ROW = F + H
    TILES = -(-E // P)
    TJ = -(-TILES // P)
    SG = 16
    NSG = -(-(TILES + NB - 1) // SG)
    STEPS = NSG * SG
    KC = -(-STEPS // P)
    PAD_DST = 8191
    assert H * D == F and SG * H == P and FULL % 2 == 0 and G == DH == 64
    C_DST, C_IDX, C_TYP, C_BRK, C_FIRST, C_BLK, TROW = 0, P, 2 * P, 3 * P, 4 * P + 1, 4 * P + 2, 4 * P + 4

    table_d = nc.dram_tensor("table", (NB * P * R, ROW), F32)
    tiles_d = nc.dram_tensor("tiles", (TJ * P, TROW), F32)
    table_rows = table_d.ap()
    table_blocks = table_d.ap().rearrange("(n r) c -> n (r c)", r=R)

    with ExitStack() as ctx:
        def sb(name, shape, dt=F32):
            return ctx.enter_context(nc.sbuf_tensor(name, shape, dt))

        def sem(name):
            return ctx.enter_context(nc.semaphore(name))

        pb = [ctx.enter_context(nc.psum_tensor(f"bank{i}", [P, 512], F32)) for i in range(8)]

        x_sb = sb("x_sb", [P, NB, F])
        ident = sb("ident", [P, P])
        upper = sb("upper", [P, P])
        ones = sb("ones", [P, P])
        iota_row = sb("iota_row", [P, 512])
        step_no = sb("step_no", [P, KC])
        step_i = sb("step_i", [P, KC], I32)
        mv = sb("mv", [P, NB, 2])
        bn6 = sb("bn6", [P, NB, 6])
        rstd = sb("rstd", [P, NB])
        nmr = sb("nmr", [P, NB])

        work = sb("work", [P, 5690])

        class Phase:
            def __init__(self):
                self.at = 0

            def __call__(self, shape, dt=F32, parts=P):
                n = 1
                for k in shape[1:]:
                    n *= k
                words = n if dt is not BF16 else n // 2
                t = work[0:shape[0], self.at:self.at + words]
                self.at += words
                assert self.at <= 5690, self.at
                t = t if dt is F32 else t.bitcast(dt)
                names = "abcd"[:len(shape) - 1]
                sizes = {k: v for k, v in zip(names, shape[1:])}
                return t.rearrange(f"p ({' '.join(names)}) -> p {' '.join(names)}", **sizes) if len(names) > 1 else t
        mixing, edging, slicing = Phase(), Phase(), Phase()

        arena = sb("arena", [P, NB * INNER])
        w_nat = arena[:, 0:R * FC * F].rearrange("p (r c f) -> p r c f", r=R, c=FC)
        w_t = arena[:, R * FC * F:R * FC * F + FC * R * ROW].rearrange("p (c r k) -> p c r k", c=FC, r=R)
        a1 = R * FC * F + FC * R * ROW
        tab_row = arena[:, a1:a1 + 2 * R * ROW].rearrange("p (s k) -> p s k", s=2)
        rows = arena[:, 0:3 * SG * ROW].rearrange("p (s t k) -> p s t k", s=3, t=SG)
        sw = arena[:, :].rearrange("p (b k) -> p b k", b=NB)
        arena2 = sb("arena2", [P, NB * ROW])
        xnT_all = arena2[:, 0:FC * NB * P].rearrange("p (c n) -> p c n", c=FC)
        acc = arena2[:, :].rearrange("p (b k) -> p b k", b=NB)
        tile_row = arena2[:, 0:TJ * TROW].rearrange("p (j c) -> p j c", j=TJ)
        a2 = [TJ * TROW]

        def place(width, dt=F32):
            a2[0] += TJ * width
            t = arena2[:, a2[0] - TJ * width:a2[0]]
            return (t if dt is F32 else t.bitcast(dt)).rearrange("p (j e) -> p j e", j=TJ)
        dstw_i, dstw = place(P + 2, I32), place(P + 2)
        src_i, typ_i, real = place(P, I32), place(P, I32), place(P)
        step_row = arena2[:, TJ * TROW:(TJ + KC) * TROW].rearrange("p (c k) -> p c k", c=KC)
        tcol = sb("tcol", [P, 8, TJ])
        tcol_i = sb("tcol_i", [P, 4, TJ], I32)
        reached = sb("reached", [P, TJ, 512], BF16)
        ones_bf = sb("ones_bf", [P, 1], BF16)

        dstlT = sb("dstlT", [P, 512])
        idxT = sb("idxT", [P, 512], I32)
        typT = sb("typT", [P, 512])
        tyoh = sb("tyoh", [P, STEPS, R], BF16)
        brow = sb("brow", [P, 512], I32)
        brk = sb("brk", [P, NSG, P + 1])
        brk_sum = sb("brk_sum", [P, NSG, 2])
        adst = sb("adst", [P, NB, H * R])

        weights = sb("weights", [P, 4096])
        oh = weights[:, :].rearrange("p (s t d) -> p s t d", s=2, t=SG)
        nat = weights[:, 0:2048]
        wq_nat, wkv_nat = nat[:, 0:512], nat[:, 512:1536]
        wproj_nat = nat[:, 1536:2048]
        wqT = weights[:, 2048:2560].rearrange("p (c k) -> p c k", c=FC)
        wkvT = weights[:, 2560:3584].rearrange("p (c k) -> p c k", c=FC)
        wprojT = weights[:, 3584:4096].rearrange("p (c k) -> p c k", c=FC)
        wx_nat, wfx = nat[:, 0:1024].rearrange("p (c k) -> p c k", c=FC), nat[:, 1024:2048].rearrange("p (c k) -> p c k", c=FC)
        wout = weights[:, 2560:3584].rearrange("p (c k) -> p c k", k=F)
        slice2 = wprojT[:, 0, 0:P]
        att = sb("att", [P, 2, FC])
        attbd = sb("attbd", [P, FC, 2 * H])
        w_adst = sb("w_adst", [P, FC, H, R])
        bproj_b = sb("bproj_b", [P, F])
        bout_b = sb("bout_b", [P, F])

        xn = sb("xn", [P, 2, F])
        xnT = sb("xnT", [P, 2, FC, P])
        kphi = mixing([P, 2, F])
        kmin = mixing([P, 2, F])
        kexp = mixing([P, 2, F])
        vones = mixing([P, 2, FC, P + 1])
        ctx_bd = sb("ctx_bd", [P, FC, P])
        ks_bd = sb("ks_bd", [P, FC, P])
        ctx_sb = sb("ctx_sb", [P, FC, P + 1])
        qbuf = mixing([P, FC, 512])
        qT = mixing([P, FC, 512])
        attT = mixing([P, FC, 512])
        bproj_r, bout_r = kphi[0:1, 0, :], kphi[0:1, 1, :]
        iota_i = qT[:, 0, :].bitcast(I32)
        spread = attT[:, :, :].rearrange("p c n -> p (c n)")

        SLOTS = 18
        idx_stage = sb("idx_stage", [P, 3, SG], I32)
        idle = sb("idle", [P, 2])
        ohT = edging([P, SG, P])
        sel = edging([P, SG // 2, H, R])
        score = edging([P, SG, H])
        brk2 = edging([P, 2])
        brk_g = edging([P, P + 1])
        run = edging([P, 2, P])
        chunk_row = sb("chunk_row", [1, 4, H, SLOTS])
        carry = edging([1, 2, H, SLOTS])
        carry_flat = edging([1, 2, P])
        ex = sb("ex", [1, 4, H])
        seg0 = edging([P, 2])
        below = edging([P, P])
        wT = edging([P, P])
        w_sb = edging([P, SG, H])
        fac = edging([P, H])
        rden = edging([P, NB, H])

        PAIRS = INNER // P
        late = Phase()
        late.at = 4900
        wqkv = late([DH, 3, DH])
        bx_col = late([P, PAIRS])
        temp_r, bslice_r, bfx_r = late([1, H]), late([1, G]), late([1, INNER])
        itemp_b = slicing([P, INNER])
        itemp_r, bias_r = slicing([1, INNER]), slicing([1, INNER])
        logit = slicing([P, 2, INNER])
        top, tot = slicing([P, 2, H]), slicing([P, 2, H])
        a3 = [0]

        def place3(n):
            a3[0] += n
            return arena2[:, a3[0] - n:a3[0]]
        wxT = place3(PAIRS * F).rearrange("p (q f) -> p q f", q=PAIRS)
        comb = place3(FC * INNER).rearrange("p (c k) -> p c k", c=FC)
        swsum = place3(INNER)
        swxT = place3(FC * INNER).rearrange("p (c k) -> p c k", c=FC)
        v2 = place3(PAIRS * F).rearrange("p (q f) -> p q f", q=PAIRS)
        norm_r = slicing([1, INNER])
        rnorm = place3(INNER)
        tokT = slicing([DH, INNER])
        assert max(slicing.at, edging.at) <= 4900, (slicing.at, edging.at)
        qs, ks, vs = place3(INNER), place3(INNER), tokT
        att_g = itemp_b
        attnT = logit[:, 0, :]
        osbd = logit[:, 1, :].rearrange("p (q k) -> p q k", q=PAIRS)
        sws = arena2[:, a3[0] - 2 * INNER:a3[0]].rearrange("p (s k) -> p s k", s=2)
        swT = logit
        y = xn

        sems = {}

        def S(name):
            if name not in sems:
                sems[name] = sem(name)
            return sems[name]

        dve_own, act_own, pool_own, pe_own = S("dve_own"), S("act_own"), S("pool_own"), S("pe_own")
        square = lambda t, o, f: t[:, o * F + f * P:o * F + (f + 1) * P]
        set_jobs = [(w_t[:, :, r, 0:F], [w_nat[:, r, o, f * P:(f + 1) * P] for f in range(FC) for o in range(FC)]) for r in range(R)]
        set_jobs += [(wqT[:, :, :], [square(wq_nat, o, f) for f in range(FC) for o in range(FC)])]
        set_jobs += [(wkvT[:, f, :], [square(wkv_nat, o, f) for o in range(2 * FC)]) for f in range(FC)]
        set_jobs += [(wprojT[:, :, :], [square(wproj_nat, o, f) for f in range(FC) for o in range(FC)])]
        FFN_LOADS = 11 + INNER // P
        NCH = FULL * P // 512

        block = ctx.enter_context(nc.Block())

        @block.sync
        def _(sp):
            sp.sem_inc(S("row_free"), 2)
            sp.sem_inc(S("y_free"), 2)
            sp.wait_ge(S("x_zeroed"), 1)
            sp.dma_start(x_sb[:, 0:FULL, :], x_d[0:FULL * P, :].rearrange("(b p) f -> p b f", p=P)).then_inc(S("ld_x"), 16)
            sp.dma_start(x_sb[0:TAIL, FULL, :], x_d[FULL * P:N, :]).then_inc(S("ld_x"), 16)
            sp.wait_ge(S("pads_set"), 1)
            per = P * P
            flat = [(src_i, src_d), (typ_i, typ_d)]
            whole, rest = TJ - 1, E - (TJ - 1) * per
            for t, d in flat:
                sp.dma_start(t[:, 0:whole, :], d[0:whole * per].rearrange("(j p e) -> p j e", p=P, e=P)).then_inc(S("ld_edges"), 16)
                sp.dma_start(t[0:rest // P, whole, :], d[whole * per:whole * per + rest // P * P].rearrange("(p e) -> p e", e=P)).then_inc(S("ld_edges"), 16)
                sp.dma_start(t[rest // P:rest // P + 1, whole, 0:rest % P], d[E - rest % P:E].rearrange("(p e) -> p e", p=1)).then_inc(S("ld_edges"), 16)
            dt_ = dst_d.tensor
            sp.dma_start(dstw_i[0:1, 0, 1:P + 2], dst_d[0:P + 1].rearrange("(p e) -> p e", p=1)).then_inc(S("ld_edges"), 16)
            sp.dma_start(dstw_i[1:P, 0, :], bass.AP(dt_, P - 1, [[P, P - 1], [1, P + 2]])).then_inc(S("ld_edges"), 16)
            for j in range(1, whole):
                sp.dma_start(dstw_i[:, j, :], bass.AP(dt_, j * per - 1, [[P, P], [1, P + 2]])).then_inc(S("ld_edges"), 16)
            sp.dma_start(dstw_i[0:rest // P, whole, :], bass.AP(dt_, whole * per - 1, [[P, rest // P], [1, P + 2]])).then_inc(S("ld_edges"), 16)
            sp.dma_start(dstw_i[rest // P:rest // P + 1, whole, 0:rest % P + 1],
                         dst_d[E - rest % P - 1:E].rearrange("(p e) -> p e", p=1)).then_inc(S("ld_edges"), 16)
            sp.wait_ge(S("tiles_ready"), 1)
            sp.wait_ge(S("consts"), 1)
            sp.dma_start(tiles_d.ap().rearrange("(j p) c -> p j c", p=P), tile_row[:, :, :]).then_inc(S("tiles_stored"), 16)

            def store_rows(b, s):
                for k in range(2):
                    sp.wait_ge(S(f"tab_taken{k}"), (b + 1) * (R // 2) + 1)
                sp.dma_start(table_blocks[ds(b * P, P), :], tab_row[:, s, :]).then_inc(S("tab_stored"), 16)
                sp.wait_ge(S("tab_stored"), (b + 1) * 16)
                sp.sem_inc(S("row_free"), 1)
            with sp.Fori(0, FULL // 2) as i:
                for s in range(2):
                    store_rows(i * 2 + s, s)
            store_rows(FULL, 0)

            sp.wait_ge(S("proj_taken"), NB + 1)
            sp.wait_ge(S("slice2_zeroed"), 1)
            row = lambda name: a[name].rearrange("(p f) -> p f", p=1)
            ffn = [(wx_nat, a["L0_ffn_W_x"].rearrange("(c p) k -> p c k", p=P)), (wfx, a["L0_ffn_W_fx"].rearrange("(c p) k -> p c k", p=P)),
                   (wout, a["L0_ffn_W_out"].rearrange("(c p) k -> p c k", p=P)),
                   (slice2[0:DH, 0:G], a["L0_ffn_W_slice"]), (slice2[DH:P, G:2 * G], a["L0_ffn_W_slice"]),
                   (wqkv[:, 0, :], a["L0_ffn_W_q"]), (wqkv[:, 1, :], a["L0_ffn_W_k"]), (wqkv[:, 2, :], a["L0_ffn_W_v"]),
                   (temp_r, a["L0_ffn_temperature"].rearrange("a h b c -> (a b) (h c)")), (bslice_r, row("L0_ffn_b_slice")), (bfx_r, row("L0_ffn_b_fx"))]
            ffn += [(bx_col[:, q:q + 1], a["L0_ffn_b_x"][q * P:(q + 1) * P].rearrange("(p o) -> p o", o=1)) for q in range(PAIRS)]
            assert len(ffn) == FFN_LOADS
            for to, frm in ffn:
                sp.dma_start(to, frm).then_inc(S("ld_ffn"), 16)

            def store_out(b, s, n):
                sp.wait_ge(S("y_ready"), b + 3)
                sp.dma_start(out[ds(b * P, n), :], y[0:n, s, :]).then_inc(S("out_done"), 16)
                sp.wait_ge(S("out_done"), (b + 1) * 16)
                sp.sem_inc(S("y_free"), 1)
            with sp.Fori(0, FULL // 2) as i:
                for s in range(2):
                    store_out(i * 2 + s, s, P)
            store_out(FULL, 0, TAIL)

        @block.gpsimd
        def _(pool):
            own = Chain(pool, pool_own)
            g = nc.gpsimd
            g.memset(x_sb[:, FULL, :], 0.0).then_inc(S("x_zeroed"), 1)
            own.link(g.memset(src_i[:, :, :], 0))
            own.link(g.memset(typ_i[:, :, :], 0))
            g.memset(dstw_i[:, :, :], PAD_DST).then_inc(S("pads_set"), 1)
            own.link(g.memset(ident[:, :], 0.0))
            own.link(g.memset(ones[:, :], 1.0))
            own.link(g.memset(ones_bf[:, :], 1.0))
            own.link(g.affine_select(out=ident[:, :], in_=ident[:, :], compare_op=ALU.not_equal, fill=1.0,
                                     base=0, pattern=[[-1, P]], channel_multiplier=1))
            own.link(g.affine_select(out=upper[:, :], in_=ones[:, :], compare_op=ALU.is_gt, fill=0.0,
                                     base=0, pattern=[[1, P]], channel_multiplier=-1))
            own.link(g.iota(iota_i[:, :], pattern=[[1, 512]], base=0, channel_multiplier=0))
            own.link(g.iota(step_i[:, :], pattern=[[P, KC]], base=0, channel_multiplier=1))
            own.link(g.tensor_copy(iota_row[:, :], iota_i[:, :]))
            own.link(g.tensor_copy(step_no[:, :], step_i[:, :]))
            own.link(g.tensor_copy(spread.rearrange("p (k h) -> p k h", h=H), ident[:, :].unsqueeze(2).to_broadcast([P, P, H])))
            own.link(g.memset(idle[:, :], 0.0))
            own.link(g.memset(chunk_row[:, :, :, :], -BIG))
            own.link(g.memset(attbd[:, :, :], 0.0))
            own.link(g.memset(tile_row[:, :, C_BLK + 1], 0.0))
            own.link(g.memset(ctx_bd[:, :, :], 0.0))
            own.link(g.memset(ks_bd[:, :, :], 0.0))
            own.link(g.memset(vones[:, :, :, P:P + 1], 1.0))
            for c in range(FC):
                if c == 0:
                    pool.wait_ge(S("ld_small"), 16 * 4)
                for j in range(P // D):
                    h = c * (P // D) + j
                    q = slice(D * j, D * j + D)
                    for k in range(2):
                        ins = g.tensor_copy(attbd[q, c, k * H + h:k * H + h + 1], att[q, k, c:c + 1])
                        if c == FC - 1 and j == P // D - 1 and k == 1:
                            ins.then_inc(S("consts"), 1)
                        else:
                            own.link(ins)
            pool.wait_ge(S("tiles_stored"), 16)
            pool.wait_ge(S("tk_ready"), 1)
            for c in range(KC):
                g.indirect_dma_start(step_row[:, c, :], None, tiles_d.ap(),
                                     bass.IndirectOffsetOnAxis(tcol_i[:, 3, c:c + 1].bitcast(U32), 0)).then_inc(S("steps_here"), 16)
            pool.wait_ge(S("xnT_ps"), NB)
            pool.wait_ge(S("bcast_done"), 1)
            g.tensor_tensor(x_sb[:, :, :], x_sb[:, :, :], bproj_b[:, :].unsqueeze(1).to_broadcast([P, NB, F]), ALU.add).then_inc(S("x_biased"), 1)

            pool.wait_ge(S("tab_stored"), 16 * NB)
            pool.wait_ge(S("cols_taken"), KC)

            def gather(g_, s):
                pool.wait_ge(S("msg_ps"), g_ * SG + SG)
                own.link(g.tensor_copy(idx_stage[:, s, :], idxT[:, ds(g_ * SG, SG)]))
                g.tensor_tensor(idle[:, 0:1], idle[:, 1:2], idle[:, 1:2], ALU.add)
                for t in range(SG):
                    g.indirect_dma_start(rows[:, s, t, :], None, table_rows,
                                         bass.IndirectOffsetOnAxis(idx_stage[:, s, t:t + 1].bitcast(U32), 0)).then_inc(S(f"rows_here{s}"), 16)
            with pool.Fori(0, NSG // 3) as i:
                own.enter(i, 3)
                for s in range(3):
                    gather(i * 3 + s, s)
                own.leave(NSG // 3)
            for g_ in range(NSG // 3 * 3, NSG):
                gather(g_, g_ % 3)

        @block.scalar
        def _(act):
            own = Chain(act, act_own)
            act.sem_inc(S("tab_taken0"), 1)
            act.sem_inc(S("ohT_ready"), 2)
            s_ = nc.scalar
            for k, name in enumerate(("L0_gnn_attn_src", "L0_gnn_attn_dst")):
                for c in range(FC):
                    act.dma_start(att[:, k, c:c + 1], a[name][c * (P // D):(c + 1) * (P // D), :].rearrange("h (d o) -> (h d) o", o=1)) \
                       .then_inc(S("ld_small"), 16)
            act.dma_start(w_nat, a["L0_gnn_W"].rearrange("r (c o) f -> o r c f", c=FC)).then_inc(S("ld_w"), 16)
            act.dma_start(wq_nat.rearrange("p (c f) -> p c f", c=FC), a["L0_mix_Wq"].rearrange("(c o) f -> o c f", o=P)).then_inc(S("ld_w"), 16)
            act.dma_start(wkv_nat.rearrange("p (c f) -> p c f", f=F), a["L0_mix_Wkv"].rearrange("(c o) f -> o c f", o=P)).then_inc(S("ld_w"), 16)
            act.dma_start(wproj_nat.rearrange("p (c f) -> p c f", c=FC), a["L0_mix_Wproj"].rearrange("(c o) f -> o c f", o=P)).then_inc(S("ld_w"), 16)
            act.dma_start(bproj_r, a["L0_mix_bproj"].rearrange("(p f) -> p f", p=1)).then_inc(S("ld_w"), 16)
            act.dma_start(bout_r, a["L0_ffn_b_out"].rearrange("(p f) -> p f", p=1)).then_inc(S("ld_w"), 16)
            act.wait_ge(S("stats"), 1)
            s_.activation(rstd[:, :], rstd[:, :], ACT.Sqrt).then_inc(S("sqrt_done"), 1)
            n = 0
            for dst, _ in set_jobs:
                act.wait_ge(S("set_ps"), n + 1)
                src = pb[n % 4][:, 0:dst.free_size()]
                if len(dst.shape) == 3:
                    src = src.rearrange("p (a b) -> p a b", a=dst.shape[1])
                s_.activation(dst, src, ACT.Copy).then_inc(S("set_taken"), 1)
                n += 1
            act.wait_ge(S("att_ready"), 1)
            wa = pb[4][:, 0:FC * R * 2 * H].rearrange("p (c r k) -> p c r k", c=FC, r=R)
            for c in range(FC):
                own.link(s_.activation(w_t[:, c, :, F:ROW], wa[:, c, :, 0:H], ACT.Copy))
            for c in range(FC):
                ins = s_.activation(w_adst[:, c, :, :].rearrange("p h r -> p r h"), wa[:, c, :, H:2 * H], ACT.Copy)
                if c == FC - 1:
                    ins.then_inc(S("set_taken"), 1)
                else:
                    own.link(ins)

            def normalise(b, s):
                s_.activation(xn[:, s, :], x_sb[:, ds(b, 1), :].rearrange("p b f -> p (b f)"), ACT.Identity,
                              bias=nmr[:, ds(b, 1)], scale=rstd[:, ds(b, 1)]).then_inc(S("xn_ready"), 1)

            def block_work(b, s, last=False):
                act.wait_ge(S("xnT_ps"), b + 1)
                s_.activation(xnT[:, s, :, :].rearrange("p c n -> p (c n)"), pb[s][:, 0:FC * P], ACT.Copy).then_inc(S("xnT_ready"), 1)
                if not last:
                    normalise(b + 1, 1 - s)
                act.wait_ge(S("kv_ps"), b + 1)
                s_.activation(vones[:, s, :, 0:P], pb[5 + s][:, F:2 * F].rearrange("p (c n) -> p c n", c=FC), ACT.Copy).then_inc(S("v_ready"), 1)
                act.wait_ge(S("kmin_ready"), b + 1)
                s_.activation(kexp[:, s, :], kmin[:, s, :], ACT.Exp).then_inc(S("kexp_ready"), 1)
                for r in range(0, R, 2):
                    act.wait_ge(S("tab_ps0"), b * (R // 2) + r // 2 + 1)
                    if r == 0:
                        act.wait_ge(S("row_free"), b + 1)
                    s_.activation(tab_row[:, s, r * ROW:(r + 1) * ROW], pb[2][:, 0:ROW], ACT.Copy).then_inc(S("tab_taken0"), 1)

            act.wait_ge(S("rstd_ready"), 1)
            act.wait_ge(S("consts"), 1)
            normalise(0, 0)
            with act.Fori(0, FULL // 2) as i:
                for s in range(2):
                    block_work(i * 2 + s, s)
            block_work(FULL, 0, last=True)

            act.wait_ge(S("ctx_ps"), 1)
            own.link(s_.activation(ctx_sb[:, :, :], pb[7][:, 0:FC * (P + 1)].rearrange("p (c n) -> p c n", c=FC), ACT.Copy))
            for c in range(FC):
                for j in range(P // D):
                    q = slice(D * j, D * j + D)
                    own.link(s_.activation(ctx_bd[q, c, D * j:D * j + D], ctx_sb[q, c, D * j:D * j + D], ACT.Copy))
                    ins = s_.activation(ks_bd[q, c, D * j:D * j + D], ones[q, 0:D], ACT.Copy, scale=ctx_sb[q, c, P:P + 1])
                    if c == FC - 1 and j == P // D - 1:
                        ins.then_inc(S("ctx_ready"), 1)
                    else:
                        own.link(ins)

            def chunk(qn, n):
                for c in range(FC):
                    act.wait_ge(S("qmin_ready"), qn * FC + c + 1)
                    s_.activation(qbuf[:, c, 0:n], qbuf[:, c, 0:n], ACT.Exp).then_inc(S("qexp_ready"), 1)
            with act.Fori(0, NCH) as i:
                chunk(i, 512)
            chunk(NCH, TAIL)


            def turn(g_, u, third, scores=True, messages=True):
                if not scores:
                    return
                n, slot = g_ + 1, (u + 1) % 3
                for q in range(4):
                    act.wait_ge(S("ohT_ps"), n * 4 + q + 1)
                    s_.activation(ohT[:, q * 4:q * 4 + 4, :].rearrange("p t e -> p (t e)"), pb[q % 2][:, :], ACT.Copy).then_inc(S("ohT_ready"), 1)
                act.wait_ge(S("fac_ps"), n + 1)
                s_.activation(fac[:, :], pb[5][:, 8:8 + H], ACT.Exp).then_inc(S("fac_ready"), 1)
                act.wait_ge(S("below_ready"), n + 1)
                s_.activation(wT[:, :], below[:, :], ACT.Exp).then_inc(S("exp_ready"), 1)
                act.wait_ge(S("w_ps"), n + 1)
                wp = pb[4][:, P:2 * P].rearrange("p (t h) -> p t h", h=H)
                s_.activation(w_sb[:, :, :], wp, ACT.Copy).then_inc(S("w_ready"), 1)
                s_.activation(rows[:, slot, :, F:ROW], wp, ACT.Copy).then_inc(S("w_ready"), 1)
            turn(-1, -1, 0, messages=False)
            with act.Fori(0, NSG // 6) as i:
                for u in range(6):
                    turn(i * 6 + u, u, i * 2)
            for g_ in range(NSG // 6 * 6, NSG):
                turn(g_, g_ % 6, NSG // 6 * 2, scores=g_ + 1 < NSG)
            act.wait_ge(S("stats"), 2)
            s_.activation(rstd[:, :], rstd[:, :], ACT.Sqrt).then_inc(S("sqrt_done"), 1)

            act.wait_ge(S("x2_ready"), 1)
            for k in range(2):
                act.wait_ge(S("wxT_ps"), k + 1)
                s_.activation(wxT[:, k * 2:k * 2 + 2, :].rearrange("p q f -> p (q f)"), pb[k][:, :], ACT.Copy).then_inc(S("wxT_ready"), 1)

            def slice_block(b, s, last=False):
                act.wait_ge(S("xnT_ps"), NB + b + 1)
                s_.activation(xnT[:, s, :, :].rearrange("p c n -> p (c n)"), pb[s][:, 0:FC * P], ACT.Copy).then_inc(S("xnT_ready"), 1)
                if not last:
                    normalise(b + 1, 1 - s)
                act.wait_ge(S("logit_ready"), b + 1)
                s_.activation(logit[:, s, :], logit[:, s, :], ACT.Exp).then_inc(S("lexp_ready"), 1)
            act.wait_ge(S("rstd_ready"), 2)
            normalise(0, 0)
            with act.Fori(0, FULL // 2) as i:
                for s in range(2):
                    slice_block(i * 2 + s, s)
            slice_block(FULL, 0, last=True)
            for k, to in enumerate((qs, ks, vs)):
                act.wait_ge(S("qkv_ps"), k + 1)
                s_.activation(to[0:DH, :], pb[k][0:DH, :], ACT.Copy).then_inc(S("qkv_ready"), 1)
            act.wait_ge(S("attn_below"), 1)
            s_.activation(att_g[0:G, :], att_g[0:G, :], ACT.Exp, scale=float(DH) ** -0.5).then_inc(S("attn_exp"), 1)
            for k in range(2):
                act.wait_ge(S("v2_ps"), k + 1)
                s_.activation(v2[:, 2 * k:2 * k + 2, :].rearrange("p q f -> p (q f)"), pb[6 + k][:, :], ACT.Copy).then_inc(S("v2_ready"), 1)

            def stage(b, s):
                s_.activation(sws[:, s, :], sw[:, ds(b, 1), :].rearrange("p b k -> p (b k)"), ACT.Copy).then_inc(S("sws_ready"), 1)

            def out_block(b, s, more):
                act.wait_ge(S("swT_ps"), b + 1)
                s_.activation(swT[:, s, :], pb[s][:, :], ACT.Copy).then_inc(S("swT_ready"), 1)
                if more:
                    stage(b + 2, s)
            act.wait_ge(S("v2_ready"), 2)
            stage(0, 0)
            stage(1, 1)
            with act.Fori(0, FULL // 2 - 1) as i:
                for s in range(2):
                    out_block(i * 2 + s, s, True)
            out_block(FULL - 2, 0, True)
            out_block(FULL - 1, 1, False)
            out_block(FULL, 0, False)

        @block.tensor
        def _(pe):
            mm, tr = nc.tensor.matmul, nc.tensor.transpose
            pe.sem_inc(S("msg_ps"), 3 * SG)
            pe.wait_ge(S("consts"), 1)
            pe.wait_ge(S("ld_w"), 16 * 6)
            pe.wait_ge(S("n_ready"), 1)
            mm(pb[5][:, 0:TJ], upper[:, :], tcol[:, 0, :], start=True, stop=False)
            mm(pb[5][:, 0:TJ], ones[:, :], tcol[:, 1, :], start=False, stop=True).then_inc(S("first_ps"), 1)
            pe.wait_ge(S("cmp_ready"), 1)
            for c in range(KC):
                for j in range(TJ):
                    ins = mm(pb[6][:, c:c + 1], reached[:, j, c * P:(c + 1) * P], ones_bf[:, :], start=(j == 0), stop=(j == TJ - 1))
            ins.then_inc(S("tk_ps"), 1)
            n = 0
            for _, srcs in set_jobs:
                if n >= 4:
                    pe.wait_ge(S("set_taken"), n - 3)
                for k, src in enumerate(srcs):
                    ins = tr(pb[n % 4][:, k * P:(k + 1) * P], src, ident[:, :])
                ins.then_inc(S("set_ps"), 1)
                n += 1
            for c in range(FC):
                for r in range(R):
                    o = (c * R + r) * 2 * H
                    for k in range(FC):
                        ins = mm(pb[4][:, o:o + 2 * H], w_nat[:, r, k, c * P:(c + 1) * P], attbd[:, k, :], start=(k == 0), stop=(k == FC - 1))
            ins.then_inc(S("att_ready"), 1)
            mm(pb[7][:, 0:F], ones[0:1, :], bproj_r, start=True, stop=True)
            mm(pb[7][:, F:2 * F], ones[0:1, :], bout_r, start=True, stop=True).then_inc(S("bcast_ps"), 1)
            pe.wait_ge(S("steprow_ready"), 1)
            pe.wait_ge(S("set_taken"), len(set_jobs))
            for k, col in enumerate((C_DST, C_IDX, C_TYP)):
                for c in range(KC):
                    ins = tr(pb[k][:, c * P:(c + 1) * P], step_row[:, c, col:col + P], ident[:, :])
                ins.then_inc(S("cols_ps"), 1)
            for c in range(KC):
                ins = tr(pb[3][0:1, c * P:(c + 1) * P], tcol[:, 6, c:c + 1], ident[:, :])
            ins.then_inc(S("b_ps"), 1)
            for gq in range(0, NSG, 3):
                bank = pb[5 + (gq // 3) % 2]
                if gq >= 6:
                    pe.wait_ge(S("brk_taken"), gq // 3 - 1)
                for gg in range(gq, min(gq + 3, NSG)):
                    c, off = gg * SG // P, gg * SG % P
                    ins = mm(bank[:, (gg - gq) * (P + 1):(gg - gq + 1) * (P + 1)], spread[:, off * H:off * H + P], step_row[:, c, C_BRK:C_BRK + P + 1], start=True, stop=True)
                ins.then_inc(S("brk_ps"), 1)
            pe.wait_ge(S("brk_taken"), -(-NSG // 3))
            pe.wait_ge(S("bcast_done"), 1)
            pe.wait_ge(S("set_taken"), len(set_jobs) + 1)
            pe.wait_ge(S("cols_taken"), 4)

            mm(pb[7][:, 0:FC * (P + 1)], ks_bd[:, 0, :], iota_row[:, 0:FC * (P + 1)], start=True, stop=False, skip_group_check=True)

            def block_work(b, s, last=False):
                k = TAIL if last else P
                pe.wait_ge(S("xn_ready"), b + 1)
                pe.wait_ge(S("xnT_kept"), b + 1)
                for c in range(FC):
                    ins = tr(pb[s][:, c * P:(c + 1) * P], xn[:, s, c * P:(c + 1) * P], ident[:, :])
                ins.then_inc(S("xnT_ps"), 1)
                pe.wait_ge(S("xnT_ready"), b + 1)
                pe.wait_ge(S("ad_taken"), b + 1)
                for c in range(FC):
                    ins = mm(pb[4][:, 0:H * R], xnT[:, s, c, :], w_adst[:, c, :, :].rearrange("p h r -> p (h r)"), start=(c == 0), stop=(c == FC - 1))
                ins.then_inc(S("ad_ps"), 1)
                for c in range(FC):
                    ins = mm(pb[5 + s][:, :], xnT[:, s, c, :], wkvT[:, c, :], start=(c == 0), stop=(c == FC - 1))
                ins.then_inc(S("kv_ps"), 1)
                for r in range(R):
                    pe.wait_ge(S(f"tab_taken{r % 2}"), b * (R // 2) + r // 2 + 1)
                    for c in range(FC):
                        ins = mm(pb[2 + r % 2][:, 0:ROW], xnT[:, s, c, :], w_t[:, c, r, :], start=(c == 0), stop=(c == FC - 1))
                    ins.then_inc(S(f"tab_ps{r % 2}"), 1)
                pe.wait_ge(S("k_ready"), b + 1)
                pe.wait_ge(S("v_ready"), b + 1)
                for c in range(FC):
                    ins = mm(pb[7][:, c * (P + 1):(c + 1) * (P + 1)], kphi[0:k, s, c * P:(c + 1) * P], vones[0:k, s, c, :],
                             start=False, stop=last and c == FC - 1, skip_group_check=True)
                if last:
                    ins.then_inc(S("ctx_ps"), 1)

            with pe.Fori(0, FULL // 2) as i:
                for s in range(2):
                    block_work(i * 2 + s, s)
            block_work(FULL, 0, last=True)

            pe.wait_ge(S("ctx_ready"), 1)

            def chunk(qn, n):
                cols = ds(qn * 512, n)
                for c in range(FC):
                    for f in range(FC):
                        ins = mm(pb[c][:, 0:n], wqT[:, f, c * P:(c + 1) * P], xnT_all[:, f, cols], start=(f == 0), stop=(f == FC - 1))
                    ins.then_inc(S("q_ps"), 1)
                for c in range(FC):
                    pe.wait_ge(S("q_ready"), qn * FC + c + 1)
                    mm(pb[2 + c][:, 0:n], ctx_bd[:, c, :], qT[:, c, 0:n], start=True, stop=True)
                    mm(pb[4 + c][:, 0:n], ks_bd[:, c, :], qT[:, c, 0:n], start=True, stop=True).then_inc(S("lin_ps"), 1)
                pe.wait_ge(S("lin_ready"), qn * FC + FC)
                for j in range(-(-n // P)):
                    m = min(P, n - j * P)
                    pe.wait_ge(S("proj_taken"), qn * 4 + max(j - 1, 0) + 1)
                    for c in range(FC):
                        ins = mm(pb[6 + j % 2][0:m, 0:F], attT[:, c, j * P:j * P + m], wprojT[:, c, :], start=(c == 0), stop=(c == FC - 1))
                    ins.then_inc(S("proj_ps"), 1)
            with pe.Fori(0, NCH) as i:
                chunk(i, 512)
            chunk(NCH, TAIL)


            regs = [pe.alloc_register(f"pe_block{k}") for k in range(8)]

            def turn(g_, u, third, scores=True, messages=True):
                n, so, slot, mo = g_ + 1, (u + 1) % 2, u % 3, u % 2

                def send(t0, t1):
                    for t in range(t0, t1) if messages else ():
                        if t % 8 == 0:
                            pe.wait_ge(S("msg_ready"), g_ * 2 + t // 8 + 1)
                        pe.wait_ge(S("acc_added"), g_ * SG + t + 1)
                        mm(pb[6 + t % 2][:, 0:ROW], oh[:, mo, t, :], rows[:, slot, t, :], start=True, stop=True).then_inc(S("msg_ps"), 1)

                def dst_scores(half):
                    bs = load_blocks(pe, brow[0:1, ds(n * SG + half * 8, 8)], NB - 1, regs)
                    for t in range(half * 8, half * 8 + 8):
                        if t % 4 == 0:
                            pe.wait_ge(S("ohT_ready"), n * 4 + t // 4 + 3)
                        ins = mm(pb[2 + half][:, t % 8 * H * R:(t % 8 + 1) * H * R], ohT[:, t, :], adst[:, ds(bs[t % 8], 1), :].rearrange("p b k -> p (b k)"),
                                 start=True, stop=True)
                    ins.then_inc(S("dsc_ps"), 1)
                if not scores:
                    send(0, SG)
                    return
                pe.wait_ge(S("oh_ready"), n + 1)
                for q in range(4):
                    pe.wait_ge(S("ohT_ready"), n * 4 + q + 1)
                    for t in range(4):
                        ins = tr(pb[q % 2][:, t * P:(t + 1) * P], oh[:, so, q * 4 + t, :], ident[:, :])
                    ins.then_inc(S("ohT_ps"), 1)
                send(0, 2)
                dst_scores(0)
                send(2, 4)
                dst_scores(1)
                send(4, 8)
                pe.wait_ge(S("score_ready"), n + 1)
                tr(pb[4][:, 0:P], score[:, :, :].rearrange("p t h -> p (t h)"), ident[:, :]).then_inc(S("scoreT_ps"), 1)
                send(8, 10)
                pe.wait_ge(S("ends_ready"), n + 1)
                for k, col in enumerate((run[:, 0, P - 1:P], run[:, 1, 0:1], brk2[:, 0:1], brk2[:, 1:2])):
                    ins = tr(pb[5][0:1, k * P:(k + 1) * P], col, ident[:, :])
                ins.then_inc(S("ends_ps"), 1)
                send(10, 12)
                pe.wait_ge(S("carry_ready"), n + 1)
                for k in range(2):
                    ins = mm(pb[5][:, k:k + 1], carry_flat[0:1, k, :], ones[0:1, 0:1], start=True, stop=True)
                ins.then_inc(S("seg0_ps"), 1)
                send(12, 14)
                pe.wait_ge(S("seg0_taken"), n + 1)
                mm(pb[5][:, 8:8 + H], oh[0:1, so, 0, :], ex[0:1, 2, :], start=True, stop=True).then_inc(S("fac_ps"), 1)
                send(14, 16)
                pe.wait_ge(S("exp_ready"), n + 1)
                tr(pb[4][:, P:2 * P], wT[:, :], ident[:, :]).then_inc(S("w_ps"), 1)
            turn(-1, -1, 0, messages=False)
            with pe.Fori(0, NSG // 6) as i:
                for u in range(6):
                    turn(i * 6 + u, u, i * 2)
            for g_ in range(NSG // 6 * 6, NSG):
                turn(g_, g_ % 6, NSG // 6 * 2, scores=g_ + 1 < NSG)

            pe.wait_ge(S("ld_ffn"), 16 * FFN_LOADS)
            pe.wait_ge(S("acc_added"), STEPS + 2)
            for k in range(2):
                for q in range(2):
                    for c in range(FC):
                        ins = tr(pb[k][:, (q * FC + c) * P:(q * FC + c + 1) * P], wx_nat[:, c, (2 * k + q) * P:(2 * k + q + 1) * P], ident[:, :])
                ins.then_inc(S("wxT_ps"), 1)
            for q in range(PAIRS):
                mm(pb[4][0:1, q * P:(q + 1) * P], bx_col[:, q:q + 1], slice2, start=True, stop=True)
            pe.wait_ge(S("itemp_ready"), 1)
            mm(pb[5][:, :], ones[0:1, :], itemp_r, start=True, stop=True).then_inc(S("itemp_ps"), 1)
            pe.wait_ge(S("wxT_ready"), 2)
            for c in range(FC):
                for q in range(PAIRS):
                    ins = mm(pb[2 + c][:, q * P:(q + 1) * P], wxT[:, q, c * P:(c + 1) * P], slice2, start=True, stop=True)
                ins.then_inc(S("comb_ps"), 1)
            pe.wait_ge(S("comb_ready"), 1)
            for c in range(FC):
                mm(pb[4 + c][:, :], ctx_bd[:, 0, :], iota_row[:, :], start=True, stop=False, skip_group_check=True)

            def slice_block(b, s, last=False):
                k = TAIL if last else P
                pe.wait_ge(S("xn_ready"), NB + b + 1)
                for c in range(FC):
                    ins = tr(pb[s][:, c * P:(c + 1) * P], xn[:, s, c * P:(c + 1) * P], ident[:, :])
                ins.then_inc(S("xnT_ps"), 1)
                pe.wait_ge(S("xnT_ready"), NB + b + 1)
                mm(pb[2 + s][:, :], ones[0:1, :], bias_r, start=True, stop=False)
                for c in range(FC):
                    ins = mm(pb[2 + s][:, :], xnT[:, s, c, :], comb[:, c, :], start=False, stop=(c == FC - 1))
                ins.then_inc(S("logit_ps"), 1)
                pe.wait_ge(S("sw_ready"), b + 1)
                for c in range(FC):
                    ins = mm(pb[4 + c][:, :], xn[0:k, s, c * P:(c + 1) * P], sw[0:k, ds(b, 1), :].rearrange("p b k -> p (b k)"),
                             start=False, stop=last, skip_group_check=True)
                ins.then_inc(S("swx_ps"), 1)
            with pe.Fori(0, FULL // 2) as i:
                for s in range(2):
                    slice_block(i * 2 + s, s)
            slice_block(FULL, 0, last=True)

            heads = [slice(h * G, (h + 1) * G) for h in range(H)]
            pe.wait_ge(S("sw_summed"), NB)
            mm(pb[6][:, :], ones[:, :], swsum, start=True, stop=True).then_inc(S("norm_ps"), 1)
            pe.wait_ge(S("norm_ready"), 1)
            for h in heads:
                for c in range(FC):
                    mm(pb[7][0:DH, h], wfx[:, c, h], swxT[:, c, h], start=(c == 0), stop=False)
                ins = mm(pb[7][0:DH, h], bfx_r[0:1, h], norm_r[0:1, h], start=False, stop=True)
            ins.then_inc(S("tok_ps"), 1)
            pe.wait_ge(S("tok_ready"), 1)
            for k in range(2):
                mm(pb[k][0:DH, :], wqkv[:, k, :], tokT[:, :], start=True, stop=True).then_inc(S("qkv_ps"), 1)
            for h in heads:
                ins = mm(pb[2][0:G, h], tokT[:, h], wqkv[:, 2, :], start=True, stop=True)
            ins.then_inc(S("qkv_ps"), 1)
            pe.wait_ge(S("qkv_ready"), 2)
            for h in heads:
                ins = mm(pb[3][0:G, h], qs[0:DH, h], ks[0:DH, h], start=True, stop=True)
            ins.then_inc(S("attn_ps"), 1)
            pe.wait_ge(S("attn_ready"), 1)
            for h in heads:
                ins = tr(pb[4][0:G, h], att_g[0:G, h], ident[0:G, 0:G])
            ins.then_inc(S("attnT_ps"), 1)
            pe.wait_ge(S("attnT_ready"), 1)
            pe.wait_ge(S("qkv_ready"), 3)
            for n, h in enumerate(heads):
                ins = mm(pb[5][:, h], vs[0:G, n // 2 * P:n // 2 * P + P], attnT[0:G, h], start=True, stop=True)
            ins.then_inc(S("os_ps"), 1)
            pe.wait_ge(S("os_ready"), 1)
            for k in range(2):
                for q in range(2):
                    ins = mm(pb[6 + k][:, q * F:(q + 1) * F], osbd[:, 2 * k + q, :], wout[:, 2 * k + q, :], start=True, stop=True)
                ins.then_inc(S("v2_ps"), 1)

            pe.wait_ge(S("v2_ready"), 2)

            def out_block(b, s):
                pe.wait_ge(S("sws_ready"), b + 1)
                for q in range(PAIRS):
                    ins = tr(pb[s][:, q * P:(q + 1) * P], sws[:, s, q * P:(q + 1) * P], ident[:, :])
                ins.then_inc(S("swT_ps"), 1)
                pe.wait_ge(S("swT_ready"), b + 1)
                pe.wait_ge(S("y_ready"), b + 1)
                for q in range(PAIRS):
                    ins = mm(pb[2 + s][:, 0:F], swT[:, s, q * P:(q + 1) * P], v2[:, q, :], start=(q == 0), stop=(q == PAIRS - 1))
                ins.then_inc(S("y_ps"), 1)
            with pe.Fori(0, FULL // 2) as i:
                for s in range(2):
                    out_block(i * 2 + s, s)
            out_block(FULL, 0)

        @block.vector
        def _(dve):
            own = Chain(dve, dve_own)
            for name, free in (("xnT_kept", 1), ("ad_taken", 1), ("tab_taken1", 1), ("proj_taken", 1), ("acc_added", 2), ("y_ready", 2)):
                dve.sem_inc(S(name), free)
            v = nc.vector
            tt, ts, stt, cp = v.tensor_tensor, v.tensor_scalar, v.scalar_tensor_tensor, v.tensor_copy
            dve.wait_ge(S("ld_edges"), 16 * (6 + 2 + (TJ - 2) + 2))
            own.link(cp(dstw[:, :, :], dstw_i[:, :, :]))
            own.link(cp(tile_row[:, :, C_DST:C_DST + P], dstw_i[:, :, 1:P + 1]))
            own.link(stt(tile_row[:, :, C_IDX:C_IDX + P], src_i[:, :, :], float(R), typ_i[:, :, :], ALU.mult, ALU.add))
            own.link(cp(tile_row[:, :, C_TYP:C_TYP + P], typ_i[:, :, :]))
            own.link(tt(tile_row[:, :, C_BRK:C_BRK + P + 1], dstw[:, :, 1:P + 2], dstw[:, :, 0:P + 1], ALU.not_equal))
            own.link(ts(tile_row[:, :, C_BRK:C_BRK + P + 1], tile_row[:, :, C_BRK:C_BRK + P + 1], -BIG, None, ALU.mult))
            own.link(cp(tcol_i[:, 0, :], dstw_i[:, :, 1]))
            own.link(stt(real, dstw[:, :, 1:P + 1], float(PAD_DST), dstw[:, :, 1:P + 1], ALU.is_lt, ALU.mult))
            own.link(v.tensor_reduce(tcol[:, 2, :], real, AX, ALU.max))
            own.link(cp(tcol_i[:, 1, :], tcol[:, 2, :]))
            own.link(ts(tcol_i[:, 2:4, :], tcol_i[:, 0:2, :], 7, None, ALU.arith_shift_right))
            own.link(cp(tcol[:, 3:5, :], tcol_i[:, 2:4, :]))
            own.link(tt(tcol[:, 0, :], tcol[:, 4, :], tcol[:, 3, :], ALU.subtract))
            own.link(ts(tcol[:, 0, :], tcol[:, 0, :], 1.0, 0.0, ALU.add, ALU.max))
            own.link(v.memset(tcol[:, 1, 0:1], 0.0))
            for j in range(1, TJ):
                own.link(tt(tcol[:, 1, j:j + 1], tcol[:, 1, j - 1:j], tcol[:, 0, j - 1:j], ALU.add))
            cp(tile_row[:, :, C_BLK], tcol[:, 3, :]).then_inc(S("n_ready"), 1)
            dve.wait_ge(S("first_ps"), 1)
            cp(tile_row[:, :, C_FIRST], pb[5][:, 0:TJ]).then_inc(S("tiles_ready"), 1)
            dve.wait_ge(S("tiles_ready"), 1)
            dve.wait_ge(S("consts"), 1)
            tt(reached[:, :, :], iota_row[:, :].unsqueeze(1).to_broadcast([P, TJ, 512]),
               tile_row[:, :, C_FIRST:C_FIRST + 1].to_broadcast([P, TJ, 512]), ALU.is_ge).then_inc(S("cmp_ready"), 1)
            dve.wait_ge(S("ld_x"), 32)

            def node_stats(turn):
                with dve.Fori(0, NB) as i:
                    v.bn_stats(bn6[:, ds(i, 1), :].rearrange("p b k -> p (b k)"), x_sb[:, ds(i, 1), :].rearrange("p b f -> p (b f)")).then_inc(S("bn_done"), 1)
                dve.wait_ge(S("bn_done"), turn * NB)
                for b in range(NB):
                    ins = v.bn_aggr(mv[:, b, :], bn6[:, b, :])
                own.link(ins)

            def node_rstd(turn):
                ts(rstd[:, :], mv[:, :, 1], LN_EPS, None, ALU.add).then_inc(S("stats"), 1)
                dve.wait_ge(S("sqrt_done"), turn)
                own.link(v.reciprocal(rstd[:, :], rstd[:, :]))
                stt(nmr[:, :], mv[:, :, 0], -1.0, rstd[:, :], ALU.mult, ALU.mult).then_inc(S("rstd_ready"), 1)
            node_stats(1)
            dve.wait_ge(S("tk_ps"), 1)
            own.link(ts(tcol[:, 5, :], pb[6][:, 0:KC], -1.0, float(TILES - 1), ALU.add, ALU.min))
            cp(tcol_i[:, 3, :], tcol[:, 5, :]).then_inc(S("tk_ready"), 1)
            node_rstd(1)
            dve.wait_ge(S("bcast_ps"), 1)
            own.link(cp(bproj_b[:, :], pb[7][:, 0:F]))
            cp(bout_b[:, :], pb[7][:, F:2 * F]).then_inc(S("bcast_done"), 1)
            dve.wait_ge(S("steps_here"), 16 * KC)
            own.link(tt(tcol[:, 7, :], step_no[:, :], step_row[:, :, C_FIRST], ALU.subtract))
            own.link(tt(tcol[:, 7, :], tcol[:, 7, :], step_row[:, :, C_BLK], ALU.add))
            own.link(ts(tcol[:, 5, :], tcol[:, 7, :], -float(P), None, ALU.mult))
            for c in range(KC):
                own.link(ts(step_row[:, c, C_DST:C_DST + P], step_row[:, c, C_DST:C_DST + P], tcol[:, 5, c:c + 1], None, ALU.add))
            ts(tcol[:, 6, :], tcol[:, 7, :], float(NB - 1), None, ALU.min).then_inc(S("steprow_ready"), 1)
            for k, dst in enumerate((dstlT, idxT, typT)):
                dve.wait_ge(S("cols_ps"), k + 1)
                cp(dst[:, :], pb[k][:, :]).then_inc(S("cols_taken"), 1)
            dve.wait_ge(S("b_ps"), 1)
            cp(brow[0:1, :], pb[3][0:1, :]).then_inc(S("cols_taken"), 1)
            dve.wait_ge(S("cols_taken"), 4)
            own.link(tt(tyoh[:, :, :], typT[:, 0:STEPS].unsqueeze(2).to_broadcast([P, STEPS, R]),
                        iota_row[:, 0:R].unsqueeze(1).to_broadcast([P, STEPS, R]), ALU.is_equal))
            for q, gq in enumerate(range(0, NSG, 3)):
                m = min(3, NSG - gq)
                dve.wait_ge(S("brk_ps"), q + 1)
                cp(brk[:, gq:gq + m, :], pb[5 + q % 2][:, 0:m * (P + 1)].rearrange("p (g e) -> p g e", g=m)).then_inc(S("brk_taken"), 1)
            dve.wait_ge(S("brk_taken"), -(-NSG // 3))
            for k in range(2):
                own.link(v.tensor_reduce(brk_sum[:, :, k], brk[:, :, k:k + P], AX, ALU.add))

            def block_work(b, s):
                dve.wait_ge(S("xnT_ready"), b + 1)
                cp(xnT_all[:, :, ds(b * P, P)], xnT[:, s, :, :]).then_inc(S("xnT_kept"), 1)
                dve.wait_ge(S("ad_ps"), b + 1)
                cp(adst[:, ds(b, 1), :].rearrange("p b k -> p (b k)"), pb[4][:, 0:H * R]).then_inc(S("ad_taken"), 1)
                dve.wait_ge(S("v_ready"), b + 1)
                ts(kmin[:, s, :], pb[5 + s][:, 0:F], 0.0, None, ALU.min).then_inc(S("kmin_ready"), 1)
                for r in range(1, R, 2):
                    dve.wait_ge(S("tab_ps1"), b * (R // 2) + r // 2 + 1)
                    if r == 1:
                        dve.wait_ge(S("row_free"), b + 1)
                    cp(tab_row[:, s, r * ROW:(r + 1) * ROW], pb[3][:, 0:ROW]).then_inc(S("tab_taken1"), 1)
                    if r == 1:
                        dve.wait_ge(S("kexp_ready"), b + 1)
                        stt(kphi[:, s, :], pb[5 + s][:, 0:F], 0.0, kexp[:, s, :], ALU.max, ALU.add).then_inc(S("k_ready"), 1)
            with dve.Fori(0, FULL // 2) as i:
                for s in range(2):
                    block_work(i * 2 + s, s)
            block_work(FULL, 0)

            dve.wait_ge(S("x_biased"), 1)

            def chunk(qn, n):
                for c in range(FC):
                    dve.wait_ge(S("q_ps"), qn * FC + c + 1)
                    ts(qbuf[:, c, 0:n], pb[c][:, 0:n], 0.0, None, ALU.min).then_inc(S("qmin_ready"), 1)
                for c in range(FC):
                    dve.wait_ge(S("qexp_ready"), qn * FC + c + 1)
                    stt(qT[:, c, 0:n], pb[c][:, 0:n], 0.0, qbuf[:, c, 0:n], ALU.max, ALU.add).then_inc(S("q_ready"), 1)
                for c in range(FC):
                    dve.wait_ge(S("lin_ps"), qn * FC + c + 1)
                    own.link(ts(qbuf[:, c, 0:n], pb[4 + c][:, 0:n], 1e-6, None, ALU.max))
                    own.link(v.reciprocal(qbuf[:, c, 0:n], qbuf[:, c, 0:n]))
                    tt(attT[:, c, 0:n], pb[2 + c][:, 0:n], qbuf[:, c, 0:n], ALU.mult).then_inc(S("lin_ready"), 1)
                for j in range(-(-n // P)):
                    m = min(P, n - j * P)
                    dve.wait_ge(S("proj_ps"), qn * 4 + j + 1)
                    xb = x_sb[0:m, ds(qn * 4 + j, 1), :].rearrange("p b f -> p (b f)")
                    tt(xb, xb, pb[6 + j % 2][0:m, 0:F], ALU.add).then_inc(S("proj_taken"), 1)
            with dve.Fori(0, NCH) as i:
                own.enter(i, 4)
                chunk(i, 512)
                own.leave(NCH)
            chunk(NCH, TAIL)

            own.link(v.memset(arena2[:, :], 0.0))
            dve.wait_ge(S("tab_stored"), 16 * NB)
            flatrow = lambda t: t.rearrange("p h c -> p (h c)")
            scan = lambda o, brk_, data, first: v.tensor_tensor_scan(o, brk_, data, first, ALU.add, ALU.max)

            regs = [dve.alloc_register(f"dve_block{k}") for k in range(SG)]

            def turn(g_, u, third, scores=True, messages=True):
                n, slot, so, mslot = g_ + 1, (u + 1) % 3, (u + 1) % 2, u % 3

                if messages:
                    bs = load_blocks(dve, brow[0:1, ds(g_ * SG, SG)], NB - 1, regs)

                def rescale():
                    dve.wait_ge(S("fac_ready"), g_ + 1)
                    dve.wait_ge(S("acc_added"), g_ * SG + 2)
                    at = acc[:, ds(bs[0], 1), 0:F].rearrange("p b (h d) -> p (b h) d", h=H)
                    own.link(tt(at, at, fac[:, :].unsqueeze(2).to_broadcast([P, H, D]), ALU.mult))
                    at = acc[:, ds(bs[0], 1), F:ROW].rearrange("p b h -> p (b h)")
                    own.link(tt(at, at, fac[:, :], ALU.mult))

                def weigh(half):
                    dve.wait_ge(S("w_ready"), g_ * 2 + 2)
                    t8 = slice(half * 8, half * 8 + 8)
                    m = rows[:, mslot, t8, 0:F].rearrange("p t (h d) -> p t h d", h=H)
                    tt(m, m, w_sb[:, t8, :].unsqueeze(3).to_broadcast([P, SG // 2, H, D]), ALU.mult).then_inc(S("msg_ready"), 1)

                def add(t0, t1):
                    for t in range(t0, t1) if messages else ():
                        if t == t0:
                            own.settle()
                        dve.wait_ge(S("msg_ps"), g_ * SG + 3 * SG + t + 1)
                        dve.wait_ge(S("acc_added"), g_ * SG + t + 2)
                        at = acc[:, ds(bs[t], 1), :].rearrange("p b k -> p (b k)")
                        tt(at, at, pb[6 + t % 2][:, 0:ROW], ALU.add).then_inc(S("acc_added"), 1)

                def dst_scores(half):
                    own.settle()
                    dve.wait_ge(S("dsc_ps"), n * 2 + half + 1)
                    own.link(tt(sel[:, :, :, :], pb[2 + half][:, :].rearrange("p (t h r) -> p t h r", h=H, r=R),
                                tyoh[:, ds(n * SG + half * 8, 8), :].unsqueeze(2).to_broadcast([P, SG // 2, H, R]), ALU.mult))
                    own.count(v.tensor_reduce(score[:, half * 8:half * 8 + 8, :], sel[:, :, :, :], AX, ALU.add))

                if scores:
                    tt(oh[:, so, :, :], iota_row[:, 0:P].unsqueeze(1).to_broadcast([P, SG, P]),
                       dstlT[:, ds(n * SG, SG)].unsqueeze(2).to_broadcast([P, SG, P]), ALU.is_equal).then_inc(S("oh_ready"), 1)
                if messages:
                    weigh(0)
                    weigh(1)
                    rescale()
                if not scores:
                    add(0, SG)
                    return
                own.link(cp(brk_g[:, :], brk[:, ds(n, 1), :].rearrange("p g e -> p (g e)")))
                own.count(cp(brk2[:, :], brk_sum[:, ds(n, 1), :].rearrange("p g k -> p (g k)")))
                add(0, 2)
                dst_scores(0)
                add(2, 4)
                dst_scores(1)
                own.settle()
                dve.wait_ge(S(f"rows_here{slot}"), (third + (u + 1) // 3 + 1) * SG * 16)
                own.link(tt(score[:, :, :], score[:, :, :], rows[:, slot, :, F:ROW], ALU.add))
                stt(score[:, :, :], score[:, :, :], 0.2, score[:, :, :], ALU.mult, ALU.max).then_inc(S("score_ready"), 1)
                add(4, 8)
                dve.wait_ge(S("scoreT_ps"), n + 1)
                sT = pb[4][:, 0:P]
                own.link(scan(run[:, 0, :], brk_g[:, 0:P], sT, -BIG))
                scan(run[:, 1, ::-1], brk_g[:, P:0:-1], sT[:, ::-1], -BIG).then_inc(S("ends_ready"), 1)
                add(8, 10)
                dve.wait_ge(S("ends_ps"), n + 1)
                own.link(cp(chunk_row[0:1, :, :, 1:SG + 1], pb[5][0:1, :].rearrange("p (k t h) -> p k h t", k=4, h=H)))
                own.link(scan(flatrow(carry[0:1, 0]), flatrow(chunk_row[0:1, 2]), flatrow(chunk_row[0:1, 0]), -BIG))
                own.link(scan(flatrow(carry[0:1, 1])[:, ::-1], flatrow(chunk_row[0:1, 3])[:, ::-1], flatrow(chunk_row[0:1, 1])[:, ::-1], -BIG))
                own.link(cp(carry_flat[0:1, 0, :].rearrange("p (t h) -> p h t", h=H), carry[0:1, 0, :, 0:SG]))
                cp(carry_flat[0:1, 1, :].rearrange("p (t h) -> p h t", h=H), carry[0:1, 1, :, 2:SG + 2]).then_inc(S("carry_ready"), 1)
                add(10, 12)
                own.link(tt(ex[0:1, 0, :], carry[0:1, 1, :, 1], carry[0:1, 0, :, 0], ALU.max))
                own.link(ts(ex[0:1, 0, :], ex[0:1, 0, :], 0.0, None, ALU.max))
                own.link(stt(ex[0:1, 1, :], carry[0:1, 0, :, 0], 0.0, ex[0:1, 0, :], ALU.max, ALU.subtract))
                own.link(ts(ex[0:1, 3, 0:1], brk_g[0:1, 0:1], 0.0, None, ALU.is_equal))
                own.link(ts(ex[0:1, 2, :], ex[0:1, 1, :], ex[0:1, 3, 0:1], None, ALU.mult))
                own.link(cp(chunk_row[0:1, 0, :, 0], carry[0:1, 0, :, SG]))
                dve.wait_ge(S("seg0_ps"), n + 1)
                cp(seg0[:, :], pb[5][:, 0:2]).then_inc(S("seg0_taken"), 1)
                add(12, 14)
                dve.wait_ge(S("seg0_taken"), n + 1)
                own.link(scan(run[:, 0, :], brk_g[:, 0:P], sT, seg0[:, 0:1]))
                own.link(scan(run[:, 1, ::-1], brk_g[:, P:0:-1], sT[:, ::-1], seg0[:, 1:2]))
                own.link(stt(run[:, 0, :], run[:, 0, :], 0.0, run[:, 1, :], ALU.max, ALU.max))
                tt(below[:, :], sT, run[:, 0, :], ALU.subtract).then_inc(S("below_ready"), 1)
                add(14, 16)
            turn(-1, -1, 0, messages=False)
            with dve.Fori(0, NSG // 6) as i:
                own.enter(i, 6 * 23)
                for u in range(6):
                    turn(i * 6 + u, u, i * 2)
                own.leave(NSG // 6)
            for g_ in range(NSG // 6 * 6, NSG):
                turn(g_, g_ % 6, NSG // 6 * 2, scores=g_ + 1 < NSG)
            dve.wait_ge(S("acc_added"), STEPS + 2)
            v.memset(slice2, 0.0).then_inc(S("slice2_zeroed"), 1)
            own.link(ts(rden[:, :, :], acc[:, :, F:ROW], 1e-12, None, ALU.add))
            own.link(v.reciprocal(rden[:, :, :], rden[:, :, :]))
            at = acc[:, :, 0:F].rearrange("p b (h d) -> p b h d", h=H)
            own.link(tt(at, at, rden[:, :, :].unsqueeze(3).to_broadcast([P, NB, H, D]), ALU.mult))
            tt(x_sb[:, :, :], x_sb[:, :, :], acc[:, :, 0:F], ALU.add).then_inc(S("x2_ready"), 1)
            dve.wait_ge(S("x2_ready"), 1)
            node_stats(2)
            node_rstd(2)

            own.link(v.memset(ctx_bd[:, 0, :], 0.0))
            own.link(v.memset(swsum, 0.0))
            dve.wait_ge(S("ld_ffn"), 16 * FFN_LOADS)
            own.link(ts(temp_r, temp_r, 0.1, 5.0, ALU.max, ALU.min))
            own.link(v.reciprocal(temp_r, temp_r))
            by_head = lambda t: t.rearrange("p (h g) -> p h g", h=H)
            cp(by_head(itemp_r), temp_r.unsqueeze(2).to_broadcast([1, H, G])).then_inc(S("itemp_ready"), 1)
            dve.wait_ge(S("itemp_ps"), 1)
            own.link(cp(itemp_b[:, :], pb[5][:, :]))
            own.link(tt(by_head(bias_r), by_head(pb[4][0:1, :]), bslice_r.unsqueeze(1).to_broadcast([1, H, G]), ALU.add))
            own.link(tt(bias_r, bias_r, itemp_r, ALU.mult))
            for c in range(FC):
                dve.wait_ge(S("comb_ps"), c + 1)
                ins = tt(comb[:, c, :], pb[2 + c][:, :], itemp_b[:, :], ALU.mult)
            ins.then_inc(S("comb_ready"), 1)

            def slice_block(b, s, last=False):
                k = TAIL if last else P
                dve.wait_ge(S("logit_ps"), b + 1)
                lg = by_head(logit[:, s, :])
                own.link(v.tensor_reduce(top[:, s, :], by_head(pb[2 + s][:, :]), AX, ALU.max))
                tt(lg, by_head(pb[2 + s][:, :]), top[:, s, :].unsqueeze(2).to_broadcast([P, H, G]), ALU.subtract).then_inc(S("logit_ready"), 1)
                dve.wait_ge(S("lexp_ready"), b + 1)
                own.link(v.tensor_reduce(tot[:, s, :], lg, AX, ALU.add))
                own.link(v.reciprocal(tot[:, s, :], tot[:, s, :]))
                sw_b = sw[:, ds(b, 1), :].rearrange("p b k -> p (b k)")
                tt(by_head(sw_b), lg, tot[:, s, :].unsqueeze(2).to_broadcast([P, H, G]), ALU.mult).then_inc(S("sw_ready"), 1)
                dve.wait_ge(S("sw_ready"), b + 1)
                tt(swsum[0:k, :], swsum[0:k, :], sw_b[0:k, :], ALU.add).then_inc(S("sw_summed"), 1)
            with dve.Fori(0, FULL // 2) as i:
                own.enter(i, 6)
                for s in range(2):
                    slice_block(i * 2 + s, s)
                own.leave(FULL // 2)
            slice_block(FULL, 0, last=True)

            dve.wait_ge(S("norm_ps"), 1)
            own.link(cp(norm_r, pb[6][0:1, :]))
            own.link(ts(rnorm, pb[6][:, :], 1e-5, None, ALU.add))
            own.link(v.reciprocal(rnorm, rnorm))
            dve.wait_ge(S("swx_ps"), NB)
            for c in range(FC):
                ins = cp(swxT[:, c, :], pb[4 + c][:, :])
            ins.then_inc(S("norm_ready"), 1)
            dve.wait_ge(S("tok_ps"), 1)
            tt(tokT[:, :], pb[7][0:DH, :], rnorm[0:DH, :], ALU.mult).then_inc(S("tok_ready"), 1)
            dve.wait_ge(S("attn_ps"), 1)
            scores, ag = by_head(pb[3][0:G, :]), by_head(att_g[0:G, :])
            own.link(v.tensor_reduce(top[0:G, 0, :], scores, AX, ALU.max))
            tt(ag, scores, top[0:G, 0, :].unsqueeze(2).to_broadcast([G, H, G]), ALU.subtract).then_inc(S("attn_below"), 1)
            dve.wait_ge(S("attn_exp"), 1)
            own.link(v.tensor_reduce(tot[0:G, 0, :], ag, AX, ALU.add))
            own.link(v.reciprocal(tot[0:G, 0, :], tot[0:G, 0, :]))
            tt(ag, ag, tot[0:G, 0, :].unsqueeze(2).to_broadcast([G, H, G]), ALU.mult).then_inc(S("attn_ready"), 1)
            dve.wait_ge(S("attnT_ps"), 1)
            cp(attnT[0:G, :], pb[4][0:G, :]).then_inc(S("attnT_ready"), 1)
            own.link(v.memset(osbd, 0.0))
            dve.wait_ge(S("os_ps"), 1)
            own.link(cp(osbd[0:G, :, 0:G], pb[5][0:G, :].rearrange("p (q e g) -> p q e g", e=2, g=G)[:, :, 0, :]))
            cp(osbd[G:P, :, G:P], pb[5][G:P, :].rearrange("p (q e g) -> p q e g", e=2, g=G)[:, :, 1, :]).then_inc(S("os_ready"), 1)

            def out_block(b, s):
                dve.wait_ge(S("y_ps"), b + 1)
                dve.wait_ge(S("y_free"), b + 1)
                own.link(tt(y[:, s, :], pb[2 + s][:, 0:F], x_sb[:, ds(b, 1), :].rearrange("p b f -> p (b f)"), ALU.add))
                tt(y[:, s, :], y[:, s, :], bout_b[:, :], ALU.add).then_inc(S("y_ready"), 1)
            with dve.Fori(0, FULL // 2) as i:
                own.enter(i, 2)
                for s in range(2):
                    out_block(i * 2 + s, s)
                own.leave(FULL // 2)
            out_block(FULL, 0)


def kernel(**inputs):
    import numpy as np
    import concourse.bacc as bacc
    from concourse.bass_utils import run_bass_kernel_spmd

    nc = bacc.Bacc("TRN2", target_bir_lowering=False, num_devices=1)
    arrays, aps = {}, {}
    for name, value in inputs.items():
        value = np.ascontiguousarray(value)
        arrays[f"in_{name}"] = value
        aps[name] = nc.dram_tensor(f"in_{name}", value.shape, mybir.dt.from_np(value.dtype), kind="ExternalInput").ap()
    out = nc.dram_tensor("out_0", inputs["x"].shape, F32, kind="ExternalOutput").ap()
    build(nc, aps, out)
    result = run_bass_kernel_spmd(nc, [arrays], core_ids=[0])
    return result.results[0]["out_0"]
```

```python
from contextlib import ExitStack

import concourse.bass as bass
from concourse import mybir

ds = bass.ds
ALU = mybir.AluOpType
ACT = mybir.ActivationFunctionType
F32 = mybir.dt.float32
BF16 = mybir.dt.bfloat16
I32 = mybir.dt.int32
U32 = mybir.dt.uint32
AX = mybir.AxisListType.X

P = 128
BIG = 1.0e30
LN_EPS = 1e-5


class Chain:

    def __init__(self, eng, sem):
        self.eng, self.sem, self.base, self.n, self.done = eng, sem, 0, 0, 0

    def link(self, ins):
        self.count(ins)
        self.settle()

    def count(self, ins):
        self.n += 1
        ins.then_inc(self.sem, 1)

    def settle(self):
        self.eng.wait_ge(self.sem, self.base + self.n)

    def enter(self, i, per):
        self.done += self.n
        self.base, self.n, self.per = i * per + self.done, 0, per

    def leave(self, turns):
        assert self.n == self.per, (self.n, self.per)
        self.done += self.per * turns
        self.base, self.n = self.done, 0


def load_blocks(eng, row, most, regs):
    eng.load(regs, row)
    return [eng.snap(r, min_val=0, max_val=most) for r in regs]


def build(nc, a, out):
    x_d, src_d, dst_d, typ_d = a["x"], a["src"], a["dst"], a["edge_type_8"]
    N, F = x_d.shape
    E = src_d.shape[0]
    R = a["L0_gnn_W"].shape[0]
    H, D = a["L0_gnn_attn_src"].shape
    G, DH = a["L0_ffn_W_slice"].shape
    INNER = a["L0_ffn_W_fx"].shape[1]
    FULL, TAIL = N // P, N % P
    NB = FULL + 1
    FC = F // P
    ROW = F + H
    TILES = -(-E // P)
    TJ = -(-TILES // P)
    SG = 16
    NSG = -(-(TILES + NB - 1) // SG)
    STEPS = NSG * SG
    KC = -(-STEPS // P)
    PAD_DST = 8191
    assert H * D == F and SG * H == P and FULL % 2 == 0 and G == DH == 64
    C_DST, C_IDX, C_TYP, C_BRK, C_FIRST, C_BLK, TROW = 0, P, 2 * P, 3 * P, 4 * P + 1, 4 * P + 2, 4 * P + 4

    table_d = nc.dram_tensor("table", (NB * P * R, ROW), F32)
    tiles_d = nc.dram_tensor("tiles", (TJ * P, TROW), F32)
    table_rows = table_d.ap()
    table_blocks = table_d.ap().rearrange("(n r) c -> n (r c)", r=R)

    with ExitStack() as ctx:
        def sb(name, shape, dt=F32):
            return ctx.enter_context(nc.sbuf_tensor(name, shape, dt))

        def sem(name):
            return ctx.enter_context(nc.semaphore(name))

        pb = [ctx.enter_context(nc.psum_tensor(f"bank{i}", [P, 512], F32)) for i in range(8)]

        x_sb = sb("x_sb", [P, NB, F])
        ident = sb("ident", [P, P])
        upper = sb("upper", [P, P])
        ones = sb("ones", [P, P])
        iota_row = sb("iota_row", [P, 512])
        step_no = sb("step_no", [P, KC])
        step_i = sb("step_i", [P, KC], I32)
        mv = sb("mv", [P, NB, 2])
        bn6 = sb("bn6", [P, NB, 6])
        rstd = sb("rstd", [P, NB])
        nmr = sb("nmr", [P, NB])

        work = sb("work", [P, 5690])

        class Phase:
            def __init__(self):
                self.at = 0

            def __call__(self, shape, dt=F32, parts=P):
                n = 1
                for k in shape[1:]:
                    n *= k
                words = n if dt is not BF16 else n // 2
                t = work[0:shape[0], self.at:self.at + words]
                self.at += words
                assert self.at <= 5690, self.at
                t = t if dt is F32 else t.bitcast(dt)
                self.last = t
                names = "abcd"[:len(shape) - 1]
                sizes = {k: v for k, v in zip(names, shape[1:])}
                return t.rearrange(f"p ({' '.join(names)}) -> p {' '.join(names)}", **sizes) if len(names) > 1 else t
        mixing, edging, slicing = Phase(), Phase(), Phase()

        arena = sb("arena", [P, NB * INNER])
        w_nat = arena[:, 0:R * FC * F].rearrange("p (r c f) -> p r c f", r=R, c=FC)
        w_t = arena[:, R * FC * F:R * FC * F + FC * R * ROW].rearrange("p (c r k) -> p c r k", c=FC, r=R)
        a1 = R * FC * F + FC * R * ROW
        tab_row = arena[:, a1:a1 + 2 * R * ROW].rearrange("p (s k) -> p s k", s=2)
        rows = arena[:, 0:3 * SG * ROW].rearrange("p (s t k) -> p s t k", s=3, t=SG)
        sw = arena[:, :].rearrange("p (b k) -> p b k", b=NB)
        arena2 = sb("arena2", [P, NB * ROW])
        xnT_all = arena2[:, 0:FC * NB * P].rearrange("p (c n) -> p c n", c=FC)
        acc = arena2[:, :].rearrange("p (b k) -> p b k", b=NB)
        tile_row = arena2[:, 0:TJ * TROW].rearrange("p (j c) -> p j c", j=TJ)
        a2 = [TJ * TROW]

        def place(width, dt=F32):
            a2[0] += TJ * width
            t = arena2[:, a2[0] - TJ * width:a2[0]]
            return (t if dt is F32 else t.bitcast(dt)).rearrange("p (j e) -> p j e", j=TJ)
        dstw_i, dstw = place(P + 2, I32), place(P + 2)
        src_i, typ_i, real = place(P, I32), place(P, I32), place(P)
        step_row = arena2[:, TJ * TROW:(TJ + KC) * TROW].rearrange("p (c k) -> p c k", c=KC)
        tcol = sb("tcol", [P, 8, TJ])
        tcol_i = sb("tcol_i", [P, 4, TJ], I32)
        ones_bf = sb("ones_bf", [P, 1], BF16)

        dstlT = sb("dstlT", [P, 512])
        idxT = sb("idxT", [P, 512], I32)
        typT = sb("typT", [P, 512])
        tyoh = sb("tyoh", [P, STEPS, R], BF16)
        brow = sb("brow", [P, 512], I32)
        brk = sb("brk", [P, NSG, P + 1])
        brk_sum = sb("brk_sum", [P, NSG, 2])
        adst = sb("adst", [P, NB, H * R])

        weights = sb("weights", [P, 4096])
        spare = sb("spare", [P, 2048])
        oh = [t.rearrange("p (t d) -> p t d", t=SG) for t in (weights[:, 0:2048], weights[:, 2048:4096], spare[:, :])]
        nat = weights[:, 0:2048]
        wq_nat, wkv_nat = nat[:, 0:512], nat[:, 512:1536]
        wproj_nat = nat[:, 1536:2048]
        wqT = weights[:, 2048:2560].rearrange("p (c k) -> p c k", c=FC)
        wkvT = weights[:, 2560:3584].rearrange("p (c k) -> p c k", c=FC)
        wprojT = weights[:, 3584:4096].rearrange("p (c k) -> p c k", c=FC)
        wx_nat, wfx = nat[:, 0:1024].rearrange("p (c k) -> p c k", c=FC), nat[:, 1024:2048].rearrange("p (c k) -> p c k", c=FC)
        wout = weights[:, 2560:3584].rearrange("p (c k) -> p c k", k=F)
        slice2 = arena[:, NB * INNER - P:NB * INNER]
        assert 3 * SG * ROW <= NB * INNER - P
        att = sb("att", [P, 2, FC])
        attbd = sb("attbd", [P, FC, 2 * H])
        w_adst = sb("w_adst", [P, FC, H, R])
        bproj_b = sb("bproj_b", [P, F])
        bout_b = sb("bout_b", [P, F])

        xn = spare[:, 0:2 * F].rearrange("p (s f) -> p s f", s=2)
        xnT = spare[:, 2 * F:4 * F].rearrange("p (s c n) -> p s c n", s=2, c=FC)
        reached = spare[:, 4 * F:8 * F].bitcast(BF16).rearrange("p (j k) -> p j k", j=TJ)
        kphi = mixing([P, 2, F])
        kmin = mixing([P, 2, F])
        kexp = mixing([P, 2, F])
        vones = mixing([P, 2, FC, P + 1])
        ctx_bd = sb("ctx_bd", [P, FC, P])
        ks_bd = sb("ks_bd", [P, FC, P])
        ctx_sb = sb("ctx_sb", [P, FC, P + 1])
        qexp = work[:, 0:FC * 512].rearrange("p (c n) -> p c n", c=FC)
        qden = mixing([P, 512])
        q1a = mixing([P, 512])
        qT0 = mixing([P, FC, 512])
        attT = mixing([P, FC, 512])
        q1b = mixing([P, 512])
        qT = [[qT0[:, c, :] for c in range(FC)], [q1a, q1b]]
        attT2 = [attT, work[:, 2 * FC * 512 // 2:2 * FC * 512].rearrange("p (c n) -> p c n", c=FC)]
        bproj_r, bout_r = kphi[0:1, 0, :], kphi[0:1, 1, :]
        iota_i = qT0[:, 0, :].bitcast(I32)
        spread = attT[:, :, :].rearrange("p c n -> p (c n)")

        SLOTS = 18
        idx_stage = sb("idx_stage", [P, 3, SG], I32)
        idle = sb("idle", [P, 2])
        ohT = edging([P, SG, P])
        sel = edging([P, SG // 2, H, R])
        score = edging([P, SG, H])
        brk2 = edging([P, 2])
        brk_g = edging([P, P + 1])
        run = edging([P, 2, P])
        chunk_row = sb("chunk_row", [1, 4, H, SLOTS])
        CW = H * SLOTS + 2
        carry2 = edging([1, 2, CW])
        carry_both = edging.last.rearrange("p (a b) -> p a b", a=2)[:, :, 0:H * SLOTS].rearrange("p a (h t) -> p a t h", h=H)[:, :, 0:SG, :]
        carry = [edging.last[:, k:k + H * SLOTS].rearrange("p (h t) -> p h t", h=H) for k in (0, CW - 2)]
        carry_flat = edging([1, 2, P])
        ex = sb("ex", [1, 4, H])
        seg0 = edging([P, 2])
        below = edging([P, P])
        wT = edging([P, P])
        w_sb = edging([P, SG, H])
        fac = edging([P, H])
        rden = edging([P, NB, H])

        PAIRS = INNER // P
        late = Phase()
        late.at = 4900
        wqkv = late([DH, 3, DH])
        bx_col = late([P, PAIRS])
        temp_r, bslice_r, bfx_r = late([1, H]), late([1, G]), late([1, INNER])
        slice2t = slicing([P, INNER])
        itemp_r, bias_r = slicing([1, INNER]), slicing([1, INNER])
        logit = slicing([P, 2, INNER])
        top, tot = slicing([P, 2, H]), slicing([P, 2, H])
        a3 = [0]

        def place3(n):
            a3[0] += n
            return arena2[:, a3[0] - n:a3[0]]
        wxT = arena[:, 0:PAIRS * F].rearrange("p (q f) -> p q f", q=PAIRS)
        comb = weights[:, 0:FC * INNER].rearrange("p (c k) -> p c k", c=FC)
        swsum = place3(INNER)
        swxT = place3(FC * INNER).rearrange("p (c k) -> p c k", c=FC)
        v2 = place3(PAIRS * F).rearrange("p (q f) -> p q f", q=PAIRS)
        norm_r = slicing([1, INNER])
        xn4 = spare[:, 4 * F:8 * F].rearrange("p (s f) -> p s f", s=4)
        bias_b = slicing([P, INNER])
        rnorm = place3(INNER)
        tokT = slicing([DH, INNER])
        assert max(slicing.at, edging.at) <= 4900, (slicing.at, edging.at)
        qs, ks, vs = place3(INNER), place3(INNER), tokT
        att_g = slice2t
        attnT = logit[:, 0, :]
        osbd = logit[:, 1, :].rearrange("p (q k) -> p q k", q=PAIRS)
        sws = arena2[:, a3[0] - 2 * INNER:a3[0]].rearrange("p (s k) -> p s k", s=2)
        swT = logit
        y = xn

        sums = (pb[1], pb[6], pb[7])

        sems = {}

        def S(name):
            if name not in sems:
                sems[name] = sem(name)
            return sems[name]

        dve_own, act_own, pool_own, pe_own = S("dve_own"), S("act_own"), S("pool_own"), S("pe_own")
        square = lambda t, o, f: t[:, o * F + f * P:o * F + (f + 1) * P]
        set_jobs = [(w_t[:, :, r, 0:F], [w_nat[:, r, o, f * P:(f + 1) * P] for f in range(FC) for o in range(FC)]) for r in range(R)]
        set_jobs += [(wqT[:, :, :], [square(wq_nat, o, f) for f in range(FC) for o in range(FC)])]
        set_jobs += [(wkvT[:, f, :], [square(wkv_nat, o, f) for o in range(2 * FC)]) for f in range(FC)]
        set_jobs += [(wprojT[:, :, :], [square(wproj_nat, o, f) for f in range(FC) for o in range(FC)])]
        FFN_SMALL = 8 + INNER // P
        DVE_STEPS = 10
        DVE_BLOCKS = 16
        NCH = FULL * P // 512

        block = ctx.enter_context(nc.Block())

        @block.sync
        def _(sp):
            sp.sem_inc(S("row_free"), 2)
            sp.sem_inc(S("y_free"), 2)
            sp.wait_ge(S("pads_set"), 1)
            per = P * P
            flat = [(src_i, src_d), (typ_i, typ_d)]
            whole, rest = TJ - 1, E - (TJ - 1) * per
            for t, d in flat:
                sp.dma_start(t[:, 0:whole, :], d[0:whole * per].rearrange("(j p e) -> p j e", p=P, e=P)).then_inc(S("ld_edges"), 16)
                sp.dma_start(t[0:rest // P, whole, :], d[whole * per:whole * per + rest // P * P].rearrange("(p e) -> p e", e=P)).then_inc(S("ld_edges"), 16)
                sp.dma_start(t[rest // P:rest // P + 1, whole, 0:rest % P], d[E - rest % P:E].rearrange("(p e) -> p e", p=1)).then_inc(S("ld_edges"), 16)
            dt_ = dst_d.tensor
            sp.dma_start(dstw_i[0:1, 0, 1:P + 2], dst_d[0:P + 1].rearrange("(p e) -> p e", p=1)).then_inc(S("ld_edges"), 16)
            sp.dma_start(dstw_i[1:P, 0, :], bass.AP(dt_, P - 1, [[P, P - 1], [1, P + 2]])).then_inc(S("ld_edges"), 16)
            for j in range(1, whole):
                sp.dma_start(dstw_i[:, j, :], bass.AP(dt_, j * per - 1, [[P, P], [1, P + 2]])).then_inc(S("ld_edges"), 16)
            sp.dma_start(dstw_i[0:rest // P, whole, :], bass.AP(dt_, whole * per - 1, [[P, rest // P], [1, P + 2]])).then_inc(S("ld_edges"), 16)
            sp.dma_start(dstw_i[rest // P:rest // P + 1, whole, 0:rest % P + 1],
                         dst_d[E - rest % P - 1:E].rearrange("(p e) -> p e", p=1)).then_inc(S("ld_edges"), 16)
            sp.wait_ge(S("x_zeroed"), 1)
            sp.dma_start(x_sb[:, 0:FULL, :], x_d[0:FULL * P, :].rearrange("(b p) f -> p b f", p=P)).then_inc(S("ld_x"), 16)
            sp.dma_start(x_sb[0:TAIL, FULL, :], x_d[FULL * P:N, :]).then_inc(S("ld_x"), 16)
            sp.wait_ge(S("tiles_ready"), 1)
            sp.wait_ge(S("consts"), 1)
            sp.dma_start(tiles_d.ap().rearrange("(j p) c -> p j c", p=P), tile_row[:, :, :]).then_inc(S("tiles_stored"), 16)

            def store_rows(b, s):
                for k in range(2):
                    sp.wait_ge(S(f"tab_taken{k}"), (b + 1) * (R // 2) + 1)
                sp.dma_start(table_blocks[ds(b * P, P), :], tab_row[:, s, :]).then_inc(S("tab_stored"), 16)
                sp.wait_ge(S("tab_stored"), (b + 1) * 16)
                sp.sem_inc(S("row_free"), 1)
            with sp.Fori(0, FULL // 2) as i:
                for s in range(2):
                    store_rows(i * 2 + s, s)
            store_rows(FULL, 0)

            def load_ffn(sem_, jobs):
                for to, frm in jobs:
                    sp.dma_start(to, frm).then_inc(S(sem_), 16)
            row = lambda name: a[name].rearrange("(p f) -> p f", p=1)
            tiled = lambda name: a[name].rearrange("(c p) k -> p c k", p=P)
            sp.wait_ge(S("proj_taken"), NB + 1)
            sp.wait_ge(S("slice2_zeroed"), 1)
            small = [(slice2[0:DH, 0:G], a["L0_ffn_W_slice"]), (slice2[DH:P, G:2 * G], a["L0_ffn_W_slice"]),
                     (wqkv[:, 0, :], a["L0_ffn_W_q"]), (wqkv[:, 1, :], a["L0_ffn_W_k"]), (wqkv[:, 2, :], a["L0_ffn_W_v"]),
                     (temp_r, a["L0_ffn_temperature"].rearrange("a h b c -> (a b) (h c)")), (bslice_r, row("L0_ffn_b_slice")), (bfx_r, row("L0_ffn_b_fx"))]
            small += [(bx_col[:, q:q + 1], a["L0_ffn_b_x"][q * P:(q + 1) * P].rearrange("(p o) -> p o", o=1)) for q in range(PAIRS)]
            assert len(small) == FFN_SMALL
            load_ffn("ld_small_ffn", small)
            sp.wait_ge(S("msg_ps"), 3 * SG + (NSG - 1) * SG)
            assert (NSG - 2) % 3 == 0
            load_ffn("ld_wx", [(wx_nat, tiled("L0_ffn_W_x"))])
            load_ffn("ld_ffn", [(wfx, tiled("L0_ffn_W_fx"))])
            sp.wait_ge(S("msg_ps"), 3 * SG + NSG * SG)
            load_ffn("ld_ffn", [(wout, tiled("L0_ffn_W_out"))])

            def store_out(b, s, n):
                sp.wait_ge(S("y_ready"), b + 3)
                sp.dma_start(out[ds(b * P, n), :], y[0:n, s, :]).then_inc(S("out_done"), 16)
                sp.wait_ge(S("out_done"), (b + 1) * 16)
                sp.sem_inc(S("y_free"), 1)
            with sp.Fori(0, FULL // 2) as i:
                for s in range(2):
                    store_out(i * 2 + s, s, P)
            store_out(FULL, 0, TAIL)

        @block.gpsimd
        def _(pool):
            own = Chain(pool, pool_own)
            g = nc.gpsimd
            g.memset(x_sb[:, FULL, :], 0.0).then_inc(S("x_zeroed"), 1)
            own.link(g.memset(src_i[:, :, :], 0))
            own.link(g.memset(typ_i[:, :, :], 0))
            g.memset(dstw_i[:, :, :], PAD_DST).then_inc(S("pads_set"), 1)
            own.link(g.memset(ident[:, :], 0.0))
            g.affine_select(out=ident[:, :], in_=ident[:, :], compare_op=ALU.not_equal, fill=1.0,
                            base=0, pattern=[[-1, P]], channel_multiplier=1).then_inc(S("ident_ready"), 1)
            pool.wait_ge(S("ident_ready"), 1)
            own.link(g.memset(ones[:, :], 1.0))
            own.link(g.memset(ones_bf[:, :], 1.0))
            own.link(g.affine_select(out=upper[:, :], in_=ones[:, :], compare_op=ALU.is_gt, fill=0.0,
                                     base=0, pattern=[[1, P]], channel_multiplier=-1))
            own.link(g.iota(iota_i[:, :], pattern=[[1, 512]], base=0, channel_multiplier=0))
            own.link(g.iota(step_i[:, :], pattern=[[P, KC]], base=0, channel_multiplier=1))
            own.link(g.tensor_copy(iota_row[:, :], iota_i[:, :]))
            own.link(g.tensor_copy(step_no[:, :], step_i[:, :]))
            own.link(g.tensor_copy(spread.rearrange("p (k h) -> p k h", h=H), ident[:, :].unsqueeze(2).to_broadcast([P, P, H])))
            own.link(g.memset(idle[:, :], 0.0))
            own.link(g.memset(chunk_row[:, :, :, :], -BIG))
            own.link(g.memset(attbd[:, :, :], 0.0))
            own.link(g.memset(tile_row[:, :, C_BLK + 1], 0.0))
            own.link(g.memset(ctx_bd[:, :, :], 0.0))
            own.link(g.memset(ks_bd[:, :, :], 0.0))
            own.link(g.memset(vones[:, :, :, P:P + 1], 1.0))
            for c in range(FC):
                if c == 0:
                    pool.wait_ge(S("ld_small"), 16 * 4)
                for j in range(P // D):
                    h = c * (P // D) + j
                    q = slice(D * j, D * j + D)
                    for k in range(2):
                        ins = g.tensor_copy(attbd[q, c, k * H + h:k * H + h + 1], att[q, k, c:c + 1])
                        if c == FC - 1 and j == P // D - 1 and k == 1:
                            ins.then_inc(S("consts"), 1)
                        else:
                            own.link(ins)
            pool.wait_ge(S("tiles_stored"), 16)
            pool.wait_ge(S("tk_ready"), 1)
            for c in range(KC):
                g.indirect_dma_start(step_row[:, c, :], None, tiles_d.ap(),
                                     bass.IndirectOffsetOnAxis(tcol_i[:, 3, c:c + 1].bitcast(U32), 0)).then_inc(S("steps_here"), 16)
            pool.wait_ge(S("xnT_ps"), NB)
            pool.wait_ge(S("bcast_done"), 1)
            g.tensor_tensor(x_sb[:, :, :], x_sb[:, :, :], bproj_b[:, :].unsqueeze(1).to_broadcast([P, NB, F]), ALU.add).then_inc(S("x_biased"), 1)

            pool.wait_ge(S("tab_stored"), 16 * NB)
            pool.wait_ge(S("cols_taken"), KC)

            def gather(g_, s):
                pool.wait_ge(S("msg_ps"), g_ * SG + SG)
                own.link(g.tensor_copy(idx_stage[:, s, :], idxT[:, ds(g_ * SG, SG)]))
                g.tensor_tensor(idle[:, 0:1], idle[:, 1:2], idle[:, 1:2], ALU.add)
                for t in range(SG):
                    g.indirect_dma_start(rows[:, s, t, :], None, table_rows,
                                         bass.IndirectOffsetOnAxis(idx_stage[:, s, t:t + 1].bitcast(U32), 0)).then_inc(S(f"rows_here{s}"), 16)
            def weigh(g_, s):
                pool.wait_ge(S("w_ready"), g_ * 2 + 2)
                m = rows[:, s, DVE_STEPS:SG, 0:F].rearrange("p t (h d) -> p t h d", h=H)
                g.tensor_tensor(m, m, w_sb[:, DVE_STEPS:SG, :].unsqueeze(3).to_broadcast([P, SG - DVE_STEPS, H, D]), ALU.mult).then_inc(S("msg_ready_pool"), 1)
            for g_ in range(2):
                gather(g_, g_)
            pool.wait_ge(S("q_ps"), FC * (NCH + 1))
            g.memset(arena2[:, :], 0.0).then_inc(S("acc_zeroed"), 1)
            assert (NSG - 2) % 3 == 0
            with pool.Fori(0, (NSG - 2) // 3) as i:
                own.enter(i, 3)
                for s in range(3):
                    weigh(i * 3 + s, s)
                    gather(i * 3 + s + 2, (s + 2) % 3)
                own.leave((NSG - 2) // 3)
            for g_ in range(NSG - 2, NSG):
                weigh(g_, g_ % 3)
            pool.wait_ge(S("rden_ready"), 1)
            at = acc[:, DVE_BLOCKS:NB, 0:F].rearrange("p b (h d) -> p b h d", h=H)
            own.link(g.tensor_tensor(at, at, rden[:, DVE_BLOCKS:NB, :].unsqueeze(3).to_broadcast([P, NB - DVE_BLOCKS, H, D]), ALU.mult))
            g.tensor_tensor(x_sb[:, DVE_BLOCKS:NB, :], x_sb[:, DVE_BLOCKS:NB, :], acc[:, DVE_BLOCKS:NB, 0:F], ALU.add).then_inc(S("x2_ready"), 1)

            def sum_up(b, k):
                pool.wait_ge(S("sw_ready"), b + 1)
                pool.wait_ge(S("sw_summed"), b + 1)
                g.tensor_tensor(idle[:, 0:1], idle[:, 1:2], idle[:, 1:2], ALU.add)
                g.tensor_tensor(swsum[0:k, :], swsum[0:k, :], sw[0:k, ds(b, 1), :].rearrange("p b k -> p (b k)"), ALU.add).then_inc(S("sw_summed"), 1)
            with pool.Fori(0, FULL) as i:
                sum_up(i, P)
            sum_up(FULL, TAIL)

        @block.scalar
        def _(act):
            own = Chain(act, act_own)
            act.sem_inc(S("tab_taken0"), 1)
            act.sem_inc(S("ohT_ready"), 1)
            s_ = nc.scalar
            for k, name in enumerate(("L0_gnn_attn_src", "L0_gnn_attn_dst")):
                for c in range(FC):
                    act.dma_start(att[:, k, c:c + 1], a[name][c * (P // D):(c + 1) * (P // D), :].rearrange("h (d o) -> (h d) o", o=1)) \
                       .then_inc(S("ld_small"), 16)
            act.dma_start(w_nat, a["L0_gnn_W"].rearrange("r (c o) f -> o r c f", c=FC)).then_inc(S("ld_w"), 16)
            act.dma_start(wq_nat.rearrange("p (c f) -> p c f", c=FC), a["L0_mix_Wq"].rearrange("(c o) f -> o c f", o=P)).then_inc(S("ld_w"), 16)
            act.dma_start(wkv_nat.rearrange("p (c f) -> p c f", f=F), a["L0_mix_Wkv"].rearrange("(c o) f -> o c f", o=P)).then_inc(S("ld_w"), 16)
            act.dma_start(wproj_nat.rearrange("p (c f) -> p c f", c=FC), a["L0_mix_Wproj"].rearrange("(c o) f -> o c f", o=P)).then_inc(S("ld_w"), 16)
            act.dma_start(bproj_r, a["L0_mix_bproj"].rearrange("(p f) -> p f", p=1)).then_inc(S("ld_w"), 16)
            act.dma_start(bout_r, a["L0_ffn_b_out"].rearrange("(p f) -> p f", p=1)).then_inc(S("ld_w"), 16)
            n = 0
            for dst, _ in set_jobs:
                act.wait_ge(S("set_ps"), n + 1)
                src = pb[n % 4][:, 0:dst.free_size()]
                if len(dst.shape) == 3:
                    src = src.rearrange("p (a b) -> p a b", a=dst.shape[1])
                s_.activation(dst, src, ACT.Copy).then_inc(S("set_taken"), 1)
                n += 1
            act.wait_ge(S("att_ready"), 1)
            wa = pb[4][:, 0:FC * R * 2 * H].rearrange("p (c r k) -> p c r k", c=FC, r=R)
            for c in range(FC):
                own.link(s_.activation(w_t[:, c, :, F:ROW], wa[:, c, :, 0:H], ACT.Copy))
            for c in range(FC):
                ins = s_.activation(w_adst[:, c, :, :].rearrange("p h r -> p r h"), wa[:, c, :, H:2 * H], ACT.Copy)
                if c == FC - 1:
                    ins.then_inc(S("set_taken"), 1)
                else:
                    own.link(ins)

            act.wait_ge(S("stats"), 1)
            s_.activation(rstd[:, :], rstd[:, :], ACT.Sqrt).then_inc(S("sqrt_done"), 1)

            def normalise(b, s):
                s_.activation(xn[:, s, :], x_sb[:, ds(b, 1), :].rearrange("p b f -> p (b f)"), ACT.Identity,
                              bias=nmr[:, ds(b, 1)], scale=rstd[:, ds(b, 1)]).then_inc(S("xn_ready"), 1)

            def take_transposes(b, s):
                act.wait_ge(S("xnT_ps"), b + 1)
                s_.activation(xnT[:, s, :, :].rearrange("p c n -> p (c n)"), pb[s][:, 0:FC * P], ACT.Copy).then_inc(S("xnT_ready"), 1)

            def block_work(b, s, last=False):
                if not last:
                    normalise(b + 1, 1 - s)
                act.wait_ge(S("kv_ps"), b + 1)
                s_.activation(vones[:, s, :, 0:P], pb[5 + s][:, F:2 * F].rearrange("p (c n) -> p c n", c=FC), ACT.Copy).then_inc(S("v_ready"), 1)
                act.wait_ge(S("kmin_ready"), b + 1)
                s_.activation(kexp[:, s, :], kmin[:, s, :], ACT.Exp).then_inc(S("kexp_ready"), 1)
                for r in range(0, R, 2):
                    if r == R // 2 and not last:
                        take_transposes(b + 1, 1 - s)
                    act.wait_ge(S("tab_ps0"), b * (R // 2) + r // 2 + 1)
                    if r == 0:
                        act.wait_ge(S("row_free"), b + 1)
                    s_.activation(tab_row[:, s, r * ROW:(r + 1) * ROW], pb[2][:, 0:ROW], ACT.Copy).then_inc(S("tab_taken0"), 1)

            act.wait_ge(S("rstd_ready"), 1)
            act.wait_ge(S("consts"), 1)
            normalise(0, 0)
            take_transposes(0, 0)
            with act.Fori(0, FULL // 2) as i:
                for s in range(2):
                    block_work(i * 2 + s, s)
            block_work(FULL, 0, last=True)

            act.wait_ge(S("ctx_ps"), 1)
            own.link(s_.activation(ctx_sb[:, :, :], pb[7][:, 0:FC * (P + 1)].rearrange("p (c n) -> p c n", c=FC), ACT.Copy))
            for c in range(FC):
                for j in range(P // D):
                    q = slice(D * j, D * j + D)
                    own.link(s_.activation(ctx_bd[q, c, D * j:D * j + D], ctx_sb[q, c, D * j:D * j + D], ACT.Copy))
                    ins = s_.activation(ks_bd[q, c, D * j:D * j + D], ones[q, 0:D], ACT.Copy, scale=ctx_sb[q, c, P:P + 1])
                    if c == FC - 1 and j == P // D - 1:
                        ins.then_inc(S("ctx_ready"), 1)
                    else:
                        own.link(ins)

            def one_hots(n, so):
                act.wait_ge(S("msg_ps"), (n + 1) * SG)
                for t in range(SG):
                    s_.activation(oh[so][:, t, :], iota_row[:, 0:P], ACT.Square, bias=dstlT[:, ds(n * SG + t, 1)], scale=-1.0).then_inc(S("squared"), 1)
                act.wait_ge(S("squared"), n * SG + SG)
                s_.activation(oh[so], oh[so], ACT.Relu, bias=ones[:, 0:1], scale=-1.0).then_inc(S("oh_ready"), 1)
            def chunk(qn, s, n):
                for c in range(FC):
                    act.wait_ge(S("q_ps"), qn * FC + c + 1)
                    act.wait_ge(S("lin_ps"), qn * FC + FC)
                    s_.activation(qT[s][c][:, 0:n], pb[c][:, 0:n], ACT.Relu).then_inc(S("qrelu_ready"), 1)
                    act.wait_ge(S("q_ready"), qn * FC + c + 1)
                    s_.activation(qexp[:, c, 0:n], pb[c][:, 0:n], ACT.Exp).then_inc(S("qexp_ready"), 1)
            with act.Fori(0, NCH // 2) as i:
                for s in range(2):
                    chunk(i * 2 + s, s, 512)
            one_hots(0, 0)
            chunk(NCH, NCH % 2, TAIL)

            def take_one_hots(n, *quads):
                for q in quads:
                    act.wait_ge(S("ohT_ps"), n * 4 + q + 1)
                    s_.activation(ohT[:, q * 4:q * 4 + 4, :].rearrange("p t e -> p (t e)"), pb[0][:, :], ACT.Copy).then_inc(S("ohT_ready"), 1)

            def stage_breaks(n):
                s_.activation(brk_g[:, :], brk[:, ds(n, 1), :].rearrange("p g e -> p (g e)"), ACT.Copy).then_inc(S("breaks_here"), 1)
                s_.activation(brk2[:, :], brk_sum[:, ds(n, 1), :].rearrange("p g k -> p (g k)"), ACT.Copy).then_inc(S("breaks_here"), 1)

            def take_breaks(n):
                act.wait_ge(S("breaks_ps"), n + 1)
                s_.activation(chunk_row[0:1, 2:4, :, 1:SG + 1], pb[4][0:1, 2 * P:4 * P].rearrange("p (k t h) -> p k h t", k=2, h=H), ACT.Copy).then_inc(S("breaks_taken"), 1)

            def turn(g_, u, third, scores=True, messages=True, more=True):
                if not scores:
                    return
                n, slot = g_ + 1, (u + 1) % 3
                if more:
                    one_hots(n + 1, (u + 2) % 3)
                    take_one_hots(n + 1, 0, 1)
                act.wait_ge(S("fac_ps"), n + 1)
                s_.activation(fac[:, :], pb[5][:, 8:8 + H], ACT.Exp).then_inc(S("fac_ready"), 1)
                if more:
                    take_one_hots(n + 1, 2)
                act.wait_ge(S("below_ready"), n + 1)
                s_.activation(wT[:, :], below[:, :], ACT.Exp).then_inc(S("exp_ready"), 1)
                if more:
                    stage_breaks(n + 1)
                act.wait_ge(S("w_ps"), n + 1)
                wp = pb[4][:, P:2 * P].rearrange("p (t h) -> p t h", h=H)
                s_.activation(w_sb[:, :, :], wp, ACT.Copy).then_inc(S("w_ready"), 1)
                s_.activation(rows[:, slot, :, F:ROW], wp, ACT.Copy).then_inc(S("w_ready"), 1)
                if more:
                    take_one_hots(n + 1, 3)
                    take_breaks(n + 1)
            act.wait_ge(S("proj_taken"), NB + 1)
            take_one_hots(0, 0, 1, 2, 3)
            stage_breaks(0)
            take_breaks(0)
            turn(-1, -1, 0, messages=False)
            with act.Fori(0, NSG // 3) as i:
                for u in range(3):
                    turn(i * 3 + u, u, i)
            for g_ in range(NSG // 3 * 3, NSG):
                turn(g_, g_ % 3, NSG // 3, scores=g_ + 1 < NSG, more=g_ + 2 < NSG)
            act.wait_ge(S("acc_added"), STEPS + 3)
            for k in range(2):
                act.wait_ge(S("wxT_ps"), k + 1)
                s_.activation(wxT[:, k * 2:k * 2 + 2, :].rearrange("p q f -> p (q f)"), pb[k][:, :], ACT.Copy).then_inc(S("wxT_ready"), 1)
            for c in range(FC):
                act.wait_ge(S("comb_ps"), c + 1)
                s_.activation(comb[:, c, :], pb[2 + c][:, :], ACT.Copy).then_inc(S("comb_ready"), 1)
            act.wait_ge(S("bias_ps"), 1)
            s_.activation(bias_b[:, :], pb[6][:, :], ACT.Copy).then_inc(S("bias_b_ready"), 1)
            act.wait_ge(S("stats"), 2)
            s_.activation(rstd[:, :], rstd[:, :], ACT.Sqrt).then_inc(S("sqrt_done"), 1)

            def node_block(b, u):
                if u >= 4:
                    act.wait_ge(S("swx_ps"), b - 3)
                s_.activation(xn4[:, u % 4, :], x_sb[:, ds(b, 1), :].rearrange("p b f -> p (b f)"), ACT.Identity,
                              bias=nmr[:, ds(b, 1)], scale=rstd[:, ds(b, 1)]).then_inc(S("xn_ready"), 1)
                act.wait_ge(S("xnT_ps"), NB + b + 1)
                s_.activation(xnT[:, u % 2, :, :].rearrange("p c n -> p (c n)"), pb[u % 2][:, 0:FC * P], ACT.Copy).then_inc(S("xnT_ready"), 1)

            def slice_exp(b, u):
                act.wait_ge(S("logit_ready"), b + 1)
                for h in range(H):
                    lg = logit[:, u % 2, h * G:(h + 1) * G]
                    s_.activation(lg, lg, ACT.Exp, bias=top[:, u % 2, h:h + 1]).then_inc(S("lexp_ready"), 1)
            act.wait_ge(S("rstd_ready"), 2)
            for b in range(4):
                node_block(b, b)
                if b > 0:
                    slice_exp(b - 1, b - 1)
            with act.Fori(0, (NB - 5) // 4) as i:
                for u in range(4, 8):
                    node_block(i * 4 + u, u)
                    slice_exp(i * 4 + u - 1, u - 1)
            for b in range((NB - 5) // 4 * 4 + 4, NB):
                node_block(b, b)
                slice_exp(b - 1, b - 1)
            slice_exp(NB - 1, NB - 1)
            for k, to in enumerate((qs, ks, vs)):
                act.wait_ge(S("qkv_ps"), k + 1)
                s_.activation(to[0:DH, :], pb[k][0:DH, :], ACT.Copy).then_inc(S("qkv_ready"), 1)
            act.wait_ge(S("attn_below"), 1)
            s_.activation(att_g[0:G, :], att_g[0:G, :], ACT.Exp, scale=float(DH) ** -0.5).then_inc(S("attn_exp"), 1)
            for k in range(2):
                act.wait_ge(S("v2_ps"), k + 1)
                s_.activation(v2[:, 2 * k:2 * k + 2, :].rearrange("p q f -> p (q f)"), pb[6 + k][:, :], ACT.Copy).then_inc(S("v2_ready"), 1)

            def stage(b, s):
                s_.activation(sws[:, s, :], sw[:, ds(b, 1), :].rearrange("p b k -> p (b k)"), ACT.Copy).then_inc(S("sws_ready"), 1)

            def out_block(b, s, more):
                act.wait_ge(S("swT_ps"), b + 1)
                act.wait_ge(S("y_ps"), b + 1)
                s_.activation(swT[:, s, :], pb[s][:, :], ACT.Copy).then_inc(S("swT_ready"), 1)
                if more:
                    stage(b + 2, s)
            act.wait_ge(S("v2_ready"), 2)
            stage(0, 0)
            stage(1, 1)
            with act.Fori(0, FULL // 2 - 1) as i:
                for s in range(2):
                    out_block(i * 2 + s, s, True)
            out_block(FULL - 2, 0, True)
            out_block(FULL - 1, 1, False)
            out_block(FULL, 0, False)

        @block.tensor
        def _(pe):
            mm, tr = nc.tensor.matmul, nc.tensor.transpose
            pe.sem_inc(S("lin_ps"), 2 * FC)
            pe.sem_inc(S("y_ps"), 2)
            pe.sem_inc(S("msg_ps"), 3 * SG)
            pe.wait_ge(S("ident_ready"), 1)
            pe.wait_ge(S("ld_w"), 16 * 6)
            n = 0
            for _, srcs in set_jobs:
                if n == R:
                    pe.wait_ge(S("consts"), 1)
                    pe.wait_ge(S("n_ready"), 1)
                    mm(pb[5][:, 0:TJ], upper[:, :], tcol[:, 0, :], start=True, stop=False)
                    mm(pb[5][:, 0:TJ], ones[:, :], tcol[:, 1, :], start=False, stop=True).then_inc(S("first_ps"), 1)
                if n >= 4:
                    pe.wait_ge(S("set_taken"), n - 3)
                for k, src in enumerate(srcs):
                    ins = tr(pb[n % 4][:, k * P:(k + 1) * P], src, ident[:, :])
                ins.then_inc(S("set_ps"), 1)
                n += 1
            pe.wait_ge(S("cmp_ready"), 1)
            for c in range(KC):
                for j in range(TJ):
                    ins = mm(pb[6][:, c:c + 1], reached[:, j, c * P:(c + 1) * P], ones_bf[:, :], start=(j == 0), stop=(j == TJ - 1))
            ins.then_inc(S("tk_ps"), 1)
            pe.wait_ge(S("consts"), 1)
            for c in range(FC):
                for r in range(R):
                    o = (c * R + r) * 2 * H
                    for k in range(FC):
                        ins = mm(pb[4][:, o:o + 2 * H], w_nat[:, r, k, c * P:(c + 1) * P], attbd[:, k, :], start=(k == 0), stop=(k == FC - 1))
            ins.then_inc(S("att_ready"), 1)
            mm(pb[7][:, 0:F], ones[0:1, :], bproj_r, start=True, stop=True)
            mm(pb[7][:, F:2 * F], ones[0:1, :], bout_r, start=True, stop=True).then_inc(S("bcast_ps"), 1)
            pe.wait_ge(S("steprow_ready"), 1)
            pe.wait_ge(S("set_taken"), len(set_jobs))
            for k, col in enumerate((C_DST, C_IDX, C_TYP)):
                for c in range(KC):
                    ins = tr(pb[k][:, c * P:(c + 1) * P], step_row[:, c, col:col + P], ident[:, :])
                ins.then_inc(S("cols_ps"), 1)
            for c in range(KC):
                ins = tr(pb[3][0:1, c * P:(c + 1) * P], tcol[:, 6, c:c + 1], ident[:, :])
            ins.then_inc(S("b_ps"), 1)
            for gq in range(0, NSG, 3):
                bank = pb[5 + (gq // 3) % 2]
                if gq >= 6:
                    pe.wait_ge(S("brk_taken"), gq // 3 - 1)
                for gg in range(gq, min(gq + 3, NSG)):
                    c, off = gg * SG // P, gg * SG % P
                    ins = mm(bank[:, (gg - gq) * (P + 1):(gg - gq + 1) * (P + 1)], spread[:, off * H:off * H + P], step_row[:, c, C_BRK:C_BRK + P + 1], start=True, stop=True)
                ins.then_inc(S("brk_ps"), 1)
            pe.wait_ge(S("brk_taken"), -(-NSG // 3))
            pe.wait_ge(S("bcast_done"), 1)
            pe.wait_ge(S("set_taken"), len(set_jobs) + 1)
            pe.wait_ge(S("cols_taken"), 4)

            mm(pb[7][:, 0:FC * (P + 1)], ks_bd[:, 0, :], iota_row[:, 0:FC * (P + 1)], start=True, stop=False, skip_group_check=True)

            def transposes(b, s):
                pe.wait_ge(S("xn_ready"), b + 1)
                pe.wait_ge(S("xnT_kept"), b + 1)
                for c in range(FC):
                    ins = tr(pb[s][:, c * P:(c + 1) * P], xn[:, s, c * P:(c + 1) * P], ident[:, :])
                ins.then_inc(S("xnT_ps"), 1)

            def block_work(b, s, last=False):
                k = TAIL if last else P
                pe.wait_ge(S("xnT_ready"), b + 1)
                for c in range(FC):
                    ins = mm(pb[5 + s][:, :], xnT[:, s, c, :], wkvT[:, c, :], start=(c == 0), stop=(c == FC - 1))
                ins.then_inc(S("kv_ps"), 1)
                pe.wait_ge(S("ad_taken"), b + 1)
                for c in range(FC):
                    ins = mm(pb[4][:, 0:H * R], xnT[:, s, c, :], w_adst[:, c, :, :].rearrange("p h r -> p (h r)"), start=(c == 0), stop=(c == FC - 1))
                ins.then_inc(S("ad_ps"), 1)
                for r in range(R):
                    if r == R // 2 and not last:
                        transposes(b + 1, 1 - s)
                    pe.wait_ge(S(f"tab_taken{r % 2}"), b * (R // 2) + r // 2 + 1)
                    for c in range(FC):
                        ins = mm(pb[2 + r % 2][:, 0:ROW], xnT[:, s, c, :], w_t[:, c, r, :], start=(c == 0), stop=(c == FC - 1))
                    ins.then_inc(S(f"tab_ps{r % 2}"), 1)
                pe.wait_ge(S("k_ready"), b + 1)
                pe.wait_ge(S("v_ready"), b + 1)
                for c in range(FC):
                    ins = mm(pb[7][:, c * (P + 1):(c + 1) * (P + 1)], kphi[0:k, s, c * P:(c + 1) * P], vones[0:k, s, c, :],
                             start=False, stop=last and c == FC - 1, skip_group_check=True)
                if last:
                    ins.then_inc(S("ctx_ps"), 1)

            transposes(0, 0)
            with pe.Fori(0, FULL // 2) as i:
                for s in range(2):
                    block_work(i * 2 + s, s)
            block_work(FULL, 0, last=True)


            def queries(qn, n):
                for c in range(FC):
                    pe.wait_ge(S("q_ready"), qn * FC + c + 1)
                    for f in range(FC):
                        ins = mm(pb[c][:, 0:n], wqT[:, f, c * P:(c + 1) * P], xnT_all[:, f, ds(qn * 512, n)], start=(f == 0), stop=(f == FC - 1))
                    ins.then_inc(S("q_ps"), 1)

            def attend(qn, s, n, c):
                pe.wait_ge(S("q_ready"), qn * FC + FC + c + 1)
                mm(pb[2 + c][:, 0:n], ctx_bd[:, c, :], qT[s][c][:, 0:n], start=True, stop=True)
                mm(pb[4 + c][:, 0:n], ks_bd[:, c, :], qT[s][c][:, 0:n], start=True, stop=True).then_inc(S("lin_ps"), 1)

            def project(qn, s, n):
                pe.wait_ge(S("lin_ready"), qn * FC + FC)
                pe.wait_ge(S("proj_taken"), qn * 4 + 1)
                for j in range(-(-n // P)):
                    m = min(P, n - j * P)
                    for c in range(FC):
                        ins = mm(pb[6 + j // 2][0:m, j % 2 * F:j % 2 * F + F], attT2[s][:, c, j * P:j * P + m], wprojT[:, c, :], start=(c == 0), stop=(c == FC - 1))
                ins.then_inc(S("proj_ps"), 1)

            size = lambda qn: 512 if qn < NCH else TAIL

            def chunk(qn, s, static=False):
                attend(qn + 1, 1 - s, size(qn + 1) if static else 512, 0)
                if not static or qn + 2 <= NCH:
                    queries(qn + 2, size(qn + 2) if static else 512)
                project(qn, s, 512)
                attend(qn + 1, 1 - s, size(qn + 1) if static else 512, 1)
            queries(0, 512)
            pe.wait_ge(S("ctx_ready"), 1)
            attend(0, 0, 512, 0)
            queries(1, 512)
            attend(0, 0, 512, 1)
            with pe.Fori(0, (NCH - 2) // 2) as i:
                for s in range(2):
                    chunk(i * 2 + s, s)
            for qn in range((NCH - 2) // 2 * 2, NCH):
                chunk(qn, qn % 2, static=True)
            project(NCH, NCH % 2, TAIL)

            regs = [pe.alloc_register(f"pe_block{k}") for k in range(8)]

            def transposes(n, so, *quads):
                pe.wait_ge(S("oh_ready"), n + 1)
                for q in quads:
                    pe.wait_ge(S("ohT_ready"), n * 4 + q + 1)
                    for t in range(4):
                        ins = tr(pb[0][:, t * P:(t + 1) * P], oh[so][:, q * 4 + t, :], ident[:, :])
                    ins.then_inc(S("ohT_ps"), 1)

            def breaks(n):
                pe.wait_ge(S("breaks_here"), (n + 1) * 2)
                for k in range(2):
                    ins = tr(pb[4][0:1, (2 + k) * P:(3 + k) * P], brk2[:, k:k + 1], ident[:, :])
                ins.then_inc(S("breaks_ps"), 1)

            def turn(g_, u, third, scores=True, messages=True, more=True):
                n, so, slot, mo = g_ + 1, (u + 1) % 3, u % 3, u % 3

                def send(t0, t1):
                    for t in range(t0, t1) if messages else ():
                        if t % 8 == 0:
                            pe.wait_ge(S("msg_ready"), g_ * 2 + t // 8 + 1)
                        if t == DVE_STEPS:
                            pe.wait_ge(S("msg_ready_pool"), g_ + 1)
                        pe.wait_ge(S("acc_added"), g_ * SG + t + 1)
                        mm(sums[(u * SG + t) % 3][:, 0:ROW], oh[mo][:, t, :], rows[:, slot, t, :], start=True, stop=True).then_inc(S("msg_ps"), 1)

                def dst_scores(half):
                    bs = load_blocks(pe, brow[0:1, ds(n * SG + half * 8, 8)], NB - 1, regs)
                    for t in range(half * 8, half * 8 + 8):
                        if t % 4 == 0:
                            pe.wait_ge(S("ohT_ready"), n * 4 + t // 4 + 2)
                        ins = mm(pb[2 + half][:, t % 8 * H * R:(t % 8 + 1) * H * R], ohT[:, t, :], adst[:, ds(bs[t % 8], 1), :].rearrange("p b k -> p (b k)"),
                                 start=True, stop=True)
                    ins.then_inc(S("dsc_ps"), 1)
                if not scores:
                    send(0, SG)
                    return
                dst_scores(0)
                dst_scores(1)
                send(0, 6)
                pe.wait_ge(S("breaks_taken"), n + 1)
                pe.wait_ge(S("score_ready"), n + 1)
                tr(pb[4][:, 0:P], score[:, :, :].rearrange("p t h -> p (t h)"), ident[:, :]).then_inc(S("scoreT_ps"), 1)
                send(6, 8)
                pe.wait_ge(S("ends_ready"), n + 1)
                for k, col in enumerate((run[:, 0, P - 1:P], run[:, 1, 0:1])):
                    ins = tr(pb[5][0:1, k * P:(k + 1) * P], col, ident[:, :])
                ins.then_inc(S("ends_ps"), 1)
                send(8, 10)
                if more:
                    transposes(n + 1, (u + 2) % 3, 0)
                pe.wait_ge(S("carry_ready"), n + 1)
                for k in range(2):
                    ins = mm(pb[5][:, k:k + 1], carry_flat[0:1, k, :], ones[0:1, 0:1], start=True, stop=True)
                ins.then_inc(S("seg0_ps"), 1)
                send(10, 12)
                if more:
                    transposes(n + 1, (u + 2) % 3, 1)
                pe.wait_ge(S("seg0_taken"), n + 1)
                mm(pb[5][:, 8:8 + H], oh[so][0:1, 0, :], ex[0:1, 2, :], start=True, stop=True).then_inc(S("fac_ps"), 1)
                if more:
                    transposes(n + 1, (u + 2) % 3, 2)
                send(12, 14)
                pe.wait_ge(S("exp_ready"), n + 1)
                tr(pb[4][:, P:2 * P], wT[:, :], ident[:, :]).then_inc(S("w_ps"), 1)
                send(14, 16)
                if more:
                    transposes(n + 1, (u + 2) % 3, 3)
                if more:
                    pe.wait_ge(S("w_ready"), (n + 1) * 2)
                    breaks(n + 1)
            transposes(0, 0, 0, 1, 2, 3)
            breaks(0)
            turn(-1, -1, 0, messages=False)
            with pe.Fori(0, NSG // 3) as i:
                for u in range(3):
                    turn(i * 3 + u, u, i)
            for g_ in range(NSG // 3 * 3, NSG):
                if g_ == NSG - 1:
                    pe.wait_ge(S("itemp_ready"), 1)
                    mm(pb[2][:, :], ones[0:1, :], itemp_r, start=True, stop=True).then_inc(S("itemp_ps"), 1)
                turn(g_, g_ % 3, NSG // 3, scores=g_ + 1 < NSG, more=g_ + 2 < NSG)

            pe.wait_ge(S("ld_wx"), 16)
            pe.wait_ge(S("acc_added"), STEPS + 3)
            for k in range(2):
                for q in range(2):
                    for c in range(FC):
                        ins = tr(pb[k][:, (q * FC + c) * P:(q * FC + c + 1) * P], wx_nat[:, c, (2 * k + q) * P:(2 * k + q + 1) * P], ident[:, :])
                ins.then_inc(S("wxT_ps"), 1)
            pe.wait_ge(S("slice2_ready"), 1)
            for q in range(PAIRS):
                ins = mm(pb[4][0:1, q * P:(q + 1) * P], bx_col[:, q:q + 1], slice2t[:, q * P:(q + 1) * P], start=True, stop=True)
            ins.then_inc(S("bx_ps"), 1)
            pe.wait_ge(S("wxT_ready"), 2)
            for c in range(FC):
                for q in range(PAIRS):
                    ins = mm(pb[2 + c][:, q * P:(q + 1) * P], wxT[:, q, c * P:(c + 1) * P], slice2t[:, q * P:(q + 1) * P], start=True, stop=True)
                ins.then_inc(S("comb_ps"), 1)
            pe.wait_ge(S("bias_ready"), 1)
            mm(pb[6][:, :], ones[0:1, :], bias_r, start=True, stop=True).then_inc(S("bias_ps"), 1)
            pe.wait_ge(S("comb_ready"), FC)
            for c in range(FC):
                mm(pb[4 + c][:, :], ctx_bd[:, 0, :], iota_row[:, :], start=True, stop=False, skip_group_check=True)

            def transposes(b, u):
                pe.wait_ge(S("xn_ready"), NB + b + 1)
                for c in range(FC):
                    ins = tr(pb[u % 2][:, c * P:(c + 1) * P], xn4[:, u % 4, c * P:(c + 1) * P], ident[:, :])
                ins.then_inc(S("xnT_ps"), 1)

            def logits(b, u):
                pe.wait_ge(S("xnT_ready"), NB + b + 1)
                for c in range(FC):
                    ins = mm(pb[2 + u % 2][:, :], xnT[:, u % 2, c, :], comb[:, c, :], start=(c == 0), stop=(c == FC - 1))
                ins.then_inc(S("logit_ps"), 1)

            def weighted(b, u, last=False):
                k = TAIL if last else P
                pe.wait_ge(S("sw_ready"), b + 1)
                for c in range(FC):
                    ins = mm(pb[4 + c][:, :], xn4[0:k, u % 4, c * P:(c + 1) * P], sw[0:k, ds(b, 1), :].rearrange("p b k -> p (b k)"),
                             start=False, stop=last, skip_group_check=True)
                ins.then_inc(S("swx_ps"), 1)
            def slice_turn(b, u):
                logits(b + 2, u + 2)
                transposes(b + 3, u + 3)
                weighted(b, u)
            for b in range(2):
                transposes(b, b)
                logits(b, b)
            transposes(2, 2)
            slice_turn(0, 0)
            with pe.Fori(0, (NB - 5) // 4) as i:
                for u in range(1, 5):
                    slice_turn(i * 4 + u, u)
            for b in range((NB - 5) // 4 * 4 + 1, NB - 3):
                slice_turn(b, b)
            logits(NB - 1, NB - 1)
            weighted(NB - 3, NB - 3)
            weighted(NB - 2, NB - 2)
            weighted(NB - 1, NB - 1, last=True)

            heads = [slice(h * G, (h + 1) * G) for h in range(H)]
            pe.wait_ge(S("sw_summed"), NB + 1)
            mm(pb[6][:, :], ones[:, :], swsum, start=True, stop=True).then_inc(S("norm_ps"), 1)
            pe.wait_ge(S("norm_ready"), 1)
            pe.wait_ge(S("ld_ffn"), 16 * 2)
            for h in heads:
                for c in range(FC):
                    mm(pb[7][0:DH, h], wfx[:, c, h], swxT[:, c, h], start=(c == 0), stop=False)
                ins = mm(pb[7][0:DH, h], bfx_r[0:1, h], norm_r[0:1, h], start=False, stop=True)
            ins.then_inc(S("tok_ps"), 1)
            pe.wait_ge(S("tok_ready"), 1)
            for k in range(2):
                mm(pb[k][0:DH, :], wqkv[:, k, :], tokT[:, :], start=True, stop=True).then_inc(S("qkv_ps"), 1)
            for h in heads:
                ins = mm(pb[2][0:G, h], tokT[:, h], wqkv[:, 2, :], start=True, stop=True)
            ins.then_inc(S("qkv_ps"), 1)
            pe.wait_ge(S("qkv_ready"), 2)
            for h in heads:
                ins = mm(pb[3][0:G, h], qs[0:DH, h], ks[0:DH, h], start=True, stop=True)
            ins.then_inc(S("attn_ps"), 1)
            pe.wait_ge(S("attn_ready"), 1)
            for h in heads:
                ins = tr(pb[4][0:G, h], att_g[0:G, h], ident[0:G, 0:G])
            ins.then_inc(S("attnT_ps"), 1)
            pe.wait_ge(S("attnT_ready"), 1)
            pe.wait_ge(S("qkv_ready"), 3)
            for n, h in enumerate(heads):
                ins = mm(pb[5][:, h], vs[0:G, n // 2 * P:n // 2 * P + P], attnT[0:G, h], start=True, stop=True)
            ins.then_inc(S("os_ps"), 1)
            pe.wait_ge(S("os_ready"), 1)
            for k in range(2):
                for q in range(2):
                    ins = mm(pb[6 + k][:, q * F:(q + 1) * F], osbd[:, 2 * k + q, :], wout[:, 2 * k + q, :], start=True, stop=True)
                ins.then_inc(S("v2_ps"), 1)

            pe.wait_ge(S("v2_ready"), 2)

            def transposes(b, s):
                pe.wait_ge(S("sws_ready"), b + 1)
                for q in range(PAIRS):
                    ins = tr(pb[s][:, q * P:(q + 1) * P], sws[:, s, q * P:(q + 1) * P], ident[:, :])
                ins.then_inc(S("swT_ps"), 1)

            def out_block(b, s, last=False):
                if not last:
                    transposes(b + 1, 1 - s)
                pe.wait_ge(S("swT_ready"), b + 1)
                pe.wait_ge(S("y_ready"), b + 1)
                for q in range(PAIRS):
                    ins = mm(pb[2 + s][:, 0:F], swT[:, s, q * P:(q + 1) * P], v2[:, q, :], start=(q == 0), stop=(q == PAIRS - 1))
                ins.then_inc(S("y_ps"), 1)
            transposes(0, 0)
            with pe.Fori(0, FULL // 2) as i:
                for s in range(2):
                    out_block(i * 2 + s, s)
            out_block(FULL, 0, last=True)

        @block.vector
        def _(dve):
            own = Chain(dve, dve_own)
            for name, free in (("xnT_kept", 1), ("ad_taken", 1), ("tab_taken1", 1), ("proj_taken", 1), ("q_ready", FC), ("acc_added", 3), ("y_ready", 2)):
                dve.sem_inc(S(name), free)
            v = nc.vector
            tt, ts, stt, cp = v.tensor_tensor, v.tensor_scalar, v.scalar_tensor_tensor, v.tensor_copy
            dve.wait_ge(S("ld_edges"), 16 * (6 + 2 + (TJ - 2) + 2))
            own.link(cp(dstw[:, :, :], dstw_i[:, :, :]))
            own.link(cp(tile_row[:, :, C_DST:C_DST + P], dstw_i[:, :, 1:P + 1]))
            own.link(stt(tile_row[:, :, C_IDX:C_IDX + P], src_i[:, :, :], float(R), typ_i[:, :, :], ALU.mult, ALU.add))
            own.link(cp(tile_row[:, :, C_TYP:C_TYP + P], typ_i[:, :, :]))
            own.link(tt(tile_row[:, :, C_BRK:C_BRK + P + 1], dstw[:, :, 1:P + 2], dstw[:, :, 0:P + 1], ALU.not_equal))
            own.link(ts(tile_row[:, :, C_BRK:C_BRK + P + 1], tile_row[:, :, C_BRK:C_BRK + P + 1], -BIG, None, ALU.mult))
            own.link(cp(tcol_i[:, 0, :], dstw_i[:, :, 1]))
            own.link(stt(real, dstw[:, :, 1:P + 1], float(PAD_DST), dstw[:, :, 1:P + 1], ALU.is_lt, ALU.mult))
            own.link(v.tensor_reduce(tcol[:, 2, :], real, AX, ALU.max))
            own.link(cp(tcol_i[:, 1, :], tcol[:, 2, :]))
            own.link(ts(tcol_i[:, 2:4, :], tcol_i[:, 0:2, :], 7, None, ALU.arith_shift_right))
            own.link(cp(tcol[:, 3:5, :], tcol_i[:, 2:4, :]))
            own.link(tt(tcol[:, 0, :], tcol[:, 4, :], tcol[:, 3, :], ALU.subtract))
            own.link(ts(tcol[:, 0, :], tcol[:, 0, :], 1.0, 0.0, ALU.add, ALU.max))
            own.link(v.memset(tcol[:, 1, 0:1], 0.0))
            for j in range(1, TJ):
                own.link(tt(tcol[:, 1, j:j + 1], tcol[:, 1, j - 1:j], tcol[:, 0, j - 1:j], ALU.add))
            cp(tile_row[:, :, C_BLK], tcol[:, 3, :]).then_inc(S("n_ready"), 1)
            dve.wait_ge(S("first_ps"), 1)
            cp(tile_row[:, :, C_FIRST], pb[5][:, 0:TJ]).then_inc(S("tiles_ready"), 1)
            dve.wait_ge(S("tiles_ready"), 1)
            dve.wait_ge(S("consts"), 1)
            tt(reached[:, :, :], iota_row[:, :].unsqueeze(1).to_broadcast([P, TJ, 512]),
               tile_row[:, :, C_FIRST:C_FIRST + 1].to_broadcast([P, TJ, 512]), ALU.is_ge).then_inc(S("cmp_ready"), 1)
            dve.wait_ge(S("tk_ps"), 1)
            own.link(ts(tcol[:, 5, :], pb[6][:, 0:KC], -1.0, float(TILES - 1), ALU.add, ALU.min))
            cp(tcol_i[:, 3, :], tcol[:, 5, :]).then_inc(S("tk_ready"), 1)
            dve.wait_ge(S("ld_x"), 32)

            def node_stats(turn):
                for b in range(NB):
                    ins = v.bn_stats(bn6[:, b, :], x_sb[:, b, :])
                own.link(ins)
                for b in range(NB):
                    ins = v.bn_aggr(mv[:, b, :], bn6[:, b, :])
                own.link(ins)

            def node_rstd(turn):
                dve.wait_ge(S("sqrt_done"), turn)
                own.link(v.reciprocal(rstd[:, :], rstd[:, :]))
                stt(nmr[:, :], mv[:, :, 0], -1.0, rstd[:, :], ALU.mult, ALU.mult).then_inc(S("rstd_ready"), 1)
            node_stats(1)
            ts(rstd[:, :], mv[:, :, 1], LN_EPS, None, ALU.add).then_inc(S("stats"), 1)
            dve.wait_ge(S("steps_here"), 16 * KC)
            own.link(tt(tcol[:, 7, :], step_no[:, :], step_row[:, :, C_FIRST], ALU.subtract))
            own.link(tt(tcol[:, 7, :], tcol[:, 7, :], step_row[:, :, C_BLK], ALU.add))
            own.link(ts(tcol[:, 5, :], tcol[:, 7, :], -float(P), None, ALU.mult))
            for c in range(KC):
                own.link(ts(step_row[:, c, C_DST:C_DST + P], step_row[:, c, C_DST:C_DST + P], tcol[:, 5, c:c + 1], None, ALU.add))
            ts(tcol[:, 6, :], tcol[:, 7, :], float(NB - 1), None, ALU.min).then_inc(S("steprow_ready"), 1)
            node_rstd(1)
            dve.wait_ge(S("bcast_ps"), 1)
            own.link(cp(bproj_b[:, :], pb[7][:, 0:F]))
            cp(bout_b[:, :], pb[7][:, F:2 * F]).then_inc(S("bcast_done"), 1)
            for k, dst in enumerate((dstlT, idxT, typT)):
                dve.wait_ge(S("cols_ps"), k + 1)
                cp(dst[:, :], pb[k][:, :]).then_inc(S("cols_taken"), 1)
            dve.wait_ge(S("b_ps"), 1)
            cp(brow[0:1, :], pb[3][0:1, :]).then_inc(S("cols_taken"), 1)
            for q, gq in enumerate(range(0, NSG, 3)):
                m = min(3, NSG - gq)
                dve.wait_ge(S("brk_ps"), q + 1)
                cp(brk[:, gq:gq + m, :], pb[5 + q % 2][:, 0:m * (P + 1)].rearrange("p (g e) -> p g e", g=m)).then_inc(S("brk_taken"), 1)

            def block_work(b, s):
                dve.wait_ge(S("xnT_ready"), b + 1)
                cp(xnT_all[:, :, ds(b * P, P)], xnT[:, s, :, :]).then_inc(S("xnT_kept"), 1)
                dve.wait_ge(S("v_ready"), b + 1)
                ts(kmin[:, s, :], pb[5 + s][:, 0:F], 0.0, None, ALU.min).then_inc(S("kmin_ready"), 1)
                dve.wait_ge(S("ad_ps"), b + 1)
                cp(adst[:, ds(b, 1), :].rearrange("p b k -> p (b k)"), pb[4][:, 0:H * R]).then_inc(S("ad_taken"), 1)
                for r in range(1, R, 2):
                    dve.wait_ge(S("tab_ps1"), b * (R // 2) + r // 2 + 1)
                    if r == 1:
                        dve.wait_ge(S("row_free"), b + 1)
                    cp(tab_row[:, s, r * ROW:(r + 1) * ROW], pb[3][:, 0:ROW]).then_inc(S("tab_taken1"), 1)
                    if r == 1:
                        dve.wait_ge(S("kexp_ready"), b + 1)
                        stt(kphi[:, s, :], pb[5 + s][:, 0:F], 0.0, kexp[:, s, :], ALU.max, ALU.add).then_inc(S("k_ready"), 1)
            with dve.Fori(0, FULL // 2) as i:
                for s in range(2):
                    block_work(i * 2 + s, s)
            block_work(FULL, 0)

            dve.wait_ge(S("brk_taken"), -(-NSG // 3))
            own.link(v.tensor_reduce(brk_sum[:, :, 0], brk[:, :, 0:P], AX, ALU.add))
            own.link(tt(brk_sum[:, :, 1], brk_sum[:, :, 0], brk[:, :, 0], ALU.subtract))
            own.link(tt(brk_sum[:, :, 1], brk_sum[:, :, 1], brk[:, :, P], ALU.add))
            own.link(tt(tyoh[:, :, :], typT[:, 0:STEPS].unsqueeze(2).to_broadcast([P, STEPS, R]),
                        iota_row[:, 0:R].unsqueeze(1).to_broadcast([P, STEPS, R]), ALU.is_equal))
            dve.wait_ge(S("x_biased"), 1)

            def queries(qn, s, n):
                for c in range(FC):
                    dve.wait_ge(S("qexp_ready"), qn * FC + c + 1)
                    stt(qT[s][c][:, 0:n], qexp[:, c, 0:n], 1.0, qT[s][c][:, 0:n], ALU.min, ALU.add).then_inc(S("q_ready"), 1)

            def attend(qn, s, n, c):
                dve.wait_ge(S("lin_ps"), (qn + 2) * FC + c + 1)
                own.link(v.reciprocal(qden[:, 0:n], pb[4 + c][:, 0:n]))
                stt(attT2[s][:, c, 0:n], qden[:, 0:n], 1e6, pb[2 + c][:, 0:n], ALU.min, ALU.mult).then_inc(S("lin_ready"), 1)
                dve.wait_ge(S("lin_ready"), qn * FC + c + 1)

            def project(qn, n):
                dve.wait_ge(S("proj_ps"), qn + 1)
                for j in range(-(-n // P)):
                    m = min(P, n - j * P)
                    xb = x_sb[0:m, ds(qn * 4 + j, 1), :].rearrange("p b f -> p (b f)")
                    tt(xb, xb, pb[6 + j // 2][0:m, j % 2 * F:j % 2 * F + F], ALU.add).then_inc(S("proj_taken"), 1)

            size = lambda qn: 512 if qn < NCH else TAIL

            def chunk(qn, s, static=False):
                attend(qn, s, 512, 1)
                attend(qn + 1, 1 - s, size(qn + 1) if static else 512, 0)
                if not static or qn + 2 <= NCH:
                    queries(qn + 2, s, size(qn + 2) if static else 512)
                project(qn, 512)
            queries(0, 0, 512)
            attend(0, 0, 512, 0)
            queries(1, 1, 512)
            with dve.Fori(0, (NCH - 2) // 2) as i:
                own.enter(i, 4)
                for s in range(2):
                    chunk(i * 2 + s, s)
                own.leave((NCH - 2) // 2)
            for qn in range((NCH - 2) // 2 * 2, NCH):
                chunk(qn, qn % 2, static=True)
            attend(NCH, NCH % 2, TAIL, 1)
            project(NCH, TAIL)

            dve.wait_ge(S("acc_zeroed"), 1)
            dve.wait_ge(S("tab_stored"), 16 * NB)
            v.memset(slice2, 0.0).then_inc(S("slice2_zeroed"), 1)
            by_head = lambda t: t.rearrange("p (h g) -> p h g", h=H)
            flatrow = lambda t: t.rearrange("p h c -> p (h c)")
            scan = lambda o, brk_, data, first: v.tensor_tensor_scan(o, brk_, data, first, ALU.add, ALU.max)

            regs = [dve.alloc_register(f"dve_block{k}") for k in range(SG)]

            def turn(g_, u, third, scores=True, messages=True):
                n, slot, mslot = g_ + 1, (u + 1) % 3, u % 3

                def rescale():
                    dve.wait_ge(S("fac_ready"), g_ + 1)
                    dve.wait_ge(S("acc_added"), g_ * SG + 3)
                    at = acc[:, ds(bs[0], 1), 0:F].rearrange("p b (h d) -> p (b h) d", h=H)
                    own.link(tt(at, at, fac[:, :].unsqueeze(2).to_broadcast([P, H, D]), ALU.mult))
                    at = acc[:, ds(bs[0], 1), F:ROW].rearrange("p b h -> p (b h)")
                    own.link(tt(at, at, fac[:, :], ALU.mult))

                def weigh(half):
                    dve.wait_ge(S("w_ready"), g_ * 2 + 2)
                    t8 = slice(half * 8, min(half * 8 + 8, DVE_STEPS))
                    m = rows[:, mslot, t8, 0:F].rearrange("p t (h d) -> p t h d", h=H)
                    tt(m, m, w_sb[:, t8, :].unsqueeze(3).to_broadcast([P, t8.stop - t8.start, H, D]), ALU.mult).then_inc(S("msg_ready"), 1)

                def add(t0, t1):
                    for t in range(t0, t1) if messages else ():
                        if t == t0:
                            own.settle()
                        added_before = dve.to_reg(g_ * SG + t + 3)
                        dve.wait_ge(S("msg_ps"), g_ * SG + 3 * SG + t + 1)
                        at = acc[:, ds(bs[t], 1), :].rearrange("p b k -> p (b k)")
                        tt(at, at, sums[(u * SG + t) % 3][:, 0:ROW], ALU.add).wait_op(S("acc_added"), added_before, "sem-ge").then_inc(S("acc_added"), 1)

                def dst_scores(half):
                    own.settle()
                    dve.wait_ge(S("dsc_ps"), n * 2 + half + 1)
                    own.link(tt(sel[:, :, :, :], pb[2 + half][:, :].rearrange("p (t h r) -> p t h r", h=H, r=R),
                                tyoh[:, ds(n * SG + half * 8, 8), :].unsqueeze(2).to_broadcast([P, SG // 2, H, R]), ALU.mult))
                    own.count(v.tensor_reduce(score[:, half * 8:half * 8 + 8, :], sel[:, :, :, :], AX, ALU.add))

                if messages:
                    weigh(0)
                    bs = load_blocks(dve, brow[0:1, ds(g_ * SG, SG)], NB - 1, regs)
                    rescale()
                if not scores:
                    weigh(1)
                    add(0, SG)
                    return
                dst_scores(0)
                add(0, 3)
                if messages:
                    weigh(1)
                dst_scores(1)
                own.settle()
                dve.wait_ge(S(f"rows_here{slot}"), (third + (u + 1) // 3 + 1) * SG * 16)
                own.link(tt(score[:, :, :], score[:, :, :], rows[:, slot, :, F:ROW], ALU.add))
                stt(score[:, :, :], score[:, :, :], 0.2, score[:, :, :], ALU.mult, ALU.max).then_inc(S("score_ready"), 1)
                add(3, 6)
                dve.wait_ge(S("breaks_here"), (n + 1) * 2)
                dve.wait_ge(S("scoreT_ps"), n + 1)
                sT = pb[4][:, 0:P]
                own.link(scan(run[:, 0, :], brk_g[:, 0:P], sT, -BIG))
                scan(run[:, 1, ::-1], brk_g[:, P:0:-1], sT[:, ::-1], -BIG).then_inc(S("ends_ready"), 1)
                add(6, 8)
                dve.wait_ge(S("ends_ps"), n + 1)
                dve.wait_ge(S("breaks_taken"), n + 1)
                own.link(cp(chunk_row[0:1, 0:2, :, 1:SG + 1], pb[5][0:1, 0:2 * P].rearrange("p (k t h) -> p k h t", k=2, h=H)))
                own.link(scan(flatrow(carry[0]), flatrow(chunk_row[0:1, 2]), flatrow(chunk_row[0:1, 0]), -BIG))
                own.link(scan(flatrow(carry[1])[:, ::-1], flatrow(chunk_row[0:1, 3])[:, ::-1], flatrow(chunk_row[0:1, 1])[:, ::-1], -BIG))
                cp(carry_flat[0:1, :, :].rearrange("p k (t h) -> p k t h", h=H), carry_both).then_inc(S("carry_ready"), 1)
                add(8, 10)
                own.link(stt(ex[0:1, 0, :], carry[1][:, :, 1], 0.0, carry[0][:, :, 0], ALU.max, ALU.max))
                own.link(stt(ex[0:1, 1, :], carry[0][:, :, 0], 0.0, ex[0:1, 0, :], ALU.max, ALU.subtract))
                own.link(stt(ex[0:1, 2, :], brk_g[0:1, 0:1].to_broadcast([1, H]), 0.0, ex[0:1, 1, :], ALU.is_equal, ALU.mult))
                own.link(cp(chunk_row[0:1, 0, :, 0], carry[0][:, :, SG]))
                dve.wait_ge(S("seg0_ps"), n + 1)
                cp(seg0[:, :], pb[5][:, 0:2]).then_inc(S("seg0_taken"), 1)
                add(10, 12)
                dve.wait_ge(S("seg0_taken"), n + 1)
                own.link(scan(run[:, 0, :], brk_g[:, 0:P], sT, seg0[:, 0:1]))
                own.link(scan(run[:, 1, ::-1], brk_g[:, P:0:-1], sT[:, ::-1], seg0[:, 1:2]))
                own.link(stt(run[:, 0, :], run[:, 0, :], 0.0, run[:, 1, :], ALU.max, ALU.max))
                tt(below[:, :], sT, run[:, 0, :], ALU.subtract).then_inc(S("below_ready"), 1)
                add(12, 16)
            turn(-1, -1, 0, messages=False)
            with dve.Fori(0, NSG // 3) as i:
                own.enter(i, 3 * 18)
                for u in range(3):
                    turn(i * 3 + u, u, i)
                own.leave(NSG // 3)
            for g_ in range(NSG // 3 * 3, NSG):
                if g_ == NSG - 1:
                    dve.wait_ge(S("ld_small_ffn"), 16 * FFN_SMALL)
                    own.link(ts(temp_r, temp_r, 0.1, 5.0, ALU.max, ALU.min))
                    own.link(v.reciprocal(temp_r, temp_r))
                    cp(by_head(itemp_r), temp_r.unsqueeze(2).to_broadcast([1, H, G])).then_inc(S("itemp_ready"), 1)
                turn(g_, g_ % 3, NSG // 3, scores=g_ + 1 < NSG)
            by_pair = lambda t: t.rearrange("p (q k) -> p q k", q=PAIRS)
            dve.wait_ge(S("itemp_ps"), 1)
            tt(by_pair(slice2t), by_pair(pb[2][:, :]), slice2.unsqueeze(1).to_broadcast([P, PAIRS, P]), ALU.mult).then_inc(S("slice2_ready"), 1)
            dve.wait_ge(S("acc_added"), STEPS + 3)
            own.link(ts(rden[:, :, :], acc[:, :, F:ROW], 1e-12, None, ALU.add))
            v.reciprocal(rden[:, :, :], rden[:, :, :]).then_inc(S("rden_ready"), 1)
            dve.wait_ge(S("rden_ready"), 1)
            at = acc[:, 0:DVE_BLOCKS, 0:F].rearrange("p b (h d) -> p b h d", h=H)
            own.link(tt(at, at, rden[:, 0:DVE_BLOCKS, :].unsqueeze(3).to_broadcast([P, DVE_BLOCKS, H, D]), ALU.mult))
            tt(x_sb[:, 0:DVE_BLOCKS, :], x_sb[:, 0:DVE_BLOCKS, :], acc[:, 0:DVE_BLOCKS, 0:F], ALU.add).then_inc(S("x2_ready"), 1)
            dve.wait_ge(S("x2_ready"), 2)

            own.link(v.memset(ctx_bd[:, 0, :], 0.0))
            v.memset(swsum, 0.0).then_inc(S("sw_summed"), 1)
            own.link(tt(by_head(bias_r), by_head(itemp_r), bslice_r.unsqueeze(1).to_broadcast([1, H, G]), ALU.mult))
            dve.wait_ge(S("bx_ps"), 1)
            tt(bias_r, bias_r, pb[4][0:1, :], ALU.add).then_inc(S("bias_ready"), 1)
            node_stats(2)
            ts(rstd[:, :], mv[:, :, 1], LN_EPS, None, ALU.add).then_inc(S("stats"), 1)
            node_rstd(2)

            dve.wait_ge(S("bias_b_ready"), 1)

            def slice_top(b, s, first=False):
                if not first:
                    dve.wait_ge(S("sw_ready"), b - 1)
                dve.wait_ge(S("logit_ps"), b + 1)
                own.link(tt(logit[:, s, :], pb[2 + s][:, :], bias_b[:, :], ALU.add))
                own.link(v.tensor_reduce(top[:, s, :], by_head(logit[:, s, :]), AX, ALU.max))
                ts(top[:, s, :], top[:, s, :], -1.0, None, ALU.mult).then_inc(S("logit_ready"), 1)

            def slice_norm(b, s):
                lg = by_head(logit[:, s, :])
                dve.wait_ge(S("lexp_ready"), (b + 1) * H)
                own.link(v.tensor_reduce(tot[:, s, :], lg, AX, ALU.add))
                own.link(v.reciprocal(tot[:, s, :], tot[:, s, :]))
                sw_b = sw[:, ds(b, 1), :].rearrange("p b k -> p (b k)")
                tt(by_head(sw_b), lg, tot[:, s, :].unsqueeze(2).to_broadcast([P, H, G]), ALU.mult).then_inc(S("sw_ready"), 1)
            slice_top(0, 0, first=True)
            slice_top(1, 1, first=True)
            with dve.Fori(0, FULL // 2 - 1) as i:
                own.enter(i, 8)
                for s in range(2):
                    slice_norm(i * 2 + s, s)
                    slice_top(i * 2 + s + 2, s)
                own.leave(FULL // 2 - 1)
            slice_norm(FULL - 2, 0)
            slice_top(FULL, 0)
            slice_norm(FULL - 1, 1)
            slice_norm(FULL, 0)

            dve.wait_ge(S("norm_ps"), 1)
            own.link(cp(norm_r, pb[6][0:1, :]))
            dve.wait_ge(S("swx_ps"), NB)
            for c in range(FC):
                ins = cp(swxT[:, c, :], pb[4 + c][:, :])
            ins.then_inc(S("norm_ready"), 1)
            own.link(ts(rnorm, pb[6][:, :], 1e-5, None, ALU.add))
            own.link(v.reciprocal(rnorm, rnorm))
            dve.wait_ge(S("tok_ps"), 1)
            tt(tokT[:, :], pb[7][0:DH, :], rnorm[0:DH, :], ALU.mult).then_inc(S("tok_ready"), 1)
            dve.wait_ge(S("attn_ps"), 1)
            scores, ag = by_head(pb[3][0:G, :]), by_head(att_g[0:G, :])
            own.link(v.tensor_reduce(top[0:G, 0, :], scores, AX, ALU.max))
            tt(ag, scores, top[0:G, 0, :].unsqueeze(2).to_broadcast([G, H, G]), ALU.subtract).then_inc(S("attn_below"), 1)
            dve.wait_ge(S("attn_exp"), 1)
            own.link(v.tensor_reduce(tot[0:G, 0, :], ag, AX, ALU.add))
            own.link(v.reciprocal(tot[0:G, 0, :], tot[0:G, 0, :]))
            tt(ag, ag, tot[0:G, 0, :].unsqueeze(2).to_broadcast([G, H, G]), ALU.mult).then_inc(S("attn_ready"), 1)
            dve.wait_ge(S("attnT_ps"), 1)
            cp(attnT[0:G, :], pb[4][0:G, :]).then_inc(S("attnT_ready"), 1)
            own.link(v.memset(osbd, 0.0))
            dve.wait_ge(S("os_ps"), 1)
            own.link(cp(osbd[0:G, :, 0:G], pb[5][0:G, :].rearrange("p (q e g) -> p q e g", e=2, g=G)[:, :, 0, :]))
            cp(osbd[G:P, :, G:P], pb[5][G:P, :].rearrange("p (q e g) -> p q e g", e=2, g=G)[:, :, 1, :]).then_inc(S("os_ready"), 1)

            def out_block(b, s):
                dve.wait_ge(S("y_ps"), b + 3)
                dve.wait_ge(S("y_free"), b + 1)
                own.link(tt(y[:, s, :], pb[2 + s][:, 0:F], x_sb[:, ds(b, 1), :].rearrange("p b f -> p (b f)"), ALU.add))
                tt(y[:, s, :], y[:, s, :], bout_b[:, :], ALU.add).then_inc(S("y_ready"), 1)
            with dve.Fori(0, FULL // 2) as i:
                own.enter(i, 2)
                for s in range(2):
                    out_block(i * 2 + s, s)
                own.leave(FULL // 2)
            out_block(FULL, 0)


def kernel(**inputs):
    import numpy as np
    import concourse.bacc as bacc
    from concourse.bass_utils import run_bass_kernel_spmd

    nc = bacc.Bacc("TRN2", target_bir_lowering=False, num_devices=1)
    arrays, aps = {}, {}
    for name, value in inputs.items():
        value = np.ascontiguousarray(value)
        arrays[f"in_{name}"] = value
        aps[name] = nc.dram_tensor(f"in_{name}", value.shape, mybir.dt.from_np(value.dtype), kind="ExternalInput").ap()
    out = nc.dram_tensor("out_0", inputs["x"].shape, F32, kind="ExternalOutput").ap()
    build(nc, aps, out)
    result = run_bass_kernel_spmd(nc, [arrays], core_ids=[0])
    return result.results[0]["out_0"]
```
